# Optimizing a Trainium2 kernel written in Bass

```python
import numpy as np
import jax
import jax.numpy as jnp

def _softmax(x, axis=-1):
    return jax.nn.softmax(x, axis=axis)

def _gelu(x):
    return jax.nn.gelu(x, approximate=True)

def _silu(x):
    return jax.nn.silu(x)

def _sigmoid(x):
    return jax.nn.sigmoid(x)

def _layernorm(x, axis=-1, eps=1e-05):
    m = jnp.mean(x, axis=axis, keepdims=True)
    v = jnp.var(x, axis=axis, keepdims=True)
    return (x - m) / jnp.sqrt(v + eps)

def _scatter_add(tgt, idx, src, axis=0):
    return tgt.at[idx].add(src)

def _segment_sum(src, seg, n):
    return jax.ops.segment_sum(src, seg, n)
kernel_name = 'mk_sandwich_d1_jaxref_r4_68f5f3'

def setup_inputs(seed: int=0):
    np.random.seed(seed)
    _w = jnp.asarray

    def _L0_attn_setup():
        import jax, jax.numpy as jnp
        import numpy as np
        import math
        B, S, E, H = (4, 512, 256, 16)
        HD = E // H
        key = jax.random.key(seed)
        k1, k2, k3 = jax.random.split(key, 3)
        Q = jax.random.normal(k1, (B, S, E), dtype=jnp.float32)
        W_packed = jax.random.normal(k2, (E, 3 * E), dtype=jnp.float32) * (1.0 / math.sqrt(E))
        b_packed = jnp.zeros((3 * E,), dtype=jnp.float32)
        W_out = jax.random.normal(k3, (E, E), dtype=jnp.float32) * (1.0 / math.sqrt(E))
        b_out = jnp.zeros((E,), dtype=jnp.float32)
        return {'Q': Q, 'W_packed': W_packed, 'b_packed': b_packed, 'W_out': W_out, 'b_out': b_out}
    _L0_attn_in = _L0_attn_setup()

    def _L0_ffn_setup():
        import jax, jax.numpy as jnp
        import numpy as np
        B, M, D = (4, 512, 256)
        N, P = (64, 32)
        key = jax.random.key(seed)
        k1, k2, k3, k4 = jax.random.split(key, 4)
        x = jax.random.normal(k1, (B, M, D), dtype=jnp.float32)
        phi = jax.random.normal(k2, (D, N, P), dtype=jnp.float32) * (1.0 / np.sqrt(D))
        W = jax.random.normal(k3, (N, D, D), dtype=jnp.float32) * (1.0 / np.sqrt(D))
        b = jax.random.normal(k4, (N, D), dtype=jnp.float32) * 0.01
        return {'x': x, 'phi': phi, 'W': W, 'b': b}
    _L0_ffn_in = _L0_ffn_setup()
    _d = {'L0_attn_Q': _L0_attn_in['Q'], 'L0_attn_W_packed': _L0_attn_in['W_packed'], 'L0_attn_b_packed': _L0_attn_in['b_packed'], 'L0_attn_W_out': _L0_attn_in['W_out'], 'L0_attn_b_out': _L0_attn_in['b_out'], 'L0_ffn_phi': _L0_ffn_in['phi'], 'L0_ffn_W': _L0_ffn_in['W'], 'L0_ffn_b': _L0_ffn_in['b']}
    _x0 = _d['L0_attn_Q']
    _d['L0_attn_Q'] = jax.random.normal(jax.random.fold_in(jax.random.key(seed), 1), (8, 1024, 256), dtype=_x0.dtype)
    del _x0
    return _d

def reference(L0_attn_Q, L0_attn_W_packed, L0_attn_b_packed, L0_attn_W_out, L0_attn_b_out, L0_ffn_phi, L0_ffn_W, L0_ffn_b):

    def _L0_attn_ref(Q, W_packed, b_packed, W_out, b_out):
        import jax, jax.numpy as jnp
        import numpy as np
        import math
        B, S, E, H = (4, 512, 256, 16)
        HD = E // H
        batch, seq, d = Q.shape
        qkv = Q @ W_packed + b_packed
        q, k, v = jnp.split(qkv, 3, axis=-1)

        def heads(x):
            return x.reshape(batch, seq, H, HD).transpose(0, 2, 1, 3)
        qh, kh, vh = (heads(q), heads(k), heads(v))
        scale = math.sqrt(HD)
        scores = jnp.einsum('bhqd,bhkd->bhqk', qh, kh) / scale
        causal = jnp.tril(jnp.ones((seq, seq), dtype=bool))
        scores = jnp.where(causal, scores, -jnp.inf)
        probs = jax.nn.softmax(scores, axis=-1)
        attn = jnp.einsum('bhqk,bhkd->bhqd', probs, vh)
        joined = attn.transpose(0, 2, 1, 3).reshape(batch, seq, d)
        return joined @ W_out + b_out

    def _L0_ffn_ref(x, phi, W, b):
        import jax, jax.numpy as jnp
        import numpy as np
        B, M, D = (4, 512, 256)
        N, P = (64, 32)
        logits = jnp.einsum('bmd,dnp->bmnp', x, phi)
        dispatch = jax.nn.softmax(logits, axis=0)
        bsz, m, n, p = logits.shape
        combine = jax.nn.softmax(logits.reshape(bsz, m, n * p), axis=-1).reshape(bsz, m, n, p)
        slots = jnp.einsum('bmd,bmnp->bnpd', x, dispatch)
        y = jnp.einsum('bnpd,nde->bnpe', slots, W) + b[None, :, None, :]
        out = jnp.einsum('bnpd,bmnp->bmd', y, combine)
        return out
    x = L0_attn_Q
    x = x + _layernorm(_L0_attn_ref(_layernorm(x, axis=-1), L0_attn_W_packed, L0_attn_b_packed, L0_attn_W_out, L0_attn_b_out), axis=-1)
    x = x + _layernorm(_L0_ffn_ref(_layernorm(x, axis=-1), L0_ffn_phi, L0_ffn_W, L0_ffn_b), axis=-1)
    return x

_drawn_inputs = setup_inputs


def setup_inputs(seed=0):
    import zlib

    import numpy as np

    out = dict(_drawn_inputs(seed))
    spreads = {'L0_attn_b_packed': (0.0, 0.1), 'L0_attn_b_out': (0.0, 0.1)}
    factors = {}
    for name, (base, spread) in spreads.items():
        noise = np.random.default_rng([zlib.crc32(name.encode()), seed]).standard_normal(out[name].shape)
        drawn = base * np.exp(spread * noise) if base else spread * noise
        out[name] = jnp.asarray(drawn.astype(out[name].dtype))
    for name, factor in factors.items():
        out[name] = (out[name] * factor).astype(out[name].dtype)
    return out
```

```python
from contextlib import ExitStack

import concourse.bass as bass
from concourse import mybir

F32 = mybir.dt.float32
BF16 = mybir.dt.bfloat16
ACT = mybir.ActivationFunctionType
ALU = mybir.AluOpType
AX = mybir.AxisListType

P = 128
HALF = 512
EPS = 1e-5
NEG = -3.0e38
HEADS, HD, QUAD = 16, 16, 4
NQUAD = HEADS // QUAD
Q_PART = (0, 0, 1, 1, 0, 2)
K_PART = (0, 1, 0, 1, 2, 0)
SCORE_ROWS = HD * len(Q_PART)
SHIFT_ROWS = 3
STAT = 6
ONE = 1


class Place:

    def __init__(self, nc, prefix):
        self.nc, self.prefix, self.stack, self.all_sems = nc, prefix, ExitStack(), []

    def __enter__(self):
        return self

    def __exit__(self, *exc):
        return self.stack.__exit__(*exc)

    def sb(self, name, shape, dt=F32):
        return self.stack.enter_context(self.nc.sbuf_tensor(f"{self.prefix}_{name}", shape, dt))

    def ps(self, name, shape, dt=F32):
        return self.stack.enter_context(self.nc.psum_tensor(f"{self.prefix}_{name}", shape, dt))

    def sem(self, name):
        s = self.stack.enter_context(self.nc.semaphore(f"{self.prefix}_{name}"))
        self.all_sems.append(s)
        return s

    def sems(self, name, n):
        return [self.sem(f"{name}{i}") for i in range(n)]

    def start_sems(self):
        with self.nc.Block() as block:

            @block.sync
            def _(sp):
                for s in self.all_sems:
                    sp.sem_inc(s, ONE)


class Steps:

    def __init__(self, eng, sem, base, per_body=None):
        self.eng, self.sem, self.base, self.n, self.per_body = eng, sem, base, 0, per_body

    def done(self, ins):
        ins.then_inc(self.sem, 1)
        self.n += 1
        return ins

    def wait(self):
        self.eng.wait_ge(self.sem, ONE + self.base + self.n)

    def end(self):
        assert self.per_body == self.n, (self.per_body, self.n)


def flat(ap):
    return ap.rearrange("p a b -> p (a b)")


def load_constants(nc, place, ident, identb, mask):
    made = place.sem("made")
    place.start_sems()
    with nc.Block() as block:

        @block.gpsimd
        def _(pool):
            pool.memset(ident[:, :], 0.0).then_inc(made, 1)
            pool.memset(mask[:, :], 0.0).then_inc(made, 1)
            pool.wait_ge(made, ONE + 2)
            pool.affine_select(out=ident[:, :], in_=ident[:, :], compare_op=ALU.not_equal, fill=1.0, base=0,
                               pattern=[[-1, P]], channel_multiplier=1).then_inc(made, 1)
            pool.affine_select(out=mask[:, :], in_=mask[:, :], compare_op=ALU.is_ge, fill=NEG, base=0,
                               pattern=[[-1, P]], channel_multiplier=1).then_inc(made, 1)
            pool.wait_ge(made, ONE + 4)
            pool.tensor_copy(identb[:, :], ident[:, :]).then_inc(made, 1)
            pool.wait_ge(made, ONE + 5)


class Moments:
    STEPS = 6

    def __init__(self, place, name, tiles):
        self.stats = place.sb(f"{name}_stats", [P, tiles, STAT])
        self.mean2, self.diff, self.dev, self.square = (place.sb(f"{name}_{n}", [P, tiles]) for n in ("mean2", "diff", "dev", "square"))
        self.mean, self.ve = place.sb(f"{name}_mean", [P, tiles]), place.sb(f"{name}_ve", [P, tiles])

    def of(self, dve, step, rows, columns):
        st = self.stats
        for i, t in enumerate(rows):
            step.done(dve.bn_stats(st[:, i, :], t))
        step.wait()
        step.done(dve.tensor_tensor(self.mean2[:, :], st[:, :, 1], st[:, :, 4], ALU.add))
        step.done(dve.tensor_tensor(self.diff[:, :], st[:, :, 1], st[:, :, 4], ALU.subtract))
        step.done(dve.tensor_tensor(self.dev[:, :], st[:, :, 2], st[:, :, 5], ALU.add))
        step.wait()
        step.done(dve.scalar_tensor_tensor(out=self.square[:, :], in0=self.diff[:, :], scalar=columns / 4, in1=self.diff[:, :],
                                           op0=ALU.mult, op1=ALU.mult))
        step.done(dve.tensor_scalar(self.mean[:, :], self.mean2[:, :], 0.5, None, ALU.mult))
        step.wait()
        step.done(dve.tensor_tensor(self.dev[:, :], self.dev[:, :], self.square[:, :], ALU.add))
        step.wait()
        return dve.tensor_scalar(self.ve[:, :], self.dev[:, :], 1.0 / columns, EPS, ALU.mult, ALU.add)


def project_qkv(nc, x, w_packed, b_packed, ident, parts_out, v_out):
    B, S, E = x.shape
    HALVES, NT, ET = S // HALF, HALF // P, E // P
    QKT = 2 * E // P
    with Place(nc, "qkv") as place:
        sb, ps, sem, sems = place.sb, place.ps, place.sem, place.sems
        w = sb("w", [P, ET, 3 * E])
        b_qk = sb("b_qk", [P, QKT])
        b_v = sb("b_v", [P, E])
        minus_half = sb("minus_half", [P, NT])
        xs = [sb(f"x{s}", [P, NT, E]) for s in range(2)]
        xn = [sb(f"xn{s}", [P, NT, E]) for s in range(2)]
        xnT = [sb(f"xnT{s}", [P, ET, HALF]) for s in range(2)]
        moments = Moments(place, "x", NT)
        mean, ve = moments.mean, moments.ve
        rstd = sb("rstd", [P, NT])
        qk = [sb(f"qk{c}", [P, HALF]) for c in range(QKT)]
        rest = [sb(f"rest{c}", [P, HALF]) for c in range(QKT)]
        parts = [sb(f"parts{c}", [P, 3, HALF], BF16) for c in range(QKT)]
        v_ones = [sb(f"v_ones{s}", [P, NT, HEADS, 2 * HD]) for s in range(2)]
        turned = [ps(f"turned{t}", [P, HALF]) for t in range(ET)]
        qk_ps = [ps(f"qk_ps{c}", [P, HALF]) for c in range(QKT)]
        v_ps = [ps(f"v_ps{i}", [P, 2, E]) for i in range(2)]

        w_ready = sem("w_ready")
        const_ready = sem("const_ready")
        x_ready = sems("x_ready", 2)
        ve_ready, rstd_ready = sem("ve_ready"), sem("rstd_ready")
        xn_ready = sems("xn_ready", 2)
        turned_ready, turned_used = sems("turned_ready", ET), sems("turned_used", ET)
        qk_ps_ready, qk_ps_used = sems("qk_ps_ready", QKT), sems("qk_ps_used", QKT)
        qk_used = sems("qk_used", QKT)
        part0_ready, rest_ready, part1_ready = sem("part0_ready"), sem("rest_ready"), sem("part1_ready")
        part2_ready, parts_stored = sems("part2_ready", QKT), sems("parts_stored", QKT)
        v_ps_ready, v_ps_used = sems("v_ps_ready", 2), sems("v_ps_used", 2)
        v_stored = sems("v_stored", 2)
        dve_step = sem("dve_step")
        DVE_BODY = HALVES * (NT + Moments.STEPS)

        place.start_sems()
        with nc.Block() as block:

            @block.sync
            def _(sp):
                sp.dma_start(w[:, :, :], w_packed.rearrange("(t p) n -> p t n", p=P)).then_inc(w_ready, 16)
                sp.dma_start(b_qk[:, :], b_packed[0:2 * E].rearrange("(t p) -> p t", p=P),
                             allow_slow_non_contiguous=True).then_inc(w_ready, 16)
                sp.dma_start(b_v[:, :], b_packed[2 * E:3 * E].partition_broadcast(P)).then_inc(w_ready, 16)
                with sp.Fori(0, B) as b:
                    for s in range(HALVES):
                        sp.wait_ge(xn_ready[s], ONE + b)
                        sp.dma_start(xs[s][:, :, :],
                                     x[bass.ds(b, 1), s * HALF:(s + 1) * HALF, :].rearrange("o (t p) e -> p (o t) e", p=P)
                                     ).then_inc(x_ready[s], 16)
                    for s in range(HALVES):
                        u = b * HALVES + s
                        for c in range(QKT):
                            sp.wait_ge(part2_ready[c], ONE + u + 1)
                            sp.dma_start(parts_out[:, c * P:(c + 1) * P, bass.ds(b * S + s * HALF, HALF)].rearrange("i p n -> p i n"),
                                         parts[c][:, :, :]).then_inc(parts_stored[c], 16)
                        for i in range(2):
                            sp.wait_ge(v_ps_used[i], ONE + u + 1)
                        sp.dma_start(v_out[bass.ds(b, 1), :, s * NT:(s + 1) * NT, :].rearrange("o p t n -> (o p) t n"),
                                     v_ones[s][:, :, :, :].rearrange("p t h d -> p t (h d)")).then_inc(v_stored[s], 16)
                for c in range(QKT):
                    sp.wait_ge(parts_stored[c], ONE + 16 * B * HALVES)
                for s in range(HALVES):
                    sp.wait_ge(v_stored[s], ONE + 16 * B)

            @block.gpsimd
            def _(pool):
                pool.memset(minus_half[:, :], -0.5).then_inc(const_ready, 1)
                pool.memset(v_ones[0][:, :, :, :], 1.0).then_inc(const_ready, 1)
                pool.memset(v_ones[1][:, :, :, :], 1.0).then_inc(const_ready, 1)
                pool.wait_ge(const_ready, ONE + 3)
                with pool.Fori(0, B) as b:
                    for s in range(HALVES):
                        u = b * HALVES + s
                        pool.wait_ge(ve_ready, ONE + u + 1)
                        pool.tensor_tensor(rstd[:, :], ve[:, :], minus_half[:, :], ALU.pow).then_inc(rstd_ready, 1)
                        for c in range(QKT):
                            pool.wait_ge(part1_ready, ONE + QKT * u + c + 1)
                            pool.tensor_tensor(parts[c][:, 2, :], rest[c][:, :], parts[c][:, 1, :],
                                               ALU.subtract).then_inc(part2_ready[c], 1)

            @block.vector
            def _(dve):
                dve.wait_ge(w_ready, ONE + 48)
                dve.wait_ge(const_ready, ONE + 3)
                with dve.Fori(0, B) as b:
                    step = Steps(dve, dve_step, b * DVE_BODY, DVE_BODY)
                    for s in range(HALVES):
                        u = b * HALVES + s
                        dve.wait_ge(x_ready[s], ONE + 16 * b + 16)
                        dve.wait_ge(rstd_ready, ONE + u)
                        moments.of(dve, step, [xs[s][:, i, :] for i in range(NT)], E).then_inc(ve_ready, 1)
                        dve.wait_ge(rstd_ready, ONE + u + 1)
                        for t in range(ET):
                            dve.wait_ge(turned_ready[t], ONE + u)
                        for i in range(NT):
                            ins = dve.tensor_scalar(xn[s][:, i, :], xs[s][:, i, :], mean[:, i:i + 1], rstd[:, i:i + 1],
                                                    ALU.subtract, ALU.mult)
                        ins.then_inc(xn_ready[s], 1)
                        for c in range(QKT):
                            dve.wait_ge(part0_ready, ONE + QKT * u + c + 1)
                            dve.wait_ge(part2_ready[c], ONE + u)
                            dve.tensor_tensor(rest[c][:, :], qk[c][:, :], parts[c][:, 0, :], ALU.subtract).then_inc(rest_ready, 1)
                            dve.wait_ge(rest_ready, ONE + QKT * u + c + 1)
                            dve.tensor_copy(parts[c][:, 1, :], rest[c][:, :]).then_inc(part1_ready, 1)
                        dve.wait_ge(v_stored[s], ONE + 16 * b)
                        for i in range(NT):
                            dve.wait_ge(v_ps_ready[i // 2], ONE + u + 1)
                            ins = dve.tensor_tensor(v_ones[s][:, i, :, 0:HD],
                                                    v_ps[i // 2][:, i % 2, :].rearrange("p (h d) -> p h d", d=HD),
                                                    b_v[:, :].rearrange("p (h d) -> p h d", d=HD), ALU.add)
                            if i % 2:
                                ins.then_inc(v_ps_used[i // 2], 1)
                    step.end()

            @block.scalar
            def _(act):
                act.wait_ge(w_ready, ONE + 48)
                with act.Fori(0, B) as b:
                    for s in range(HALVES):
                        u = b * HALVES + s
                        act.wait_ge(v_ps_ready[1], ONE + u)
                        for t in range(ET):
                            act.wait_ge(turned_ready[t], ONE + u + 1)
                            act.activation(xnT[s][:, t, :], turned[t][:, :], ACT.Copy).then_inc(turned_used[t], 1)
                        for c in range(QKT):
                            act.wait_ge(qk_ps_ready[c], ONE + u + 1)
                            act.wait_ge(rest_ready, ONE + QKT * u)
                            act.activation(qk[c][:, :], qk_ps[c][:, :], ACT.Identity, bias=b_qk[:, c:c + 1]).then_inc(qk_used[c], 1)
                            act.wait_ge(parts_stored[c], ONE + 16 * u)
                            act.wait_ge(qk_used[c], ONE + u + 1)
                            act.activation(parts[c][:, 0, :], qk[c][:, :], ACT.Copy).then_inc(part0_ready, 1)

            @block.tensor
            def _(pe):
                pe.wait_ge(w_ready, ONE + 48)
                with pe.Fori(0, B) as b:
                    for s in range(HALVES):
                        u = b * HALVES + s
                        pe.wait_ge(xn_ready[s], ONE + b + 1)
                        for t in range(ET):
                            pe.wait_ge(turned_used[t], ONE + u)
                            for i in range(NT):
                                ins = pe.transpose(turned[t][:, i * P:(i + 1) * P], xn[s][:, i, t * P:(t + 1) * P], ident[:, :])
                            ins.then_inc(turned_ready[t], 1)
                        for t in range(ET):
                            pe.wait_ge(turned_used[t], ONE + u + 1)
                        for c in range(QKT):
                            pe.wait_ge(qk_used[c], ONE + u)
                            for t in range(ET):
                                ins = pe.matmul(qk_ps[c][:, :], w[:, t, c * P:(c + 1) * P], xnT[s][:, t, :],
                                                start=(t == 0), stop=(t == ET - 1))
                            ins.then_inc(qk_ps_ready[c], 1)
                        for i in range(NT):
                            if i % 2 == 0:
                                pe.wait_ge(v_ps_used[i // 2], ONE + u)
                            for t in range(ET):
                                ins = pe.matmul(v_ps[i // 2][:, i % 2, :], xnT[s][:, t, i * P:(i + 1) * P], w[:, t, 2 * E:3 * E],
                                                start=(t == 0), stop=(t == ET - 1))
                            if i % 2:
                                ins.then_inc(v_ps_ready[i // 2], 1)


def attend(nc, parts_in, v_in, identb, mask, out_T):
    B, _, KT, _ = v_in.shape
    S = KT * P
    HPAD = 2 * HD
    VW = QUAD * HPAD
    with Place(nc, "att") as place:
        sb, ps, sem, sems = place.sb, place.ps, place.sem, place.sems
        q_rows = [sb(f"q{g}", [P, QUAD, S], BF16) for g in range(NQUAD)]
        k_rows = [sb(f"k{g}", [P, QUAD, S], BF16) for g in range(NQUAD)]
        v_ones = [sb(f"v{g}", [P, KT, VW]) for g in range(NQUAD)]
        maskb = sb("maskb", [P, P], BF16)
        gate = sb("gate", [1, 2])
        NPROB = 4
        probs = [sb(f"probs{i}", [P, QUAD, HALF]) for i in range(NPROB)]
        o_sb = sb("o_sb", [P, 2, HALF])
        QT = S // P
        mx = sb("mx", [P, QUAD, QT])
        neg = sb("neg", [P, QUAD * QT])
        neg_rest = sb("neg_rest", [P, QUAD * QT])
        shift = sb("shift", [P, SHIFT_ROWS, QUAD * QT], BF16)
        shift_T = sb("shift_T", [SHIFT_ROWS * QUAD * QT, P], BF16)
        row_ps = [ps(f"row_ps{i}", [P, 2, HALF]) for i in range(2)]
        NCOL = 3
        col_ps = [ps(f"col_ps{i}", [P, HALF]) for i in range(NCOL)]
        o_ps = ps("o_ps", [P, HALF])

        loaded = sems("loaded", NQUAD)
        v_loaded = sems("v_loaded", NQUAD)
        shift_loaded = sems("shift_loaded", NQUAD)
        ones_ready, gate_open = sem("ones_ready"), sem("gate_open")
        row_ready, row_used = sems("row_ready", 2), sems("row_used", 2)
        col_ready, col_used = sems("col_ready", NCOL), sems("col_used", NCOL)
        probs_masked, probs_used = sems("probs_masked", NPROB), sems("probs_used", NPROB)
        o_out = sem("o_out")
        o_stored = sem("o_stored")
        shift_ready = sem("shift_ready")
        dve_step = sem("dve_step")
        DVE_QUAD = 4

        groups = [(qt, (h, h + 1)) for qt in range(HALF // P) for h in range(0, QUAD, 2)]
        groups += [(qt, (h,)) for qt in range(HALF // P, QT) for h in range(QUAD)]
        NG = len(groups)
        RING0 = NG // 2 + 1
        RING1 = NG // 2
        TURN_AT = 6

        blocks = [(1, kt) for kt in range(KT)] + [(0, kt) for kt in range(KT // 2)]
        NB = len(blocks)
        COLS = NB * QUAD // NCOL
        BLKS = NB // NPROB

        def wait_exp(eng, q, k):
            n = k * QUAD + QUAD - 1
            eng.wait_ge(col_used[n % NCOL], ONE + COLS * q + n // NCOL + 1)

        PV_LAG = 2
        EVAC_AT = 17

        def block_columns(k):
            c, kt = blocks[k]
            first = max(0, kt * P - c * HALF)
            return c * HALF + first, first, HALF - first, kt * P >= c * HALF

        def masked_before(k):
            return sum(block_columns(j)[3] for j in range(k) if j % NPROB == k % NPROB)

        def gates_before(k):
            return sum(block_columns(j)[3] for j in range(k))

        GATES = gates_before(NB)
        MASKED = [masked_before(NB + i) for i in range(NPROB)]

        def chunks_of(g):
            qt, heads = groups[g]
            n = (qt + 1) * P
            if len(heads) == 2:
                return [(heads[i], i, 0, n, i == 1) for i in range(2)]
            return [(heads[0], 0, 0, HALF, False), (heads[0], 1, HALF, n - HALF, True)]

        def use0(q, g):
            return RING0 * q - 1 + g // 2 + (1 if g >= TURN_AT else 0) if not (isinstance(q, int) and q == 0) else g // 2

        def turn_use(q):
            if isinstance(q, int) and q == B * NQUAD - 1:
                return RING0 * (q + 1) - 1
            return RING0 * (q + 1) - 1 + TURN_AT // 2

        def use(q, g):
            return use0(q, g) if g % 2 == 0 else RING1 * q + g // 2

        def quad_loop(eng, body):
            with eng.Fori(0, B - 1) as b:
                for g in range(NQUAD):
                    body(b, g, True, True)
            for g in range(NQUAD):
                body(B - 1, g, g < NQUAD - 2, g < NQUAD - 3)

        place.start_sems()
        with nc.Block() as block:

            @block.sync
            def _(sp):
                def load(q, g, b, used=True):
                    tokens = bass.ds(b * S if isinstance(b, int) else sp.snap(b * S), S)
                    if used:
                        sp.wait_ge(probs_used[NPROB - 1], ONE + BLKS * (q - 3))
                    for rows, parts, base in ((q_rows[g], Q_PART, 0), (k_rows[g], K_PART, HEADS * HD)):
                        for i, part in enumerate(parts):
                            src = parts_in[part, base + g * QUAD * HD:base + (g + 1) * QUAD * HD, tokens]
                            sp.dma_start(rows[i * HD:(i + 1) * HD, :, :],
                                         src.rearrange("(h r) n -> r h n", r=HD)).then_inc(loaded[g], 16)
                    sp.dma_start(v_ones[g][:, :, :],
                                 v_in[bass.ds(b, 1), :, :, g * VW:(g + 1) * VW].rearrange("o p t n -> (o p) t n")
                                 ).then_inc(v_loaded[g], 16)

                def load_shift(q, g):
                    sp.wait_ge(row_used[0], ONE + turn_use(q) + 1)
                    sp.dma_start(q_rows[g][SCORE_ROWS:SCORE_ROWS + SHIFT_ROWS, :, :],
                                 shift_T[:, :]).then_inc(shift_loaded[g], 16)

                def store(q, g, b):
                    sp.wait_ge(o_out, ONE + 2 * q + 2)
                    sp.dma_start(out_T.rearrange("b r n -> (b r) n")[bass.ds(q * P, P), :], flat(o_sb[:, :, :])
                                 ).then_inc(o_stored, 16)

                for g in range(3):
                    load(g, g, 0, used=False)
                load_shift(0, 0)

                def body(b, g, two, three):
                    q = b * NQUAD + g
                    if three:
                        load(q + 3, (g + 3) % NQUAD, b + (g + 3) // NQUAD)
                    if not (isinstance(b, int) and g == NQUAD - 1):
                        load_shift(q + 1, (g + 1) % NQUAD)
                    store(q, g, b)
                quad_loop(sp, body)
                sp.wait_ge(o_stored, ONE + 16 * B * NQUAD)

            @block.gpsimd
            def _(pool):
                pool.tensor_copy(maskb[:, :], mask[:, :]).then_inc(ones_ready, 1)
                pool.memset(gate[:, :], 0.0).then_inc(gate_open, 1)
                pool.wait_ge(gate_open, ONE + 1)

                def body(b, g, two, three):
                    q = b * NQUAD + g
                    for k in range(NB):
                        _, first, width, diagonal = block_columns(k)
                        i = k % NPROB
                        if diagonal:
                            pool.wait_ge(gate_open, ONE + 1 + GATES * q + gates_before(k))
                            wait_exp(pool, q, k)
                            pool.tensor_tensor(gate[:, 1:2], gate[:, 0:1], gate[:, 0:1], ALU.add).then_inc(gate_open, 1)
                            pool.affine_select(out=probs[i][:, :, 0:P], in_=probs[i][:, :, 0:P], compare_op=ALU.is_ge, fill=0.0,
                                               base=0, pattern=[[0, QUAD], [1, P]], channel_multiplier=-1).then_inc(probs_masked[i], 1)
                quad_loop(pool, body)

            @block.scalar
            def _(act):
                def body(b, g, two, three):
                    q = b * NQUAD + g
                    for k in range(NB):
                        _, first, width, diagonal = block_columns(k)
                        i = k % NPROB
                        act.wait_ge(probs_used[i], ONE + BLKS * q + k // NPROB)
                        for h in range(QUAD):
                            n = k * QUAD + h
                            slot = n % NCOL
                            act.wait_ge(col_ready[slot], ONE + COLS * q + n // NCOL + 1)
                            ins = act.activation(probs[i][:, h, 0:width], col_ps[slot][:, 0:width], ACT.Exp, scale=float(HD) ** -0.5)
                            ins.then_inc(col_used[slot], 1)
                quad_loop(act, body)

            @block.vector
            def _(dve):
                def reduce_group(q, gi):
                    qt, heads = groups[gi]
                    n = (qt + 1) * P
                    slot = gi % 2
                    dve.wait_ge(row_ready[slot], ONE + use(q, gi) + 1)
                    if len(heads) == 2:
                        src, dst = row_ps[slot][:, :, 0:n], mx[:, heads[0]:heads[0] + 2, qt]
                    else:
                        src, dst = flat(row_ps[slot][:, :, :])[:, 0:n], mx[:, heads[0], qt:qt + 1]
                    dve.tensor_reduce(dst, src, AX.X, ALU.max).then_inc(row_used[slot], 1)

                def turn_shift(q):
                    dve.wait_ge(row_ready[0], ONE + turn_use(q) + 1)
                    g, b = shift_slot_before[0]
                    dve.wait_ge(shift_loaded[g], ONE + 16 * b)
                    rows = SHIFT_ROWS * QUAD * QT
                    dve.tensor_copy(shift_T[:, :], row_ps[0][0:rows, 0, 0:P // 2].bitcast(BF16)).then_inc(row_used[0], 1)

                def split_maxima(q):
                    dve.wait_ge(row_used[0], ONE + use(q, NG - 2) + 1)
                    dve.wait_ge(row_used[1], ONE + use(q, NG - 1) + 1)
                    step = Steps(dve, dve_step, q * DVE_QUAD, DVE_QUAD)
                    mxf = flat(mx[:, :, :])
                    step.done(dve.tensor_scalar(shift[:, 0, :], mxf, -1.0, None, ALU.mult))
                    step.done(dve.tensor_scalar(neg[:, :], mxf, -1.0, None, ALU.mult))
                    step.wait()
                    step.done(dve.tensor_tensor(neg_rest[:, :], neg[:, :], shift[:, 0, :], ALU.subtract))
                    step.wait()
                    step.done(dve.tensor_copy(shift[:, 1, :], neg_rest[:, :]))
                    step.wait()
                    step.end()
                    dve.tensor_tensor(shift[:, 2, :], neg_rest[:, :], shift[:, 1, :], ALU.subtract).then_inc(shift_ready, 1)

                def evacuate(q, n):
                    k = (KT, NB)[n] - 1
                    dve.wait_ge(probs_used[k % NPROB], ONE + BLKS * q + k // NPROB + 1)
                    dve.wait_ge(o_stored, ONE + 16 * q)
                    dve.tensor_copy(o_sb[:, 1 - n, :], o_ps[:, :]).then_inc(o_out, 1)

                for g in range(NQUAD):
                    dve.memset(k_rows[g][SCORE_ROWS:P, :, :], 1.0).then_inc(ones_ready, 1)
                shift_slot_before = [None]
                for gi in range(NG):
                    reduce_group(0, gi)
                split_maxima(0)
                for gi in range(NG):
                    if gi == TURN_AT:
                        shift_slot_before[0] = (0, 0)
                        turn_shift(0)
                    reduce_group(1, gi)
                split_maxima(1)

                def body(b, g, two, three):
                    q = b * NQUAD + g
                    shift_slot_before[0] = (g, b + 1)
                    if two:
                        for gi in range(NG):
                            if gi == TURN_AT:
                                turn_shift(q + 1)
                            if gi == EVAC_AT:
                                evacuate(q, 0)
                            reduce_group(q + 2, gi)
                        split_maxima(q + 2)
                    else:
                        if g == NQUAD - 2:
                            turn_shift(q + 1)
                        evacuate(q, 0)
                    evacuate(q, 1)
                quad_loop(dve, body)

            @block.tensor
            def _(pe):
                def row_chunk(q, g, n):
                    gi, part = n // 2, n % 2
                    qt, heads = groups[gi]
                    slot = gi % 2
                    h, bank, k0, width, last = chunks_of(gi)[part]
                    if part == 0:
                        pe.wait_ge(row_used[slot], ONE + use(q, gi))
                    dst = row_ps[slot][:, bank, 0:width]
                    diagonal = k0 + width == (qt + 1) * P
                    ins = pe.matmul(dst, q_rows[g][0:SCORE_ROWS, h, qt * P:(qt + 1) * P], k_rows[g][0:SCORE_ROWS, h, k0:k0 + width],
                                    start=True, stop=True)
                    if diagonal:
                        ins = pe.matmul(row_ps[slot][:, bank, width - P:width], identb[:, :], maskb[:, :],
                                        start=False, stop=True, skip_group_check=True)
                    if part == 1:
                        ins.then_inc(row_ready[slot], 1)

                def turn(q):
                    pe.wait_ge(shift_ready, ONE + q + 1)
                    pe.wait_ge(row_used[0], ONE + turn_use(q))
                    rows = SHIFT_ROWS * QUAD * QT
                    pe.transpose(row_ps[0][0:rows, 0, 0:P // 2].bitcast(BF16), shift[:, :, :].rearrange("p a b -> p (a b)"),
                                 identb[:, :]).then_inc(row_ready[0], 1)

                def rows_until(q, g, done, until):
                    for n in range(done, until):
                        if n == 2 * TURN_AT:
                            if not (isinstance(q, int) and q == 0):
                                turn(q - 1)
                        row_chunk(q, g, n)

                def pv(q, g, b, k):
                    c, kt = blocks[k]
                    _, first, width, diagonal = block_columns(k)
                    i = k % NPROB
                    if k == 0:
                        pe.wait_ge(v_loaded[g], ONE + 16 * b + 16)
                    if kt == 0:
                        pe.wait_ge(o_out, ONE + 2 * q + (1 - c))
                    if diagonal:
                        pe.wait_ge(probs_masked[i], ONE + MASKED[i] * q + masked_before(k) + 1)
                    else:
                        wait_exp(pe, q, k)
                    last = kt == (KT - 1 if c else KT // 2 - 1)
                    for h in range(QUAD):
                        ins = pe.matmul(o_ps[h * HPAD:(h + 1) * HPAD, first:HALF], v_ones[g][:, kt, h * HPAD:(h + 1) * HPAD],
                                        probs[i][:, h, 0:width], start=(kt == 0), stop=last, skip_group_check=True)
                    ins.then_inc(probs_used[i], 1)

                def body(b, g, two, three):
                    q = b * NQUAD + g
                    g2, b2 = (g + 2) % NQUAD, b + (g + 2) // NQUAD
                    if two:
                        pe.wait_ge(loaded[g2], ONE + 16 * 12 * (b2 + 1))
                    pe.wait_ge(shift_loaded[g], ONE + 16 * (b + 1))
                    done = 0
                    for k in range(NB):
                        q0, first, width, diagonal = block_columns(k)
                        kt = blocks[k][1]
                        more = (4, 3, 3)[k % 3]
                        for h in range(QUAD):
                            n = k * QUAD + h
                            slot = n % NCOL
                            pe.wait_ge(col_used[slot], ONE + COLS * q + n // NCOL)
                            ins = pe.matmul(col_ps[slot][:, 0:width], k_rows[g][0:SCORE_ROWS + SHIFT_ROWS, h, kt * P:(kt + 1) * P],
                                            q_rows[g][0:SCORE_ROWS + SHIFT_ROWS, h, q0:q0 + width], start=True, stop=True)
                            ins.then_inc(col_ready[slot], 1)
                            if two and h < more:
                                rows_until(q + 2, g2, done, done + 1)
                                done += 1
                        if not two and g == NQUAD - 2 and k == 3:
                            turn(q + 1)
                        if k >= PV_LAG:
                            pv(q, g, b, k - PV_LAG)
                    for k in range(NB - PV_LAG, NB):
                        if two:
                            rows_until(q + 2, g2, done, done + 4)
                            done += 4
                        pv(q, g, b, k)
                    assert not two or done == 2 * NG

                pe.wait_ge(ones_ready, ONE + NQUAD + 1)
                for g in range(2):
                    pe.wait_ge(loaded[g], ONE + 16 * 12)
                    rows_until(g, g, 0, 2 * NG)
                quad_loop(pe, body)


def close_attention(nc, x, att_T, w_out, b_out, ident, x1_out, xf_out, xfT_out):
    B, S, E = x.shape
    HALVES, NT, ET = S // HALF, HALF // P, E // P
    with Place(nc, "close") as place:
        sb, ps, sem, sems = place.sb, place.ps, place.sem, place.sems
        w = sb("w", [P, ET, E])
        bo = sb("bo", [P, E])
        minus_half = sb("minus_half", [P, NT])
        num = [sb(f"num{s}", [P, ET, HALF]) for s in range(2)]
        den = [sb(f"den{s}", [P, ET, HALF]) for s in range(2)]
        xs = [sb(f"x{s}", [P, NT, E]) for s in range(2)]
        h = [sb(f"h{s}", [P, NT, E]) for s in range(2)]
        hn = [sb(f"hn{s}", [P, NT, E]) for s in range(2)]
        xf = [sb(f"xf{s}", [P, NT, E]) for s in range(2)]
        xfT = [sb(f"xfT{s}", [P, ET, HALF]) for s in range(2)]
        moments = [Moments(place, f"m{i}", NT) for i in range(2)]
        mean, ve = [m.mean for m in moments], [m.ve for m in moments]
        rstd = [sb(f"rstd{i}", [P, NT]) for i in range(2)]
        h_ps = [ps(f"h_ps{s}", [P, NT, E]) for s in range(2)]
        turned = [ps(f"turned{t}", [P, HALF]) for t in range(ET)]

        w_ready, const_ready = sem("w_ready"), sem("const_ready")
        in_ready = sems("in_ready", 2)
        att_ready = sems("att_ready", 2)
        h_ps_ready, h_ready = sems("h_ps_ready", 2), sems("h_ready", 2)
        ve_ready, rstd_ready = sems("ve_ready", 2), sems("rstd_ready", 2)
        hn_ready, x1_ready = sems("hn_ready", 2), sems("x1_ready", 2)
        xf_ready, turned_ready, xfT_ready = sems("xf_ready", 2), sems("turned_ready", ET), sems("xfT_ready", 2)
        x1_stored, xf_stored, xfT_stored = sems("x1_stored", 2), sems("xf_stored", 2), sems("xfT_stored", 2)
        dve_step = sem("dve_step")
        DVE_HALF = 2 * (NT + Moments.STEPS) + 1
        nmr, nmr2 = sb("nmr", [P, NT]), sb("nmr2", [P, NT])
        nmr_ready, nmr2_ready = sem("nmr_ready"), sem("nmr2_ready")

        place.start_sems()
        with nc.Block() as block:

            @block.sync
            def _(sp):
                sp.dma_start(w[:, :, :], w_out.rearrange("(t p) n -> p t n", p=P)).then_inc(w_ready, 16)
                sp.dma_start(bo[:, :], b_out.partition_broadcast(P)).then_inc(w_ready, 16)
                with sp.Fori(0, B) as b:
                    for s in range(HALVES):
                        sp.wait_ge(xf_ready[s], ONE + b)
                        rows = att_T[bass.ds(b, 1), :, s * HALF:(s + 1) * HALF].rearrange("o (t h r) n -> (o t) h r n", t=ET, r=2 * HD)
                        for t in range(ET):
                            sp.dma_start(num[s][:, t, :], rows[t, :, 0:HD, :]).then_inc(in_ready[s], 16)
                            sp.dma_start(den[s][:, t, :], rows[t, :, HD:2 * HD, :]).then_inc(in_ready[s], 16)
                        sp.wait_ge(x1_ready[s], ONE + b)
                        sp.dma_start(xs[s][:, :, :], x[bass.ds(b, 1), s * HALF:(s + 1) * HALF, :].rearrange("o (t p) e -> p (o t) e", p=P)
                                     ).then_inc(in_ready[s], 16)
                    for s in range(HALVES):
                        tokens = lambda a: a[bass.ds(b, 1), s * HALF:(s + 1) * HALF, :].rearrange("o (t p) e -> p (o t) e", p=P)
                        sp.wait_ge(x1_ready[s], ONE + b + 1)
                        sp.dma_start(tokens(x1_out), hn[s][:, :, :]).then_inc(x1_stored[s], 16)
                        sp.wait_ge(xf_ready[s], ONE + b + 1)
                        sp.dma_start(tokens(xf_out), xf[s][:, :, :]).then_inc(xf_stored[s], 16)
                        sp.wait_ge(xfT_ready[s], ONE + ET * b + ET)
                        sp.dma_start(xfT_out[:, :, bass.ds(b * S + s * HALF, HALF)].rearrange("t p n -> p t n"),
                                     xfT[s][:, :, :]).then_inc(xfT_stored[s], 16)
                for s in range(HALVES):
                    for stored in (x1_stored, xf_stored, xfT_stored):
                        sp.wait_ge(stored[s], ONE + 16 * B)

            @block.gpsimd
            def _(pool):
                pool.memset(minus_half[:, :], -0.5).then_inc(const_ready, 1)
                pool.wait_ge(const_ready, ONE + 1)
                with pool.Fori(0, B) as b:
                    for s in range(HALVES):
                        u = b * HALVES + s
                        pool.wait_ge(ve_ready[0], ONE + u + 1)
                        pool.tensor_tensor(rstd[0][:, :], ve[0][:, :], minus_half[:, :], ALU.pow).then_inc(rstd_ready[0], 1)
                        pool.wait_ge(hn_ready[s], ONE + NT * b + NT)
                        pool.wait_ge(in_ready[s], ONE + 80 * b + 80)
                        pool.tensor_tensor(hn[s][:, :, :], hn[s][:, :, :], xs[s][:, :, :], ALU.add).then_inc(x1_ready[s], 1)
                        pool.wait_ge(ve_ready[1], ONE + u + 1)
                        pool.tensor_tensor(rstd[1][:, :], ve[1][:, :], minus_half[:, :], ALU.pow).then_inc(rstd_ready[1], 1)

            @block.vector
            def _(dve):
                dve.wait_ge(w_ready, ONE + 32)

                def first(b, s, step):
                    dve.wait_ge(in_ready[s], ONE + 80 * b + 80)
                    step.done(dve.reciprocal(den[s][:, :, :], den[s][:, :, :]))
                    step.wait()
                    dve.tensor_tensor(num[s][:, :, :], num[s][:, :, :], den[s][:, :, :], ALU.mult).then_inc(att_ready[s], 1)

                with dve.Fori(0, B) as b:
                    step = Steps(dve, dve_step, b * HALVES * DVE_HALF, HALVES * DVE_HALF)
                    for s in range(HALVES):
                        first(b, s, step)
                    for s in range(HALVES):
                        u = b * HALVES + s
                        dve.wait_ge(h_ps_ready[s], ONE + b + 1)
                        for i in range(NT):
                            ins = dve.tensor_tensor(h[s][:, i, :], h_ps[s][:, i, :], bo[:, :], ALU.add)
                        ins.then_inc(h_ready[s], 1)
                        dve.wait_ge(h_ready[s], ONE + b + 1)
                        dve.wait_ge(rstd_ready[0], ONE + u)
                        dve.wait_ge(hn_ready[1 - s], ONE + NT * (b + s))
                        moments[0].of(dve, step, [h[s][:, i, :] for i in range(NT)], E).then_inc(ve_ready[0], 1)
                        dve.wait_ge(x1_ready[s], ONE + b + 1)
                        moments[1].of(dve, step, [hn[s][:, i, :] for i in range(NT)], E).then_inc(ve_ready[1], 1)
                        dve.wait_ge(rstd_ready[1], ONE + u + 1)
                        dve.wait_ge(xf_stored[s], ONE + 16 * b)
                        for t in range(ET):
                            dve.wait_ge(turned_ready[t], ONE + u)
                        for i in range(NT):
                            ins = dve.tensor_scalar(xf[s][:, i, :], hn[s][:, i, :], mean[1][:, i:i + 1], rstd[1][:, i:i + 1],
                                                    ALU.subtract, ALU.mult)
                        ins.then_inc(xf_ready[s], 1)
                    step.end()

            @block.scalar
            def _(act):
                with act.Fori(0, B) as b:
                    for s in range(HALVES):
                        u = b * HALVES + s
                        act.wait_ge(rstd_ready[0], ONE + u + 1)
                        for i in range(NT):
                            act.activation(nmr[:, i:i + 1], mean[0][:, i:i + 1], ACT.Copy, scale=rstd[0][:, i:i + 1]).then_inc(nmr_ready, 1)
                        act.wait_ge(nmr_ready, ONE + NT * u + NT)
                        act.activation(nmr2[:, :], nmr[:, :], ACT.Copy, scale=-1.0).then_inc(nmr2_ready, 1)
                        act.wait_ge(nmr2_ready, ONE + u + 1)
                        act.wait_ge(x1_stored[s], ONE + 16 * b)
                        act.wait_ge(xf_ready[s], ONE + b)
                        for i in range(NT):
                            act.activation(hn[s][:, i, :], h[s][:, i, :], ACT.Identity, scale=rstd[0][:, i:i + 1],
                                           bias=nmr2[:, i:i + 1]).then_inc(hn_ready[s], 1)
                        for t in range(ET):
                            act.wait_ge(turned_ready[t], ONE + u + 1)
                            act.wait_ge(xfT_stored[s], ONE + 16 * b)
                            act.activation(xfT[s][:, t, :], turned[t][:, :], ACT.Copy).then_inc(xfT_ready[s], 1)

            @block.tensor
            def _(pe):
                pe.wait_ge(w_ready, ONE + 32)
                with pe.Fori(0, B) as b:
                    for s in range(HALVES):
                        pe.wait_ge(att_ready[s], ONE + b + 1)
                        pe.wait_ge(h_ready[s], ONE + b)
                        for i in range(NT):
                            for t in range(ET):
                                ins = pe.matmul(h_ps[s][:, i, :], num[s][:, t, i * P:(i + 1) * P], w[:, t, :],
                                                start=(t == 0), stop=(t == ET - 1))
                        ins.then_inc(h_ps_ready[s], 1)
                    for s in range(HALVES):
                        pe.wait_ge(xf_ready[s], ONE + b + 1)
                        for t in range(ET):
                            pe.wait_ge(xfT_ready[1 - s], ONE + ET * (b + s))
                            for i in range(NT):
                                ins = pe.transpose(turned[t][:, i * P:(i + 1) * P], xf[s][:, i, t * P:(t + 1) * P], ident[:, :])
                            ins.then_inc(turned_ready[t], 1)


def dispatch_and_experts(nc, res, xf_in, phi, w_exp, b_exp, ident, y_out):
    B, S, E = xf_in.shape
    _, NEXP, SLOTS = phi.shape
    ET, MT = E // P, S // P
    CHUNKS = NEXP * SLOTS // P
    PER = P // SLOTS
    xfT, phi_sb, row_max = res
    with Place(nc, "disp") as place:
        sb, ps, sem, sems = place.sb, place.ps, place.sem, place.sems
        NPROB = 4
        xf = sb("xf", [P, B * MT, E])
        probs = [sb(f"probs{i}", [P, B, P]) for i in range(NPROB)]
        batch_max = sb("batch_max", [P, P])
        total = sb("total", [P, P])
        inverse = [sb(f"inverse{i}", [P, P]) for i in range(2)]
        step_max = sb("step_max", [P, B])
        slots_sb = sb("slots_sb", [P, B, E])
        slots_T = sb("slots_T", [P, ET, B, P])
        w_sb = sb("w_sb", [P, PER, ET, E])
        bias = sb("bias", [P, E])
        y_sb = sb("y_sb", [P, B, E])
        ring = [ps(f"ring{i}", [P, B, P]) for i in range(2)]
        slots_ps = ps("slots_ps", [P, B, E])

        xf_ready, w_ready = sem("xf_ready"), sem("w_ready")
        ring_ready, ring_used = sems("ring_ready", 2), sems("ring_used", 2)
        exp_ready, probs_ready = sem("exp_ready"), sem("probs_ready")
        inverse_ready = sem("inverse_ready")
        slots_ready = sem("slots_ready")
        slots_out = sem("slots_out")
        y_stored = sem("y_stored")
        dve_step = sem("dve_step")
        RING = MT // 2 + 2

        def ring_base(c):
            return 0 if isinstance(c, int) and c == 0 else RING * c - 2

        def chunk_loop(eng, body, last):
            body(0, False)
            with eng.Fori(1, CHUNKS) as c:
                body(c, True)
            last()

        y_base = RING * CHUNKS - 2

        place.start_sems()
        with nc.Block() as block:

            @block.sync
            def _(sp):
                sp.dma_start(xf[:, :, :], xf_in.rearrange("b (m p) e -> p (b m) e", p=P)).then_inc(xf_ready, 16)

                def load_experts(c):
                    sp.dma_start(w_sb[:, :, :, :].rearrange("p x t e -> p (x t) e"),
                                 w_exp[bass.ds(c * PER, PER), :, :].rearrange("x (t p) e -> p (x t) e", p=P)).then_inc(w_ready, 16)
                    for x in range(PER):
                        sp.dma_start(bias[x * SLOTS:(x + 1) * SLOTS, :],
                                     b_exp[bass.ds(c * PER + x, 1), :].to_broadcast([SLOTS, E])).then_inc(w_ready, 16)

                def store(c, base):
                    for j in range(2):
                        sp.wait_ge(ring_used[j], ONE + base + 2)
                    sp.dma_start(y_out[:, bass.ds(c, 1), :, :].rearrange("b o p e -> p (b o) e"), y_sb[:, :, :]).then_inc(y_stored, 16)

                def body(c, before):
                    if before:
                        store(c - 1, ring_base(c) + MT // 2)
                        load_experts(c)
                    else:
                        load_experts(c)
                chunk_loop(sp, body, lambda: store(CHUNKS - 1, y_base))
                sp.wait_ge(y_stored, ONE + 16 * CHUNKS)

            @block.vector
            def _(dve):
                PER_CHUNK = 4 * MT
                buf = lambda t: probs[t % NPROB][:, :, :]

                def logits(c, t, step):
                    slot = t % 2
                    dve.wait_ge(ring_ready[slot], ONE + ring_base(c) + t // 2 + 1)
                    step.wait()
                    step.done(dve.tensor_reduce(batch_max[:, :], ring[slot][:, :, :].rearrange("p b n -> p n b"), AX.X, ALU.max))
                    step.done(dve.tensor_reduce(step_max[:, :], ring[slot][:, :, :], AX.X, ALU.max))
                    n = MT * c + t
                    if not (isinstance(c, int) and c == 0 and t < NPROB):
                        dve.wait_ge(slots_ready, ONE + n - NPROB + 1)
                    step.wait()
                    dve.tensor_tensor(buf(t), ring[slot][:, :, :], batch_max[:, :].unsqueeze(1).to_broadcast([P, B, P]),
                                      ALU.subtract).then_inc(ring_used[slot], 1)
                    step.done(dve.tensor_tensor(row_max[:, t, :], row_max[:, t, :], step_max[:, :], ALU.max))

                def sums(c, t, step):
                    n = MT * c + t
                    dve.wait_ge(exp_ready, ONE + n + 1)
                    dve.wait_ge(inverse_ready, ONE + n)
                    step.done(dve.tensor_reduce(total[:, :], buf(t).rearrange("p b n -> p n b"), AX.X, ALU.add))
                    if not (isinstance(c, int) and c == 0 and t < 2):
                        dve.wait_ge(probs_ready, ONE + n - 1)
                    step.wait()
                    dve.reciprocal(inverse[t % 2][:, :], total[:, :]).then_inc(inverse_ready, 1)

                def add_bias(c, base):
                    dve.wait_ge(w_ready, ONE + 16 * (1 + PER) * (c + 1))
                    dve.wait_ge(y_stored, ONE + 16 * c)
                    for j in range(2):
                        dve.wait_ge(ring_ready[j], ONE + base + 2)
                        out = y_sb[:, j * B // 2:(j + 1) * B // 2, :]
                        ins = dve.tensor_tensor(out, ring[j][:, :, :].rearrange("p b n -> p (b n)").rearrange("p (b e) -> p b e", e=E),
                                                bias[:, :].unsqueeze(1).to_broadcast([P, B // 2, E]), ALU.add)
                        ins.then_inc(ring_used[j], 1)

                def body(c, before):
                    step = Steps(dve, dve_step, 1 + c * PER_CHUNK, PER_CHUNK)
                    for t in range(MT):
                        logits(c, t, step)
                        if t:
                            sums(c, t - 1, step)
                    sums(c, MT - 1, step)
                    if before:
                        add_bias(c - 1, ring_base(c) + MT // 2)
                    step.end()
                dve.memset(row_max[:, :, :], NEG).then_inc(dve_step, 1)
                chunk_loop(dve, body, lambda: add_bias(CHUNKS - 1, y_base))

            @block.scalar
            def _(act):
                def turned(base):
                    for j in range(2):
                        act.wait_ge(ring_ready[j], ONE + base + 1)
                        act.activation(slots_T[:, :, j * B // 2:(j + 1) * B // 2, :].rearrange("p t b n -> p t (b n)"),
                                       ring[j][:, :, :].rearrange("p (t b) n -> p t (b n)", t=ET), ACT.Copy).then_inc(ring_used[j], 1)

                def body(c, before):
                    for t in range(MT):
                        act.wait_ge(ring_used[t % 2], ONE + ring_base(c) + t // 2 + 1)
                        act.activation(probs[t % NPROB][:, :, :], probs[t % NPROB][:, :, :], ACT.Exp).then_inc(exp_ready, 1)
                    if before:
                        turned(ring_base(c) + MT // 2)
                    act.wait_ge(slots_ready, ONE + MT * c + MT)
                    act.activation(slots_sb[:, :, :], slots_ps[:, :, :], ACT.Copy).then_inc(slots_out, 1)
                chunk_loop(act, body, lambda: turned(y_base))

            @block.gpsimd
            def _(pool):
                def body(c, before):
                    for t in range(MT):
                        n = MT * c + t
                        pool.wait_ge(inverse_ready, ONE + n + 1)
                        pool.tensor_tensor(probs[t % NPROB][:, :, :], probs[t % NPROB][:, :, :],
                                           inverse[t % 2][:, :].unsqueeze(1).to_broadcast([P, B, P]), ALU.mult).then_inc(probs_ready, 1)
                body(0, False)
                with pool.Fori(1, CHUNKS) as c:
                    body(c, True)

            @block.tensor
            def _(pe):
                def logits(c, t):
                    slot = t % 2
                    pe.wait_ge(ring_used[slot], ONE + ring_base(c) + t // 2)
                    for b in range(B):
                        for e in range(ET):
                            ins = pe.matmul(ring[slot][:, b, :], xfT[:, e, b * S + t * P:b * S + (t + 1) * P],
                                            phi_sb[:, e, bass.ds(c * P, P)], start=(e == 0), stop=(e == ET - 1), skip_group_check=True)
                    ins.then_inc(ring_ready[slot], 1)

                def slots(c, t):
                    n = MT * c + t
                    pe.wait_ge(probs_ready, ONE + n + 1)
                    if t == 0:
                        pe.wait_ge(slots_out, ONE + c)
                    for b in range(B):
                        ins = pe.matmul(slots_ps[:, b, :], probs[t % NPROB][:, b, :], xf[:, b * MT + t, :],
                                        start=(t == 0 and b % 2 == 0), stop=(t == MT - 1), skip_group_check=True)
                    ins.then_inc(slots_ready, 1)

                def turn_slots(c, base):
                    pe.wait_ge(slots_out, ONE + c + 1)
                    for j in range(2):
                        pe.wait_ge(ring_used[j], ONE + base)
                        for e in range(ET):
                            for b in range(B // 2):
                                ins = pe.transpose(ring[j][:, e * B // 2 + b, :], slots_sb[:, j * B // 2 + b, e * P:(e + 1) * P], ident[:, :])
                        ins.then_inc(ring_ready[j], 1)

                def experts(c, base):
                    pe.wait_ge(w_ready, ONE + 16 * (1 + PER) * (c + 1))
                    for j in range(2):
                        pe.wait_ge(ring_used[0], ONE + base + 1)
                        pe.wait_ge(ring_used[1], ONE + base + 1)
                        y_ps = ring[j][:, :, :].rearrange("p b n -> p (b n)").rearrange("p (b e) -> p b e", e=E)
                        for b in range(B // 2):
                            for e in range(ET):
                                for x in range(PER):
                                    ins = pe.matmul(y_ps[x * SLOTS:(x + 1) * SLOTS, b, :],
                                                    slots_T[:, e, j * B // 2 + b, x * SLOTS:(x + 1) * SLOTS], w_sb[:, x, e, :],
                                                    start=(e == 0 and b % 2 == 0), stop=(e == ET - 1), skip_group_check=True)
                        ins.then_inc(ring_ready[j], 1)

                def body(c, before):
                    for t in range(MT):
                        logits(c, t)
                        if t >= 2:
                            slots(c, t - 2)
                    if before:
                        turn_slots(c - 1, ring_base(c) + MT // 2)
                    slots(c, MT - 2)
                    if before:
                        experts(c - 1, ring_base(c) + MT // 2)
                    slots(c, MT - 1)
                pe.wait_ge(xf_ready, ONE + 16)

                def last():
                    turn_slots(CHUNKS - 1, y_base)
                    experts(CHUNKS - 1, y_base)
                chunk_loop(pe, body, last)


def combine(nc, res, y_in, x1, ident, identb, out):
    B, CHUNKS, _, E = y_in.shape
    xfT, phi_sb, row_max = res
    S = x1.shape[1]
    ET, MT, HALVES, NT = E // P, S // P, S // HALF, HALF // P
    W = E + 2
    with Place(nc, "comb") as place:
        sb, ps, sem, sems = place.sb, place.ps, place.sem, place.sems
        neg, rest = sb("neg", [P, B, MT]), sb("rest", [P, B, MT])
        part = [sb(f"part{i}", [P, B, MT], BF16) for i in range(SHIFT_ROWS)]
        part_T = sb("part_T", [B * MT, SHIFT_ROWS, P], BF16)
        shift = sb("shift", [P, B * S], BF16)
        ones = sb("ones", [P, P], BF16)
        NPROB = 4
        probs = [sb(f"probs{i}", [P, HALF]) for i in range(NPROB)]
        y = [sb(f"y{i}", [P, CHUNKS, W]) for i in range(2)]
        x1_sb = [sb(f"x1{i}", [P, NT, E]) for i in range(2)]
        h = [sb(f"h{i}", [P, NT, E]) for i in range(2)]
        inverse = sb("inverse", [P, NT])
        minus_half = sb("minus_half", [P, NT])
        rstd = sb("rstd", [P, NT])
        moments = Moments(place, "h", NT)
        mean, ve = moments.mean, moments.ve
        logit_ps = [ps(f"logit_ps{i}", [P, HALF]) for i in range(NPROB)]
        o_ps = ps("o_ps", [P, NT, HALF])

        const_ready, part_ready, turned, part_T_ready, shift_ready = (
            sem(n) for n in ("const_ready", "part_ready", "turned", "part_T_ready", "shift_ready"))
        y_ready = sems("y_ready", 2)
        x1_ready, o_stored = sems("x1_ready", 2), sems("o_stored", 2)
        logit_ready, exp_ready, prob_used = sems("logit_ready", NPROB), sems("exp_ready", NPROB), sems("prob_used", NPROB)
        o_out = sem("o_out")
        ve_ready, rstd_ready, hn_ready = sem("ve_ready"), sem("rstd_ready"), sem("hn_ready")
        out_ready = sems("out_ready", 2)
        dve_step = sem("dve_step")
        USES = CHUNKS // NPROB
        DVE_HALF = NT + Moments.STEPS + 1

        place.start_sems()
        with nc.Block() as block:

            @block.gpsimd
            def _(pool):
                pool.memset(minus_half[:, :], -0.5).then_inc(const_ready, 1)
                pool.memset(ones[:, :], 1.0).then_inc(const_ready, 1)
                pool.memset(shift[:, :], 0.0).then_inc(const_ready, 1)
                for i in range(2):
                    pool.memset(y[i][:, :, E:W], 1.0).then_inc(const_ready, 1)
                pool.wait_ge(const_ready, ONE + 5)

            @block.vector
            def _(dve):
                step = Steps(dve, dve_step, 0, 5)
                maxima = row_max[:, :, :].rearrange("p m b -> p b m")
                step.done(dve.tensor_scalar(neg[:, :, :], maxima, -1.0, None, ALU.mult))
                step.done(dve.tensor_scalar(part[0][:, :, :], maxima, -1.0, None, ALU.mult))
                step.wait()
                step.done(dve.tensor_tensor(rest[:, :, :], neg[:, :, :], part[0][:, :, :], ALU.subtract))
                step.wait()
                step.done(dve.tensor_copy(part[1][:, :, :], rest[:, :, :]))
                step.wait()
                step.done(dve.tensor_tensor(part[2][:, :, :], rest[:, :, :], part[1][:, :, :], ALU.subtract))
                step.end()
                for i in range(SHIFT_ROWS):
                    dve.wait_ge(turned, ONE + i + 1)
                    dve.tensor_copy(part_T[:, i, :], logit_ps[i][0:B * MT, 0:P // 2].bitcast(BF16)).then_inc(part_T_ready, 1)

            @block.tensor
            def _(pe):
                pe.wait_ge(dve_step, ONE + 5)
                for i in range(SHIFT_ROWS):
                    pe.transpose(logit_ps[i][0:B * MT, 0:P // 2].bitcast(BF16), flat(part[i][:, :, :]), identb[:, :]).then_inc(turned, 1)

            @block.sync
            def _(sp):
                sp.wait_ge(part_T_ready, ONE + SHIFT_ROWS)
                sp.wait_ge(const_ready, ONE + 3)
                for i in range(SHIFT_ROWS):
                    sp.dma_start(shift[i:i + 1, :].rearrange("o (m q) -> o m q", q=P), part_T[:, i, :]).then_inc(shift_ready, 16)
                sp.wait_ge(shift_ready, ONE + 16 * SHIFT_ROWS)

        def batch_loop(eng, body):
            with eng.Fori(0, B // 2 - 1) as pair:
                for j in range(2):
                    body(2 * pair + j, j, pair, True)
            for j in range(2):
                body(B - 2 + j, j, B // 2 - 1, j == 0)

        with nc.Block() as block:

            @block.sync
            def _(sp):
                def load_y(b, j):
                    sp.dma_start(y[j][:, :, 0:E], y_in[bass.ds(b, 1), :, :, :].rearrange("o c p e -> p (o c) e")).then_inc(y_ready[j], 16)
                load_y(0, 0)

                def body(b, j, pair, after):
                    if after:
                        if j == 0:
                            sp.wait_ge(prob_used[NPROB - 1], ONE + USES * HALVES * b)
                            load_y(b + 1, 1)
                        else:
                            sp.wait_ge(prob_used[NPROB - 1], ONE + USES * HALVES * b)
                            load_y(b + 1, 0)
                    for s in range(HALVES):
                        tokens = lambda a: a[bass.ds(b, 1), s * HALF:(s + 1) * HALF, :].rearrange("o (t p) e -> p (o t) e", p=P)
                        sp.wait_ge(out_ready[s], ONE + b)
                        sp.dma_start(x1_sb[s][:, :, :], tokens(x1)).then_inc(x1_ready[s], 16)
                    for s in range(HALVES):
                        tokens = lambda a: a[bass.ds(b, 1), s * HALF:(s + 1) * HALF, :].rearrange("o (t p) e -> p (o t) e", p=P)
                        sp.wait_ge(out_ready[s], ONE + b + 1)
                        sp.dma_start(tokens(out), h[s][:, :, :]).then_inc(o_stored[s], 16)
                batch_loop(sp, body)
                for s in range(HALVES):
                    sp.wait_ge(o_stored[s], ONE + 16 * B)

            @block.scalar
            def _(act):
                def body(b, j, pair, after):
                    for s in range(HALVES):
                        u = b * HALVES + s
                        for c in range(CHUNKS):
                            i, n = c % NPROB, USES * u + c // NPROB
                            act.wait_ge(logit_ready[i], ONE + n + 1)
                            act.wait_ge(prob_used[i], ONE + n)
                            act.activation(probs[i][:, :], logit_ps[i][:, :], ACT.Exp).then_inc(exp_ready[i], 1)
                batch_loop(act, body)

            @block.gpsimd
            def _(pool):
                def body(b, j, pair, after):
                    for s in range(HALVES):
                        u = b * HALVES + s
                        pool.wait_ge(ve_ready, ONE + u + 1)
                        pool.tensor_tensor(rstd[:, :], ve[:, :], minus_half[:, :], ALU.pow).then_inc(rstd_ready, 1)
                        pool.wait_ge(hn_ready, ONE + u + 1)
                        pool.wait_ge(x1_ready[s], ONE + 16 * (b + 1))
                        pool.tensor_tensor(h[s][:, :, :], h[s][:, :, :], x1_sb[s][:, :, :], ALU.add).then_inc(out_ready[s], 1)
                batch_loop(pool, body)

            @block.vector
            def _(dve):
                def body(b, j, pair, after):
                    for s in range(HALVES):
                        u = b * HALVES + s
                        step = Steps(dve, dve_step, 5 + u * DVE_HALF, DVE_HALF)
                        dve.wait_ge(prob_used[NPROB - 1], ONE + USES * (u + 1))
                        step.done(dve.reciprocal(inverse[:, :], o_ps[:, :, E]))
                        step.wait()
                        dve.wait_ge(o_stored[s], ONE + 16 * b)
                        for i in range(NT):
                            ins = dve.tensor_scalar(h[s][:, i, :], o_ps[:, i, 0:E], inverse[:, i:i + 1], None, ALU.mult)
                        ins.then_inc(o_out, 1)
                        dve.wait_ge(o_out, ONE + u + 1)
                        dve.wait_ge(rstd_ready, ONE + u)
                        moments.of(dve, step, [h[s][:, i, :] for i in range(NT)], E).then_inc(ve_ready, 1)
                        dve.wait_ge(rstd_ready, ONE + u + 1)
                        for i in range(NT):
                            ins = dve.tensor_scalar(h[s][:, i, :], h[s][:, i, :], mean[:, i:i + 1], rstd[:, i:i + 1],
                                                    ALU.subtract, ALU.mult)
                        ins.then_inc(hn_ready, 1)
                        step.end()
                batch_loop(dve, body)

            @block.tensor
            def _(pe):
                def products(u, j, c):
                    i, n = c % NPROB, USES * u + c // NPROB
                    pe.wait_ge(exp_ready[i], ONE + n + 1)
                    if c == 0:
                        pe.wait_ge(o_out, ONE + u)
                    for t in range(NT):
                        ins = pe.matmul(o_ps[:, t, 0:W], probs[i][:, t * P:(t + 1) * P], y[j][:, c, :],
                                        start=(c == 0), stop=(c == CHUNKS - 1), skip_group_check=True)
                    ins.then_inc(prob_used[i], 1)

                def body(b, j, pair, after):
                    pe.wait_ge(y_ready[j], ONE + 16 * (pair + 1))
                    for s in range(HALVES):
                        u = b * HALVES + s
                        columns = bass.ds(b * S + s * HALF, HALF)
                        for c in range(CHUNKS):
                            i, n = c % NPROB, USES * u + c // NPROB
                            pe.wait_ge(exp_ready[i], ONE + n)
                            for e in range(ET):
                                pe.matmul(logit_ps[i][:, :], phi_sb[:, e, c * P:(c + 1) * P], xfT[:, e, columns],
                                          start=(e == 0), stop=False)
                            pe.matmul(logit_ps[i][:, :], ones[:, :], shift[:, columns], start=False, stop=True).then_inc(logit_ready[i], 1)
                            if c >= 2:
                                products(u, j, c - 2)
                        for c in range(CHUNKS - 2, CHUNKS):
                            products(u, j, c)
                batch_loop(pe, body)


def block_kernel(nc, x, w_packed, b_packed, w_out, b_out, phi, w_exp, b_exp, out):
    B, S, E = x.shape
    scratch = lambda name, shape, dt=F32: nc.dram_tensor(name, shape, dt).ap()
    parts = scratch("parts", (3, 2 * E, B * S), BF16)
    v_ones = scratch("v_ones", (B, P, S // P, 2 * E))
    att_T = scratch("att_T", (B, 2 * E, S))
    x1 = scratch("x1", (B, S, E))
    xf = scratch("xf", (B, S, E))
    xfT = scratch("xfT", (E // P, P, B * S))
    y = scratch("y", (B, phi.shape[1] * phi.shape[2] // P, P, E))
    with Place(nc, "all") as place:
        ident = place.sb("ident", [P, P])
        identb = place.sb("identb", [P, P], BF16)
        with Place(nc, "mask") as m:
            mask = m.sb("mask", [P, P])
            load_constants(nc, place, ident, identb, mask)
            project_qkv(nc, x, w_packed, b_packed, ident, parts, v_ones)
            attend(nc, parts, v_ones, identb, mask, att_T)
        close_attention(nc, x, att_T, w_out, b_out, ident, x1, xf, xfT)
        with Place(nc, "moe") as moe:
            xfT_sb = moe.sb("xfT", [P, E // P, B * S])
            phi_sb = moe.sb("phi", [P, E // P, phi.shape[1] * phi.shape[2]])
            row_max = moe.sb("row_max", [P, S // P, B])
            loaded = moe.sem("loaded")
            moe.start_sems()
            with nc.Block() as block:

                @block.sync
                def _(sp):
                    sp.dma_start(phi_sb[:, :, :], phi.rearrange("(t p) x s -> p t (x s)", p=P)).then_inc(loaded, 16)
                    sp.dma_start(xfT_sb[:, :, :], xfT.rearrange("t p n -> p t n")).then_inc(loaded, 16)
                    sp.wait_ge(loaded, ONE + 32)
            res = (xfT_sb, phi_sb, row_max)
            dispatch_and_experts(nc, res, xf, phi, w_exp, b_exp, ident, y)
            combine(nc, res, y, x1, ident, identb, out)


_INS = ["L0_attn_Q", "L0_attn_W_packed", "L0_attn_b_packed", "L0_attn_W_out", "L0_attn_b_out", "L0_ffn_phi", "L0_ffn_W", "L0_ffn_b"]


def kernel(**inputs):
    import numpy as _np
    import concourse.bacc as _bacc
    from concourse.bass_utils import run_bass_kernel_spmd as _run

    nc = _bacc.Bacc("TRN2", target_bir_lowering=False, num_devices=1)
    arrays, args = {}, []
    for name in _INS:
        a = _np.ascontiguousarray(inputs[name])
        arrays[f"in_{name}_dram"] = a
        args.append(nc.dram_tensor(f"in_{name}_dram", a.shape, mybir.dt.from_np(a.dtype), kind="ExternalInput").ap())
    out = nc.dram_tensor("out_0_dram", inputs["L0_attn_Q"].shape, F32, kind="ExternalOutput").ap()
    block_kernel(nc, *args, out)
    r = _run(nc, [arrays], core_ids=[0])
    return r.results[0]["out_0_dram"]
```

```python
from contextlib import ExitStack

import concourse.bass as bass
from concourse import mybir

F32 = mybir.dt.float32
BF16 = mybir.dt.bfloat16
ACT = mybir.ActivationFunctionType
ALU = mybir.AluOpType
AX = mybir.AxisListType

P = 128
HALF = 512
EPS = 1e-5
NEG = -3.0e38
HEADS, HD, QUAD = 16, 16, 4
NQUAD = HEADS // QUAD
Q_PART = (0, 0, 1, 1, 0, 2)
K_PART = (0, 1, 0, 1, 2, 0)
SCORE_ROWS = HD * len(Q_PART)
SHIFT_ROWS = 3
STAT = 6
ONE = 1


class Place:

    def __init__(self, nc, prefix):
        self.nc, self.prefix, self.stack, self.all_sems = nc, prefix, ExitStack(), []

    def __enter__(self):
        return self

    def __exit__(self, *exc):
        return self.stack.__exit__(*exc)

    def sb(self, name, shape, dt=F32):
        return self.stack.enter_context(self.nc.sbuf_tensor(f"{self.prefix}_{name}", shape, dt))

    def ps(self, name, shape, dt=F32):
        return self.stack.enter_context(self.nc.psum_tensor(f"{self.prefix}_{name}", shape, dt))

    def sem(self, name):
        s = self.stack.enter_context(self.nc.semaphore(f"{self.prefix}_{name}"))
        self.all_sems.append(s)
        return s

    def sems(self, name, n):
        return [self.sem(f"{name}{i}") for i in range(n)]

    def start_sems(self):
        with self.nc.Block() as block:

            @block.sync
            def _(sp):
                for s in self.all_sems:
                    sp.sem_inc(s, ONE)


class Steps:

    def __init__(self, eng, sem, base, per_body=None):
        self.eng, self.sem, self.base, self.n, self.per_body = eng, sem, base, 0, per_body

    def done(self, ins):
        ins.then_inc(self.sem, 1)
        self.n += 1
        return ins

    def wait(self):
        self.eng.wait_ge(self.sem, ONE + self.base + self.n)

    def end(self):
        assert self.per_body == self.n, (self.per_body, self.n)


def flat(ap):
    return ap.rearrange("p a b -> p (a b)")


def load_constants(nc, place, ident, identb, mask):
    made = place.sem("made")
    place.start_sems()
    with nc.Block() as block:

        @block.gpsimd
        def _(pool):
            pool.memset(ident[:, :], 0.0).then_inc(made, 1)
            pool.memset(mask[:, :], 0.0).then_inc(made, 1)
            pool.wait_ge(made, ONE + 2)
            pool.affine_select(out=ident[:, :], in_=ident[:, :], compare_op=ALU.not_equal, fill=1.0, base=0,
                               pattern=[[-1, P]], channel_multiplier=1).then_inc(made, 1)
            pool.affine_select(out=mask[:, :], in_=mask[:, :], compare_op=ALU.is_ge, fill=NEG, base=0,
                               pattern=[[-1, P]], channel_multiplier=1).then_inc(made, 1)
            pool.wait_ge(made, ONE + 4)
            pool.tensor_copy(identb[:, :], ident[:, :]).then_inc(made, 1)
            pool.wait_ge(made, ONE + 5)


class Moments:
    STEPS = 6

    def __init__(self, place, name, tiles):
        self.stats = place.sb(f"{name}_stats", [P, tiles, STAT])
        self.mean2, self.diff, self.dev, self.square = (place.sb(f"{name}_{n}", [P, tiles]) for n in ("mean2", "diff", "dev", "square"))
        self.mean, self.ve = place.sb(f"{name}_mean", [P, tiles]), place.sb(f"{name}_ve", [P, tiles])

    def of(self, dve, step, rows, columns):
        st = self.stats
        for i, t in enumerate(rows):
            step.done(dve.bn_stats(st[:, i, :], t))
        step.wait()
        step.done(dve.tensor_tensor(self.mean2[:, :], st[:, :, 1], st[:, :, 4], ALU.add))
        step.done(dve.tensor_tensor(self.diff[:, :], st[:, :, 1], st[:, :, 4], ALU.subtract))
        step.done(dve.tensor_tensor(self.dev[:, :], st[:, :, 2], st[:, :, 5], ALU.add))
        step.wait()
        step.done(dve.scalar_tensor_tensor(out=self.square[:, :], in0=self.diff[:, :], scalar=columns / 4, in1=self.diff[:, :],
                                           op0=ALU.mult, op1=ALU.mult))
        step.done(dve.tensor_scalar(self.mean[:, :], self.mean2[:, :], 0.5, None, ALU.mult))
        step.wait()
        step.done(dve.tensor_tensor(self.dev[:, :], self.dev[:, :], self.square[:, :], ALU.add))
        step.wait()
        return dve.tensor_scalar(self.ve[:, :], self.dev[:, :], 1.0 / columns, EPS, ALU.mult, ALU.add)


def rounds(eng, body, total, per, extra=0):
    for j in range(per):
        body(j, j, 0)
    with eng.Fori(1, total // per - 1) as i:
        for j in range(per):
            body(per * i + j, j, i)
    for j in range(per + extra):
        body(total - per + j, j, total // per - 1)


def at_least(u, n):
    return not isinstance(u, int) or u >= n


def is_unit(u, units):
    return not isinstance(u, int) or 0 <= u < units


def project_qkv(nc, x, w_packed, b_packed, ident, parts_out, v_out):
    B, S, E = x.shape
    HALVES, NT, ET = S // HALF, HALF // P, E // P
    UNITS = B * HALVES
    QKT = 2 * E // P
    NBUF = 4
    with Place(nc, "qkv") as place:
        sb, ps, sem, sems = place.sb, place.ps, place.sem, place.sems
        w = sb("w", [P, ET, 3 * E])
        b_qk = sb("b_qk", [P, QKT])
        b_v = sb("b_v", [P, E])
        minus_half = sb("minus_half", [P, NT])
        xs = [sb(f"x{j}", [P, NT, E]) for j in range(NBUF)]
        xn = [sb(f"xn{k}", [P, NT, E]) for k in range(2)]
        xnT = [sb(f"xnT{k}", [P, ET, HALF]) for k in range(2)]
        moments = [Moments(place, f"x{k}", NT) for k in range(2)]
        rstd = [sb(f"rstd{k}", [P, NT]) for k in range(2)]
        qk = [sb(f"qk{c}", [P, HALF]) for c in range(QKT)]
        rest = [sb(f"rest{c}", [P, HALF]) for c in range(QKT)]
        parts = [[sb(f"parts{k}{c}", [P, 3, HALF], BF16) for c in range(QKT)] for k in range(2)]
        v_ones = [sb(f"v_ones{k}", [P, NT, HEADS, 2 * HD]) for k in range(2)]
        turned = [ps(f"turned{t}", [P, HALF]) for t in range(ET)]
        qk_ps = [ps(f"qk_ps{c}", [P, HALF]) for c in range(QKT)]
        v_ps = [ps(f"v_ps{i}", [P, 2, E]) for i in range(2)]

        w_ready = sem("w_ready")
        const_ready = sem("const_ready")
        x_ready = sems("x_ready", NBUF)
        ve_ready, rstd_ready, xn_ready = sem("ve_ready"), sem("rstd_ready"), sem("xn_ready")
        turned_ready, xnT_ready = sem("turned_ready"), sem("xnT_ready")
        qk_ps_ready, qk_ready = sem("qk_ps_ready"), sem("qk_ready")
        part0_ready, rest_ready, part1_ready, part2_ready = (sem(f"{n}_ready") for n in ("part0", "rest", "part1", "part2"))
        parts_stored = sems("parts_stored", 2)
        v_ps_ready, v_ready = sem("v_ps_ready"), sem("v_ready")
        v_stored = sems("v_stored", 2)
        dve_step = sem("dve_step")
        STEPS = NT + Moments.STEPS
        stored_before = lambda i, j: i * (NBUF // 2) + j // 2

        place.start_sems()
        with nc.Block() as block:

            @block.sync
            def _(sp):
                def load(i, j):
                    i, j = i + j // NBUF, j % NBUF
                    sp.dma_start(xs[j][:, :, :], x[bass.ds(i * (NBUF // HALVES) + j // HALVES, 1),
                                                   j % HALVES * HALF:(j % HALVES + 1) * HALF, :].rearrange("o (t p) e -> p (o t) e", p=P)
                                 ).then_inc(x_ready[j], 16)

                load(0, 0)
                sp.dma_start(w[:, :, :], w_packed.rearrange("(t p) n -> p t n", p=P)).then_inc(w_ready, 16)
                sp.dma_start(b_qk[:, :], b_packed[0:2 * E].rearrange("(t p) -> p t", p=P),
                             allow_slow_non_contiguous=True).then_inc(w_ready, 16)
                sp.dma_start(b_v[:, :], b_packed[2 * E:3 * E].partition_broadcast(P)).then_inc(w_ready, 16)
                AHEAD = NBUF - 1
                for j in range(1, AHEAD):
                    load(0, j)

                def body(u, j, i):
                    k = j % 2
                    if is_unit(u + AHEAD, UNITS):
                        if at_least(u, 1):
                            sp.wait_ge(xn_ready, ONE + u)
                        load(i, j + AHEAD)
                    columns = u * HALF if isinstance(u, int) else sp.snap(u * HALF)
                    for c in range(QKT):
                        sp.wait_ge(part2_ready, ONE + QKT * u + c + 1)
                        sp.dma_start(parts_out[:, c * P:(c + 1) * P, bass.ds(columns, HALF)].rearrange("i p n -> p i n"),
                                     parts[k][c][:, :, :]).then_inc(parts_stored[k], 16)
                    sp.wait_ge(v_ready, ONE + 2 * u + 2)
                    sp.dma_start(v_out[bass.ds(i * (NBUF // HALVES) + j // HALVES, 1), :, j % HALVES * NT:(j % HALVES + 1) * NT, :]
                                 .rearrange("o p t n -> (o p) t n"),
                                 v_ones[k][:, :, :, :].rearrange("p t h d -> p t (h d)")).then_inc(v_stored[k], 16)
                rounds(sp, body, UNITS, NBUF)
                for k in range(2):
                    sp.wait_ge(parts_stored[k], ONE + 16 * QKT * (UNITS // 2))
                    sp.wait_ge(v_stored[k], ONE + 16 * (UNITS // 2))

            @block.gpsimd
            def _(pool):
                pool.memset(minus_half[:, :], -0.5).then_inc(const_ready, 1)
                pool.memset(v_ones[0][:, :, :, :], 1.0).then_inc(const_ready, 1)
                pool.memset(v_ones[1][:, :, :, :], 1.0).then_inc(const_ready, 1)
                pool.wait_ge(const_ready, ONE + 3)

                def root(u, k):
                    pool.wait_ge(ve_ready, ONE + u + 1)
                    pool.tensor_tensor(rstd[k][:, :], moments[k].ve[:, :], minus_half[:, :], ALU.pow).then_inc(rstd_ready, 1)
                for k in range(2):
                    root(k, k)

                def body(u, j, i):
                    k = j % 2
                    for c in range(QKT):
                        if c == 1 and (is_unit(u + 2, UNITS)):
                            root(u + 2, k)
                        pool.wait_ge(part1_ready, ONE + QKT * u + c + 1)
                        pool.tensor_tensor(parts[k][c][:, 2, :], rest[c][:, :], parts[k][c][:, 1, :], ALU.subtract).then_inc(part2_ready, 1)
                rounds(pool, body, UNITS, NBUF)

            @block.vector
            def _(dve):
                def statistics(u, j, i):
                    k, step = j % 2, Steps(dve, dve_step, STEPS * u, STEPS)
                    dve.wait_ge(x_ready[j % NBUF], ONE + 16 * (i + j // NBUF + 1))
                    if at_least(u, 2):
                        dve.wait_ge(xn_ready, ONE + u - 1)
                    moments[k].of(dve, step, [xs[j % NBUF][:, t, :] for t in range(NT)], E).then_inc(ve_ready, 1)
                    step.end()

                def normalise(u, j):
                    k = j % 2
                    dve.wait_ge(rstd_ready, ONE + u + 1)
                    if at_least(u, 2):
                        dve.wait_ge(turned_ready, ONE + u - 1)
                    for t in range(NT):
                        ins = dve.tensor_scalar(xn[k][:, t, :], xs[j % NBUF][:, t, :], moments[k].mean[:, t:t + 1], rstd[k][:, t:t + 1],
                                                ALU.subtract, ALU.mult)
                    ins.then_inc(xn_ready, 1)

                for j in range(2):
                    statistics(j, j, 0)
                    normalise(j, j)
                dve.wait_ge(w_ready, ONE + 48)
                dve.wait_ge(const_ready, ONE + 3)

                def body(u, j, i):
                    k, more = j % 2, is_unit(u + 2, UNITS)
                    if more:
                        statistics(u + 2, j + 2, i)
                    for c in range(QKT):
                        dve.wait_ge(part0_ready, ONE + QKT * u + c + 1)
                        if at_least(u, 1):
                            dve.wait_ge(part2_ready, ONE + QKT * u - QKT + c + 1)
                        dve.tensor_tensor(rest[c][:, :], qk[c][:, :], parts[k][c][:, 0, :], ALU.subtract).then_inc(rest_ready, 1)
                        dve.wait_ge(rest_ready, ONE + QKT * u + c + 1)
                        dve.tensor_copy(parts[k][c][:, 1, :], rest[c][:, :]).then_inc(part1_ready, 1)
                        if more and c == 2:
                            normalise(u + 2, j + 2)
                    if at_least(u, 2):
                        dve.wait_ge(v_stored[k], ONE + 16 * stored_before(i, j))
                    for t in range(NT):
                        if t % 2 == 0:
                            dve.wait_ge(v_ps_ready, ONE + 2 * u + t // 2 + 1)
                        ins = dve.tensor_tensor(v_ones[k][:, t, :, 0:HD],
                                                v_ps[t // 2][:, t % 2, :].rearrange("p (h d) -> p h d", d=HD),
                                                b_v[:, :].rearrange("p (h d) -> p h d", d=HD), ALU.add)
                        if t % 2:
                            ins.then_inc(v_ready, 1)
                rounds(dve, body, UNITS, NBUF)

            @block.scalar
            def _(act):
                def turned_away(u, k):
                    act.wait_ge(turned_ready, ONE + u + 1)
                    if at_least(u, 2):
                        act.wait_ge(v_ps_ready, ONE + 2 * u - 2)
                    for t in range(ET):
                        ins = act.activation(xnT[k][:, t, :], turned[t][:, :], ACT.Copy)
                    ins.then_inc(xnT_ready, 1)

                turned_away(0, 0)
                act.wait_ge(w_ready, ONE + 48)

                def body(u, j, i):
                    k = j % 2
                    for c in range(QKT):
                        act.wait_ge(qk_ps_ready, ONE + QKT * u + c + 1)
                        if at_least(u, 1):
                            act.wait_ge(rest_ready, ONE + QKT * u - QKT + c + 1)
                        act.activation(qk[c][:, :], qk_ps[c][:, :], ACT.Identity, bias=b_qk[:, c:c + 1]).then_inc(qk_ready, 1)
                        if c == 0 and at_least(u, 2):
                            act.wait_ge(parts_stored[k], ONE + 16 * QKT * stored_before(i, j))
                        act.wait_ge(qk_ready, ONE + QKT * u + c + 1)
                        act.activation(parts[k][c][:, 0, :], qk[c][:, :], ACT.Copy).then_inc(part0_ready, 1)
                    if is_unit(u + 1, UNITS):
                        turned_away(u + 1, (j + 1) % 2)
                rounds(act, body, UNITS, NBUF)

            @block.tensor
            def _(pe):
                def turn(u, k):
                    pe.wait_ge(xn_ready, ONE + u + 1)
                    if at_least(u, 1):
                        pe.wait_ge(xnT_ready, ONE + u)
                    for e in range(ET):
                        for t in range(NT):
                            ins = pe.transpose(turned[e][:, t * P:(t + 1) * P], xn[k][:, t, e * P:(e + 1) * P], ident[:, :])
                    ins.then_inc(turned_ready, 1)

                turn(0, 0)
                pe.wait_ge(w_ready, ONE + 48)

                def body(u, j, i):
                    k = j % 2
                    pe.wait_ge(xnT_ready, ONE + u + 1)
                    for c in range(QKT):
                        if at_least(u, 1):
                            pe.wait_ge(qk_ready, ONE + QKT * u - QKT + c + 1)
                        for e in range(ET):
                            ins = pe.matmul(qk_ps[c][:, :], w[:, e, c * P:(c + 1) * P], xnT[k][:, e, :],
                                            start=(e == 0), stop=(e == ET - 1))
                        ins.then_inc(qk_ps_ready, 1)
                    if is_unit(u + 1, UNITS):
                        turn(u + 1, (j + 1) % 2)
                    for t in range(NT):
                        if t % 2 == 0 and at_least(u, 1):
                            pe.wait_ge(v_ready, ONE + 2 * u - 2 + t // 2 + 1)
                        for e in range(ET):
                            ins = pe.matmul(v_ps[t // 2][:, t % 2, :], xnT[k][:, e, t * P:(t + 1) * P], w[:, e, 2 * E:3 * E],
                                            start=(e == 0), stop=(e == ET - 1))
                        if t % 2:
                            ins.then_inc(v_ps_ready, 1)
                rounds(pe, body, UNITS, NBUF)


def attend(nc, parts_in, v_in, identb, mask, out_T):
    B, _, KT, _ = v_in.shape
    S = KT * P
    HPAD = 2 * HD
    VW = QUAD * HPAD
    with Place(nc, "att") as place:
        sb, ps, sem, sems = place.sb, place.ps, place.sem, place.sems
        q_rows = [sb(f"q{g}", [P, QUAD, S], BF16) for g in range(NQUAD)]
        k_rows = [sb(f"k{g}", [P, QUAD, S], BF16) for g in range(NQUAD)]
        v_ones = [sb(f"v{g}", [P, KT, VW]) for g in range(NQUAD)]
        maskb = sb("maskb", [P, P], BF16)
        gate = sb("gate", [1, 2])
        NPROB = 4
        probs = [sb(f"probs{i}", [P, QUAD, HALF]) for i in range(NPROB)]
        o_sb = sb("o_sb", [P, 2, HALF])
        QT = S // P
        mx = sb("mx", [P, QUAD, QT])
        neg = sb("neg", [P, QUAD * QT])
        neg_rest = sb("neg_rest", [P, QUAD * QT])
        shift = sb("shift", [P, SHIFT_ROWS, QUAD * QT], BF16)
        shift_T = sb("shift_T", [SHIFT_ROWS * QUAD * QT, P], BF16)
        row_ps = [ps(f"row_ps{i}", [P, 2, HALF]) for i in range(2)]
        NCOL = 3
        col_ps = [ps(f"col_ps{i}", [P, HALF]) for i in range(NCOL)]
        o_ps = ps("o_ps", [P, HALF])

        loaded = sems("loaded", NQUAD)
        v_loaded = sems("v_loaded", NQUAD)
        shift_loaded = sems("shift_loaded", NQUAD)
        ones_ready, gate_open = sem("ones_ready"), sem("gate_open")
        row_ready, row_used = sems("row_ready", 2), sems("row_used", 2)
        col_ready, col_used = sems("col_ready", NCOL), sems("col_used", NCOL)
        probs_masked, probs_used = sems("probs_masked", NPROB), sems("probs_used", NPROB)
        o_out = sem("o_out")
        o_stored = sem("o_stored")
        shift_ready = sem("shift_ready")
        dve_step = sem("dve_step")
        DVE_QUAD = 4

        groups = [(qt, (h, h + 1)) for qt in range(HALF // P) for h in range(0, QUAD, 2)]
        groups += [(qt, (h,)) for qt in range(HALF // P, QT) for h in range(QUAD)]
        NG = len(groups)
        RING0 = NG // 2 + 1
        RING1 = NG // 2
        TURN_AT = 6

        blocks = [(1, kt) for kt in range(KT)] + [(0, kt) for kt in range(KT // 2)]
        NB = len(blocks)
        COLS = NB * QUAD // NCOL
        BLKS = NB // NPROB

        def wait_exp(eng, q, k):
            n = k * QUAD + QUAD - 1
            eng.wait_ge(col_used[n % NCOL], ONE + COLS * q + n // NCOL + 1)

        PV_LAG = 2
        EVAC_AT = 17

        def block_columns(k):
            c, kt = blocks[k]
            first = max(0, kt * P - c * HALF)
            return c * HALF + first, first, HALF - first, kt * P >= c * HALF

        def masked_before(k):
            return sum(block_columns(j)[3] for j in range(k) if j % NPROB == k % NPROB)

        def gates_before(k):
            return sum(block_columns(j)[3] for j in range(k))

        GATES = gates_before(NB)
        MASKED = [masked_before(NB + i) for i in range(NPROB)]

        def chunks_of(g):
            qt, heads = groups[g]
            n = (qt + 1) * P
            if len(heads) == 2:
                return [(heads[i], i, 0, n, i == 1) for i in range(2)]
            return [(heads[0], 0, 0, HALF, False), (heads[0], 1, HALF, n - HALF, True)]

        def use0(q, g):
            return RING0 * q - 1 + g // 2 + (1 if g >= TURN_AT else 0) if not (isinstance(q, int) and q == 0) else g // 2

        def turn_use(q):
            if isinstance(q, int) and q == B * NQUAD - 1:
                return RING0 * (q + 1) - 1
            return RING0 * (q + 1) - 1 + TURN_AT // 2

        def use(q, g):
            return use0(q, g) if g % 2 == 0 else RING1 * q + g // 2

        def quad_loop(eng, body):
            with eng.Fori(0, B - 1) as b:
                for g in range(NQUAD):
                    body(b, g, True, True)
            for g in range(NQUAD):
                body(B - 1, g, g < NQUAD - 2, g < NQUAD - 3)

        place.start_sems()
        with nc.Block() as block:

            @block.sync
            def _(sp):
                def load(q, g, b, used=True):
                    tokens = bass.ds(b * S if isinstance(b, int) else sp.snap(b * S), S)
                    if used:
                        sp.wait_ge(probs_used[NPROB - 1], ONE + BLKS * (q - 3))
                    for rows, parts, base in ((q_rows[g], Q_PART, 0), (k_rows[g], K_PART, HEADS * HD)):
                        for i, part in enumerate(parts):
                            src = parts_in[part, base + g * QUAD * HD:base + (g + 1) * QUAD * HD, tokens]
                            sp.dma_start(rows[i * HD:(i + 1) * HD, :, :],
                                         src.rearrange("(h r) n -> r h n", r=HD)).then_inc(loaded[g], 16)
                    sp.dma_start(v_ones[g][:, :, :],
                                 v_in[bass.ds(b, 1), :, :, g * VW:(g + 1) * VW].rearrange("o p t n -> (o p) t n")
                                 ).then_inc(v_loaded[g], 16)

                def load_shift(q, g):
                    sp.wait_ge(row_used[0], ONE + turn_use(q) + 1)
                    sp.dma_start(q_rows[g][SCORE_ROWS:SCORE_ROWS + SHIFT_ROWS, :, :],
                                 shift_T[:, :]).then_inc(shift_loaded[g], 16)

                def store(q, g, b):
                    sp.wait_ge(o_out, ONE + 2 * q + 2)
                    sp.dma_start(out_T.rearrange("b r n -> (b r) n")[bass.ds(q * P, P), :], flat(o_sb[:, :, :])
                                 ).then_inc(o_stored, 16)

                for g in range(3):
                    load(g, g, 0, used=False)
                load_shift(0, 0)

                def body(b, g, two, three):
                    q = b * NQUAD + g
                    if three:
                        load(q + 3, (g + 3) % NQUAD, b + (g + 3) // NQUAD)
                    if not (isinstance(b, int) and g == NQUAD - 1):
                        load_shift(q + 1, (g + 1) % NQUAD)
                    store(q, g, b)
                quad_loop(sp, body)
                sp.wait_ge(o_stored, ONE + 16 * B * NQUAD)

            @block.gpsimd
            def _(pool):
                pool.tensor_copy(maskb[:, :], mask[:, :]).then_inc(ones_ready, 1)
                pool.memset(gate[:, :], 0.0).then_inc(gate_open, 1)
                pool.wait_ge(gate_open, ONE + 1)

                def body(b, g, two, three):
                    q = b * NQUAD + g
                    for k in range(NB):
                        _, first, width, diagonal = block_columns(k)
                        i = k % NPROB
                        if diagonal:
                            pool.wait_ge(gate_open, ONE + 1 + GATES * q + gates_before(k))
                            wait_exp(pool, q, k)
                            pool.tensor_tensor(gate[:, 1:2], gate[:, 0:1], gate[:, 0:1], ALU.add).then_inc(gate_open, 1)
                            pool.affine_select(out=probs[i][:, :, 0:P], in_=probs[i][:, :, 0:P], compare_op=ALU.is_ge, fill=0.0,
                                               base=0, pattern=[[0, QUAD], [1, P]], channel_multiplier=-1).then_inc(probs_masked[i], 1)
                quad_loop(pool, body)

            @block.scalar
            def _(act):
                def body(b, g, two, three):
                    q = b * NQUAD + g
                    for k in range(NB):
                        _, first, width, diagonal = block_columns(k)
                        i = k % NPROB
                        act.wait_ge(probs_used[i], ONE + BLKS * q + k // NPROB)
                        for h in range(QUAD):
                            n = k * QUAD + h
                            slot = n % NCOL
                            act.wait_ge(col_ready[slot], ONE + COLS * q + n // NCOL + 1)
                            ins = act.activation(probs[i][:, h, 0:width], col_ps[slot][:, 0:width], ACT.Exp, scale=float(HD) ** -0.5)
                            ins.then_inc(col_used[slot], 1)
                quad_loop(act, body)

            @block.vector
            def _(dve):
                def reduce_group(q, gi):
                    qt, heads = groups[gi]
                    n = (qt + 1) * P
                    slot = gi % 2
                    dve.wait_ge(row_ready[slot], ONE + use(q, gi) + 1)
                    if len(heads) == 2:
                        src, dst = row_ps[slot][:, :, 0:n], mx[:, heads[0]:heads[0] + 2, qt]
                    else:
                        src, dst = flat(row_ps[slot][:, :, :])[:, 0:n], mx[:, heads[0], qt:qt + 1]
                    dve.tensor_reduce(dst, src, AX.X, ALU.max).then_inc(row_used[slot], 1)

                def turn_shift(q):
                    dve.wait_ge(row_ready[0], ONE + turn_use(q) + 1)
                    g, b = shift_slot_before[0]
                    dve.wait_ge(shift_loaded[g], ONE + 16 * b)
                    rows = SHIFT_ROWS * QUAD * QT
                    dve.tensor_copy(shift_T[:, :], row_ps[0][0:rows, 0, 0:P // 2].bitcast(BF16)).then_inc(row_used[0], 1)

                def split_maxima(q):
                    dve.wait_ge(row_used[0], ONE + use(q, NG - 2) + 1)
                    dve.wait_ge(row_used[1], ONE + use(q, NG - 1) + 1)
                    step = Steps(dve, dve_step, q * DVE_QUAD, DVE_QUAD)
                    mxf = flat(mx[:, :, :])
                    step.done(dve.tensor_scalar(shift[:, 0, :], mxf, -1.0, None, ALU.mult))
                    step.done(dve.tensor_scalar(neg[:, :], mxf, -1.0, None, ALU.mult))
                    step.wait()
                    step.done(dve.tensor_tensor(neg_rest[:, :], neg[:, :], shift[:, 0, :], ALU.subtract))
                    step.wait()
                    step.done(dve.tensor_copy(shift[:, 1, :], neg_rest[:, :]))
                    step.wait()
                    step.end()
                    dve.tensor_tensor(shift[:, 2, :], neg_rest[:, :], shift[:, 1, :], ALU.subtract).then_inc(shift_ready, 1)

                def evacuate(q, n):
                    k = (KT, NB)[n] - 1
                    dve.wait_ge(probs_used[k % NPROB], ONE + BLKS * q + k // NPROB + 1)
                    dve.wait_ge(o_stored, ONE + 16 * q)
                    dve.tensor_copy(o_sb[:, 1 - n, :], o_ps[:, :]).then_inc(o_out, 1)

                for g in range(NQUAD):
                    dve.memset(k_rows[g][SCORE_ROWS:P, :, :], 1.0).then_inc(ones_ready, 1)
                shift_slot_before = [None]
                for gi in range(NG):
                    reduce_group(0, gi)
                split_maxima(0)
                for gi in range(NG):
                    if gi == TURN_AT:
                        shift_slot_before[0] = (0, 0)
                        turn_shift(0)
                    reduce_group(1, gi)
                split_maxima(1)

                def body(b, g, two, three):
                    q = b * NQUAD + g
                    shift_slot_before[0] = (g, b + 1)
                    if two:
                        for gi in range(NG):
                            if gi == TURN_AT:
                                turn_shift(q + 1)
                            if gi == EVAC_AT:
                                evacuate(q, 0)
                            reduce_group(q + 2, gi)
                        split_maxima(q + 2)
                    else:
                        if g == NQUAD - 2:
                            turn_shift(q + 1)
                        evacuate(q, 0)
                    evacuate(q, 1)
                quad_loop(dve, body)

            @block.tensor
            def _(pe):
                def row_chunk(q, g, n):
                    gi, part = n // 2, n % 2
                    qt, heads = groups[gi]
                    slot = gi % 2
                    h, bank, k0, width, last = chunks_of(gi)[part]
                    if part == 0:
                        pe.wait_ge(row_used[slot], ONE + use(q, gi))
                    dst = row_ps[slot][:, bank, 0:width]
                    diagonal = k0 + width == (qt + 1) * P
                    ins = pe.matmul(dst, q_rows[g][0:SCORE_ROWS, h, qt * P:(qt + 1) * P], k_rows[g][0:SCORE_ROWS, h, k0:k0 + width],
                                    start=True, stop=True)
                    if diagonal:
                        ins = pe.matmul(row_ps[slot][:, bank, width - P:width], identb[:, :], maskb[:, :],
                                        start=False, stop=True, skip_group_check=True)
                    if part == 1:
                        ins.then_inc(row_ready[slot], 1)

                def turn(q):
                    pe.wait_ge(shift_ready, ONE + q + 1)
                    pe.wait_ge(row_used[0], ONE + turn_use(q))
                    rows = SHIFT_ROWS * QUAD * QT
                    pe.transpose(row_ps[0][0:rows, 0, 0:P // 2].bitcast(BF16), shift[:, :, :].rearrange("p a b -> p (a b)"),
                                 identb[:, :]).then_inc(row_ready[0], 1)

                def rows_until(q, g, done, until):
                    for n in range(done, until):
                        if n == 2 * TURN_AT:
                            if not (isinstance(q, int) and q == 0):
                                turn(q - 1)
                        row_chunk(q, g, n)

                def pv(q, g, b, k):
                    c, kt = blocks[k]
                    _, first, width, diagonal = block_columns(k)
                    i = k % NPROB
                    if k == 0:
                        pe.wait_ge(v_loaded[g], ONE + 16 * b + 16)
                    if kt == 0:
                        pe.wait_ge(o_out, ONE + 2 * q + (1 - c))
                    if diagonal:
                        pe.wait_ge(probs_masked[i], ONE + MASKED[i] * q + masked_before(k) + 1)
                    else:
                        wait_exp(pe, q, k)
                    last = kt == (KT - 1 if c else KT // 2 - 1)
                    for h in range(QUAD):
                        ins = pe.matmul(o_ps[h * HPAD:(h + 1) * HPAD, first:HALF], v_ones[g][:, kt, h * HPAD:(h + 1) * HPAD],
                                        probs[i][:, h, 0:width], start=(kt == 0), stop=last, skip_group_check=True)
                    ins.then_inc(probs_used[i], 1)

                def body(b, g, two, three):
                    q = b * NQUAD + g
                    g2, b2 = (g + 2) % NQUAD, b + (g + 2) // NQUAD
                    if two:
                        pe.wait_ge(loaded[g2], ONE + 16 * 12 * (b2 + 1))
                    pe.wait_ge(shift_loaded[g], ONE + 16 * (b + 1))
                    done = 0
                    for k in range(NB):
                        q0, first, width, diagonal = block_columns(k)
                        kt = blocks[k][1]
                        more = (4, 3, 3)[k % 3]
                        for h in range(QUAD):
                            n = k * QUAD + h
                            slot = n % NCOL
                            pe.wait_ge(col_used[slot], ONE + COLS * q + n // NCOL)
                            ins = pe.matmul(col_ps[slot][:, 0:width], k_rows[g][0:SCORE_ROWS + SHIFT_ROWS, h, kt * P:(kt + 1) * P],
                                            q_rows[g][0:SCORE_ROWS + SHIFT_ROWS, h, q0:q0 + width], start=True, stop=True)
                            ins.then_inc(col_ready[slot], 1)
                            if two and h < more:
                                rows_until(q + 2, g2, done, done + 1)
                                done += 1
                        if not two and g == NQUAD - 2 and k == 3:
                            turn(q + 1)
                        if k >= PV_LAG:
                            pv(q, g, b, k - PV_LAG)
                    for k in range(NB - PV_LAG, NB):
                        if two:
                            rows_until(q + 2, g2, done, done + 4)
                            done += 4
                        pv(q, g, b, k)
                    assert not two or done == 2 * NG

                pe.wait_ge(ones_ready, ONE + NQUAD + 1)
                for g in range(2):
                    pe.wait_ge(loaded[g], ONE + 16 * 12)
                    rows_until(g, g, 0, 2 * NG)
                quad_loop(pe, body)


def close_attention(nc, x, att_T, w_out, b_out, ident, inverse_out, x1_out, xf_out, xfT):
    B, S, E = x.shape
    HALVES, NT, ET = S // HALF, HALF // P, E // P
    UNITS = B * HALVES
    TB = E // HD // ET
    with Place(nc, "close") as place:
        sb, ps, sem, sems = place.sb, place.ps, place.sem, place.sems
        NBUF = 4
        w = sb("w", [P, ET, E])
        bo = sb("bo", [1, E])
        ones = sb("ones", [1, P])
        minus_half = sb("minus_half", [P, NT])
        num = [sb(f"num{j}", [P, ET, HALF]) for j in range(NBUF)]
        inv = [sb(f"inv{j}", [P, ET, HALF]) for j in range(NBUF)]
        xs = [sb(f"x{j}", [P, NT, E]) for j in range(NBUF)]
        x1 = [sb(f"x1{j}", [P, NT, E]) for j in range(NBUF)]
        xf = [sb(f"xf{j}", [P, NT, E]) for j in range(2)]
        moments = [[Moments(place, f"m{i}{k}", NT) for k in range(2)] for i in range(2)]
        rstd = [[sb(f"rstd{i}{k}", [P, NT]) for k in range(2)] for i in range(2)]
        h_ps = [ps(f"h_ps{k}", [P, NT, E]) for k in range(2)]
        turned = [ps(f"turned{t}", [P, HALF]) for t in range(ET)]

        w_ready, const_ready = sem("w_ready"), sem("const_ready")
        den_ready, inverse_made, inverse_ready = sem("den_ready"), sem("inverse_made"), sem("inverse_ready")
        in_ready, x_ready = sems("in_ready", NBUF), sems("x_ready", NBUF)
        att_ready = sem("att_ready")
        h_ready = sem("h_ready")
        ve_ready, rstd_ready = sems("ve_ready", 2), sems("rstd_ready", 2)
        hn_ready, x1_ready, xf_ready = sem("hn_ready"), sem("x1_ready"), sem("xf_ready")
        turned_ready, xfT_ready = sem("turned_ready"), sem("xfT_ready")
        x1_stored, xf_stored = sems("x1_stored", NBUF), sems("xf_stored", 2)
        dve_step = sem("dve_step")
        STEPS = NT + Moments.STEPS

        place.start_sems()
        with nc.Block() as block:

            @block.sync
            def _(sp):
                den_rows = att_T.rearrange("b (h r) n -> (b h) r n", r=2 * HD)[:, HD, :]
                sp.dma_start(flat(num[0][:, :, :]), den_rows).then_inc(den_ready, 16)
                sp.dma_start(w[:, :, :], w_out.rearrange("(t p) n -> p t n", p=P)).then_inc(w_ready, 16)
                sp.dma_start(bo[:, :], b_out.unsqueeze(0)).then_inc(w_ready, 16)
                sp.wait_ge(inverse_made, ONE + 1)
                sp.dma_start(inverse_out.rearrange("b h n -> (b h) n"), flat(inv[0][:, :, :])).then_inc(inverse_ready, 16)
                sp.wait_ge(inverse_ready, ONE + 16)
                sp.wait_ge(w_ready, ONE + 32)

            @block.vector
            def _(dve):
                dve.wait_ge(den_ready, ONE + 16)
                dve.reciprocal(inv[0][:, :, :], num[0][:, :, :]).then_inc(inverse_made, 1)

            @block.gpsimd
            def _(pool):
                pool.memset(minus_half[:, :], -0.5).then_inc(const_ready, 1)
                pool.memset(ones[:, :], 1.0).then_inc(const_ready, 1)
                pool.wait_ge(const_ready, ONE + 2)

        with nc.Block() as block:

            @block.sync
            def _(sp):
                def place_of(i, j):
                    b, j = (i + j // NBUF) * (NBUF // HALVES) + j % NBUF // HALVES, j % NBUF
                    return bass.ds(b if isinstance(b, int) else sp.snap(b), 1), slice(j % HALVES * HALF, (j % HALVES + 1) * HALF)

                def tokens_of(a, rows):
                    return a.rearrange("b n e -> (b n) e")[rows, :].rearrange("(t p) e -> p t e", p=P)

                def tokens(a, b, n):
                    return a[b, n, :].rearrange("o (t p) e -> p (o t) e", p=P)

                def load(i, j, again):
                    b, n = place_of(i, j)
                    k, r = j % NBUF, i + j // NBUF
                    rows = att_T[b, :, n].rearrange("o (t h r) n -> (o t) h r n", t=ET, r=2 * HD)
                    inverses = inverse_out[b, :, n].rearrange("o (t h) n -> (o t) h n", t=ET)
                    if again:
                        sp.wait_ge(h_ready, ONE + NBUF * r + k - NBUF + 1)
                    for t in range(ET):
                        sp.dma_start(num[k][:, t, :], rows[t, :, 0:HD, :]).then_inc(in_ready[k], 16)
                        sp.dma_start(inv[k][:, t, :], inverses[t].unsqueeze(1).to_broadcast([TB, HD, HALF])).then_inc(in_ready[k], 16)
                    if again:
                        sp.wait_ge(x1_ready, ONE + NBUF * r + k - NBUF + 1)
                    sp.dma_start(xs[k][:, :, :], tokens(x, b, n)).then_inc(x_ready[k], 16)

                AHEAD = NBUF - 1
                for j in range(AHEAD):
                    load(0, j, False)

                def body(u, j, i):
                    if is_unit(u + AHEAD, UNITS):
                        load(i, j + AHEAD, at_least(u, NBUF - AHEAD))
                    if is_unit(u - 1, UNITS):
                        first = (u - 1) * HALF
                        rows = bass.ds(first if isinstance(u, int) else sp.snap(first), HALF)
                        sp.wait_ge(xf_ready, ONE + u)
                        sp.dma_start(tokens_of(x1_out, rows), x1[(j - 1) % NBUF][:, :, :]).then_inc(x1_stored[(j - 1) % NBUF], 16)
                        sp.dma_start(tokens_of(xf_out, rows), xf[(j - 1) % 2][:, :, :]).then_inc(xf_stored[(j - 1) % 2], 16)

                rounds(sp, body, UNITS, NBUF, extra=1)
                for j in range(NBUF):
                    sp.wait_ge(x1_stored[j], ONE + 16 * (UNITS // NBUF))
                for j in range(2):
                    sp.wait_ge(xf_stored[j], ONE + 16 * (UNITS // 2))

            @block.gpsimd
            def _(pool):
                def divide(u, j, i):
                    k = j % NBUF
                    pool.wait_ge(in_ready[k], ONE + 64 * (i + j // NBUF + 1))
                    pool.tensor_tensor(num[k][:, :, :], num[k][:, :, :], inv[k][:, :, :], ALU.mult).then_inc(att_ready, 1)

                for j in range(2):
                    divide(j, j, 0)

                def body(u, j, i):
                    if is_unit(u, UNITS):
                        pool.wait_ge(ve_ready[0], ONE + u + 1)
                        pool.tensor_tensor(rstd[0][j % 2][:, :], moments[0][j % 2].ve[:, :], minus_half[:, :], ALU.pow).then_inc(rstd_ready[0], 1)
                    if is_unit(u - 1, UNITS):
                        k = (j - 1) % 2
                        pool.wait_ge(ve_ready[1], ONE + u)
                        pool.tensor_tensor(rstd[1][k][:, :], moments[1][k].ve[:, :], minus_half[:, :], ALU.pow).then_inc(rstd_ready[1], 1)
                    if is_unit(u, UNITS):
                        pool.wait_ge(hn_ready, ONE + u + 1)
                        pool.wait_ge(x_ready[j], ONE + 16 * (i + 1))
                        pool.tensor_tensor(x1[j][:, :, :], x1[j][:, :, :], xs[j][:, :, :], ALU.add).then_inc(x1_ready, 1)
                    if is_unit(u + 2, UNITS):
                        divide(u + 2, j + 2, i)
                rounds(pool, body, UNITS, NBUF, extra=1)

            @block.vector
            def _(dve):
                def body(u, j, i):
                    now, before = is_unit(u, UNITS), is_unit(u - 1, UNITS)
                    at = 0 if isinstance(u, int) and u == 0 else 2 * STEPS * u - STEPS
                    step = Steps(dve, dve_step, at, STEPS * (now + before))
                    k, kb = j % 2, (j - 1) % 2
                    if now:
                        dve.wait_ge(h_ready, ONE + u + 1)
                        moments[0][k].of(dve, step, [h_ps[k][:, t, :] for t in range(NT)], E).then_inc(ve_ready[0], 1)
                    if before:
                        dve.wait_ge(x1_ready, ONE + u)
                        moments[1][kb].of(dve, step, [x1[(j - 1) % NBUF][:, t, :] for t in range(NT)], E).then_inc(ve_ready[1], 1)
                    if now:
                        dve.wait_ge(rstd_ready[0], ONE + u + 1)
                        if at_least(u, NBUF):
                            dve.wait_ge(x1_stored[j], ONE + 16 * i)
                        for t in range(NT):
                            ins = dve.tensor_scalar(x1[j][:, t, :], h_ps[k][:, t, :], moments[0][k].mean[:, t:t + 1],
                                                    rstd[0][k][:, t:t + 1], ALU.subtract, ALU.mult)
                        ins.then_inc(hn_ready, 1)
                    if before:
                        dve.wait_ge(rstd_ready[1], ONE + u)
                        if at_least(u, 3):
                            dve.wait_ge(xf_stored[kb], ONE + 16 * (i * (NBUF // 2) + (j - 1 - kb) // 2))
                            dve.wait_ge(turned_ready, ONE + u - 2)
                        for t in range(NT):
                            ins = dve.tensor_scalar(xf[kb][:, t, :], x1[(j - 1) % NBUF][:, t, :], moments[1][kb].mean[:, t:t + 1],
                                                    rstd[1][kb][:, t:t + 1], ALU.subtract, ALU.mult)
                        ins.then_inc(xf_ready, 1)
                    step.end()
                rounds(dve, body, UNITS, NBUF, extra=1)

            @block.scalar
            def _(act):
                with act.Fori(0, UNITS) as u:
                    act.wait_ge(turned_ready, ONE + u + 1)
                    for t in range(ET):
                        ins = act.activation(xfT[:, t, bass.ds(u * HALF, HALF)], turned[t][:, :], ACT.Copy)
                    ins.then_inc(xfT_ready, 1)

            @block.tensor
            def _(pe):
                def project(u, j):
                    k = j % 2
                    pe.wait_ge(att_ready, ONE + u + 1)
                    if at_least(u, 2):
                        pe.wait_ge(hn_ready, ONE + u - 1)
                    for t in range(NT):
                        pe.matmul(h_ps[k][:, t, :], ones[:, :], bo[:, :], start=(t % 2 == 0), stop=False, skip_group_check=True)
                        for e in range(ET):
                            ins = pe.matmul(h_ps[k][:, t, :], num[j % NBUF][:, e, t * P:(t + 1) * P], w[:, e, :],
                                            start=False, stop=(e == ET - 1), skip_group_check=True)
                    ins.then_inc(h_ready, 1)

                project(0, 0)

                def body(u, j, i):
                    if is_unit(u + 1, UNITS):
                        project(u + 1, j + 1)
                    if is_unit(u - 1, UNITS):
                        pe.wait_ge(xf_ready, ONE + u)
                        if at_least(u, 2):
                            pe.wait_ge(xfT_ready, ONE + u - 1)
                        for e in range(ET):
                            for t in range(NT):
                                ins = pe.transpose(turned[e][:, t * P:(t + 1) * P], xf[(j - 1) % 2][:, t, e * P:(e + 1) * P], ident[:, :])
                        ins.then_inc(turned_ready, 1)
                rounds(pe, body, UNITS, NBUF, extra=1)


def dispatch_and_experts(nc, res, xf_in, phi, w_exp, b_exp, ident, y_out):
    B, S, E = xf_in.shape
    _, NEXP, SLOTS = phi.shape
    ET, MT = E // P, S // P
    CHUNKS = NEXP * SLOTS // P
    PER = P // SLOTS
    xfT, phi_sb, row_max = res
    with Place(nc, "disp") as place:
        sb, ps, sem, sems = place.sb, place.ps, place.sem, place.sems
        NPROB = 4
        xf = sb("xf", [P, B * MT, E])
        probs = [sb(f"probs{i}", [P, B, P]) for i in range(NPROB)]
        batch_max = sb("batch_max", [P, P])
        total = sb("total", [P, P])
        inverse = [sb(f"inverse{i}", [P, P]) for i in range(2)]
        step_max = sb("step_max", [P, B])
        slots_sb = sb("slots_sb", [P, B, E])
        slots_T = sb("slots_T", [P, ET, B, P])
        w_sb = sb("w_sb", [P, PER, ET, E])
        bias = sb("bias", [P, E])
        y_sb = sb("y_sb", [P, B, E])
        ring = [ps(f"ring{i}", [P, B, P]) for i in range(2)]
        slots_ps = ps("slots_ps", [P, B, E])

        xf_ready, w_ready = sem("xf_ready"), sem("w_ready")
        ring_ready, ring_used = sems("ring_ready", 2), sems("ring_used", 2)
        shifted = sem("shifted")
        exp_ready, probs_ready = sem("exp_ready"), sem("probs_ready")
        inverse_ready = sem("inverse_ready")
        slots_ready = sem("slots_ready")
        slots_out = sem("slots_out")
        y_stored = sem("y_stored")
        dve_step = sem("dve_step")
        USES = ([("L", 0), ("L", 2), ("T", 0), ("L", 3), ("L", 4), ("L", 6)],
                [("L", 1), ("T", 1), ("Y", 1), ("Y", 0), ("L", 5), ("L", 7)])

        def use(c, what, i):
            slot = next(r for r in range(2) if (what, i) in USES[r])
            seen, at = USES[slot], c if what == "L" else c + 1
            logits_only = [x for x in seen if x[0] == "L"]
            if isinstance(at, int) and at == 0:
                return slot, logits_only.index((what, i))
            if isinstance(at, int) and at == CHUNKS:
                seen = [x for x in seen if x[0] != "L"]
            return slot, (at - 1) * len(USES[slot]) + len(logits_only) + seen.index((what, i))

        def chunk_loop(eng, body, last):
            body(0, False)
            with eng.Fori(1, CHUNKS) as c:
                body(c, True)
            last()

        place.start_sems()
        with nc.Block() as block:

            @block.sync
            def _(sp):
                sp.dma_start(xf[:, :, :], xf_in.rearrange("b (m p) e -> p (b m) e", p=P)).then_inc(xf_ready, 16)

                def load_experts(c):
                    sp.dma_start(w_sb[:, :, :, :].rearrange("p x t e -> p (x t) e"),
                                 w_exp[bass.ds(c * PER, PER), :, :].rearrange("x (t p) e -> p (x t) e", p=P)).then_inc(w_ready, 16)
                    for x in range(PER):
                        sp.dma_start(bias[x * SLOTS:(x + 1) * SLOTS, :],
                                     b_exp[bass.ds(c * PER + x, 1), :].to_broadcast([SLOTS, E])).then_inc(w_ready, 16)

                def store(c):
                    slot, n = use(c, "Y", 0)
                    sp.wait_ge(ring_used[slot], ONE + n + 1)
                    sp.dma_start(y_out[:, bass.ds(c, 1), :, :].rearrange("b o p e -> p (b o) e"), y_sb[:, :, :]).then_inc(y_stored, 16)

                def body(c, before):
                    if before:
                        store(c - 1)
                        load_experts(c)
                    else:
                        load_experts(c)
                chunk_loop(sp, body, lambda: store(CHUNKS - 1))
                sp.wait_ge(y_stored, ONE + 16 * CHUNKS)

            @block.vector
            def _(dve):
                PER_CHUNK = 3 * MT
                buf = lambda t: probs[t % NPROB][:, :, :]

                def logits(c, t, step):
                    slot, uses = use(c, "L", t)
                    dve.wait_ge(ring_ready[slot], ONE + uses + 1)
                    step.wait()
                    step.done(dve.tensor_reduce(batch_max[:, :], ring[slot][:, :, :].rearrange("p b n -> p n b"), AX.X, ALU.max))
                    n = MT * c + t
                    if not (isinstance(c, int) and c == 0 and t < NPROB):
                        dve.wait_ge(slots_ready, ONE + n - NPROB + 1)
                    step.wait()
                    dve.tensor_tensor(buf(t), ring[slot][:, :, :], batch_max[:, :].unsqueeze(1).to_broadcast([P, B, P]),
                                      ALU.subtract).then_inc(shifted, 1)
                    dve.tensor_reduce(step_max[:, :], ring[slot][:, :, :], AX.X, ALU.max).then_inc(ring_used[slot], 1)
                    dve.wait_ge(ring_used[slot], ONE + uses + 1)
                    step.done(dve.tensor_tensor(row_max[:, t, :], row_max[:, t, :], step_max[:, :], ALU.max))

                def sums(c, t, step):
                    n = MT * c + t
                    dve.wait_ge(exp_ready, ONE + n + 1)
                    dve.wait_ge(inverse_ready, ONE + n)
                    step.done(dve.tensor_reduce(total[:, :], buf(t).rearrange("p b n -> p n b"), AX.X, ALU.add))
                    if not (isinstance(c, int) and c == 0 and t < 2):
                        dve.wait_ge(probs_ready, ONE + n - 1)
                    step.wait()
                    dve.reciprocal(inverse[t % 2][:, :], total[:, :]).then_inc(inverse_ready, 1)

                def add_bias(c, j):
                    dve.wait_ge(w_ready, ONE + 16 * (1 + PER) * (c + 1))
                    dve.wait_ge(y_stored, ONE + 16 * c)
                    slot, n = use(c, "Y", j)
                    dve.wait_ge(ring_ready[slot], ONE + n + 1)
                    out = y_sb[:, j * B // 2:(j + 1) * B // 2, :]
                    dve.tensor_tensor(out, ring[slot][:, :, :].rearrange("p b n -> p (b n)").rearrange("p (b e) -> p b e", e=E),
                                      bias[:, :].unsqueeze(1).to_broadcast([P, B // 2, E]), ALU.add).then_inc(ring_used[slot], 1)

                def body(c, before):
                    step = Steps(dve, dve_step, 1 + c * PER_CHUNK, PER_CHUNK)
                    for t in range(MT):
                        if before and t == 3:
                            add_bias(c - 1, 1)
                        logits(c, t, step)
                        sums(c, t, step)
                        if before and t == 3:
                            add_bias(c - 1, 0)
                    step.end()
                dve.memset(row_max[:, :, :], NEG).then_inc(dve_step, 1)

                def last():
                    for j in (1, 0):
                        add_bias(CHUNKS - 1, j)
                chunk_loop(dve, body, last)

            @block.scalar
            def _(act):
                def slots_away(c):
                    act.wait_ge(slots_ready, ONE + MT * c + MT)
                    act.activation(slots_sb[:, :, :], slots_ps[:, :, :], ACT.Copy).then_inc(slots_out, 1)

                def turned(c):
                    for j in (1, 0):
                        slot, n = use(c, "T", j)
                        act.wait_ge(ring_ready[slot], ONE + n + 1)
                        act.activation(slots_T[:, :, j * B // 2:(j + 1) * B // 2, :].rearrange("p t b n -> p t (b n)"),
                                       ring[slot][:, :, :].rearrange("p (t b) n -> p t (b n)", t=ET), ACT.Copy).then_inc(ring_used[slot], 1)

                def body(c, before):
                    for t in range(MT):
                        act.wait_ge(shifted, ONE + MT * c + t + 1)
                        act.activation(probs[t % NPROB][:, :, :], probs[t % NPROB][:, :, :], ACT.Exp).then_inc(exp_ready, 1)
                        if before and t == 1:
                            slots_away(c - 1)
                        if before and t == 2:
                            turned(c - 1)

                def last():
                    slots_away(CHUNKS - 1)
                    turned(CHUNKS - 1)
                chunk_loop(act, body, last)

            @block.gpsimd
            def _(pool):
                def body(c, before):
                    for t in range(MT):
                        n = MT * c + t
                        pool.wait_ge(inverse_ready, ONE + n + 1)
                        pool.tensor_tensor(probs[t % NPROB][:, :, :], probs[t % NPROB][:, :, :],
                                           inverse[t % 2][:, :].unsqueeze(1).to_broadcast([P, B, P]), ALU.mult).then_inc(probs_ready, 1)
                body(0, False)
                with pool.Fori(1, CHUNKS) as c:
                    body(c, True)

            @block.tensor
            def _(pe):
                def logits(c, t):
                    slot, n = use(c, "L", t)
                    pe.wait_ge(ring_used[slot], ONE + n)
                    for b in range(B):
                        for e in range(ET):
                            ins = pe.matmul(ring[slot][:, b, :], xfT[:, e, b * S + t * P:b * S + (t + 1) * P],
                                            phi_sb[:, e, bass.ds(c * P, P)], start=(e == 0), stop=(e == ET - 1), skip_group_check=True)
                    ins.then_inc(ring_ready[slot], 1)

                def slots(c, t):
                    n = MT * c + t
                    pe.wait_ge(probs_ready, ONE + n + 1)
                    if t == 0:
                        pe.wait_ge(slots_out, ONE + c)
                    for b in range(B):
                        ins = pe.matmul(slots_ps[:, b, :], probs[t % NPROB][:, b, :], xf[:, b * MT + t, :],
                                        start=(t == 0 and b % 2 == 0), stop=(t == MT - 1), skip_group_check=True)
                    ins.then_inc(slots_ready, 1)

                def turn_slots(c):
                    pe.wait_ge(slots_out, ONE + c + 1)
                    for j in (1, 0):
                        slot, n = use(c, "T", j)
                        pe.wait_ge(ring_used[slot], ONE + n)
                        for e in range(ET):
                            for b in range(B // 2):
                                ins = pe.transpose(ring[slot][:, e * B // 2 + b, :], slots_sb[:, j * B // 2 + b, e * P:(e + 1) * P], ident[:, :])
                        ins.then_inc(ring_ready[slot], 1)

                def experts(c, j):
                    pe.wait_ge(w_ready, ONE + 16 * (1 + PER) * (c + 1))
                    slot, n = use(c, "T", j)
                    pe.wait_ge(ring_used[slot], ONE + n + 1)
                    slot, n = use(c, "Y", j)
                    pe.wait_ge(ring_used[slot], ONE + n)
                    y_ps = ring[slot][:, :, :].rearrange("p b n -> p (b n)").rearrange("p (b e) -> p b e", e=E)
                    for b in range(B // 2):
                        for e in range(ET):
                            for x in range(PER):
                                ins = pe.matmul(y_ps[x * SLOTS:(x + 1) * SLOTS, b, :],
                                                slots_T[:, e, j * B // 2 + b, x * SLOTS:(x + 1) * SLOTS], w_sb[:, x, e, :],
                                                start=(e == 0 and b % 2 == 0), stop=(e == ET - 1), skip_group_check=True)
                    ins.then_inc(ring_ready[slot], 1)

                def body(c, before):
                    logits(c, 0)
                    if before:
                        slots(c - 1, MT - 2)
                    logits(c, 1)
                    if before:
                        slots(c - 1, MT - 1)
                    logits(c, 2)
                    slots(c, 0)
                    if before:
                        turn_slots(c - 1)
                    slots(c, 1)
                    if before:
                        experts(c - 1, 1)
                    logits(c, 3)
                    if before:
                        experts(c - 1, 0)
                    for t in range(4, MT):
                        logits(c, t)
                        slots(c, t - 2)

                def last():
                    slots(CHUNKS - 1, MT - 2)
                    slots(CHUNKS - 1, MT - 1)
                    turn_slots(CHUNKS - 1)
                    for j in (1, 0):
                        experts(CHUNKS - 1, j)
                pe.wait_ge(xf_ready, ONE + 16)
                chunk_loop(pe, body, last)


def combine(nc, res, y_in, x1, ident, identb, out):
    B, CHUNKS, _, E = y_in.shape
    xfT, phi_sb, row_max = res
    S = x1.shape[1]
    ET, MT, HALVES, NT = E // P, S // P, S // HALF, HALF // P
    W = E + 2
    with Place(nc, "comb") as place:
        sb, ps, sem, sems = place.sb, place.ps, place.sem, place.sems
        neg, rest = sb("neg", [P, B, MT]), sb("rest", [P, B, MT])
        part = [sb(f"part{i}", [P, B, MT], BF16) for i in range(SHIFT_ROWS)]
        part_T = sb("part_T", [B * MT, SHIFT_ROWS, P], BF16)
        shift = sb("shift", [P, B * S], BF16)
        ones = sb("ones", [P, P], BF16)
        NPROB = 4
        probs = [sb(f"probs{i}", [P, HALF]) for i in range(NPROB)]
        y = [sb(f"y{i}", [P, CHUNKS, W]) for i in range(2)]
        x1_sb = [sb(f"x1{i}", [P, NT, E]) for i in range(2)]
        h = [sb(f"h{i}", [P, NT, E]) for i in range(2)]
        inverse = sb("inverse", [P, NT])
        minus_half = sb("minus_half", [P, NT])
        rstd = sb("rstd", [P, NT])
        moments = Moments(place, "h", NT)
        mean, ve = moments.mean, moments.ve
        logit_ps = [ps(f"logit_ps{i}", [P, HALF]) for i in range(NPROB)]
        o_ps = ps("o_ps", [P, NT, HALF])

        const_ready, part_ready, turned, part_T_ready, shift_ready = (
            sem(n) for n in ("const_ready", "part_ready", "turned", "part_T_ready", "shift_ready"))
        y_ready = sems("y_ready", 2)
        x1_ready, o_stored = sems("x1_ready", 2), sems("o_stored", 2)
        logit_ready, exp_ready, prob_used = sems("logit_ready", NPROB), sems("exp_ready", NPROB), sems("prob_used", NPROB)
        o_out = sem("o_out")
        ve_ready, rstd_ready, hn_ready = sem("ve_ready"), sem("rstd_ready"), sem("hn_ready")
        out_ready = sems("out_ready", 2)
        dve_step = sem("dve_step")
        USES = CHUNKS // NPROB
        DVE_HALF = NT + Moments.STEPS + 1

        place.start_sems()
        with nc.Block() as block:

            @block.gpsimd
            def _(pool):
                pool.memset(minus_half[:, :], -0.5).then_inc(const_ready, 1)
                pool.memset(ones[:, :], 1.0).then_inc(const_ready, 1)
                pool.memset(shift[:, :], 0.0).then_inc(const_ready, 1)
                for i in range(2):
                    pool.memset(y[i][:, :, E:W], 1.0).then_inc(const_ready, 1)
                pool.wait_ge(const_ready, ONE + 5)

            @block.vector
            def _(dve):
                step = Steps(dve, dve_step, 0, 5)
                maxima = row_max[:, :, :].rearrange("p m b -> p b m")
                step.done(dve.tensor_scalar(neg[:, :, :], maxima, -1.0, None, ALU.mult))
                step.done(dve.tensor_scalar(part[0][:, :, :], maxima, -1.0, None, ALU.mult))
                step.wait()
                step.done(dve.tensor_tensor(rest[:, :, :], neg[:, :, :], part[0][:, :, :], ALU.subtract))
                step.wait()
                step.done(dve.tensor_copy(part[1][:, :, :], rest[:, :, :]))
                step.wait()
                step.done(dve.tensor_tensor(part[2][:, :, :], rest[:, :, :], part[1][:, :, :], ALU.subtract))
                step.end()
                for i in range(SHIFT_ROWS):
                    dve.wait_ge(turned, ONE + i + 1)
                    dve.tensor_copy(part_T[:, i, :], logit_ps[i][0:B * MT, 0:P // 2].bitcast(BF16)).then_inc(part_T_ready, 1)

            @block.tensor
            def _(pe):
                pe.wait_ge(dve_step, ONE + 5)
                for i in range(SHIFT_ROWS):
                    pe.transpose(logit_ps[i][0:B * MT, 0:P // 2].bitcast(BF16), flat(part[i][:, :, :]), identb[:, :]).then_inc(turned, 1)

            @block.sync
            def _(sp):
                sp.wait_ge(part_T_ready, ONE + SHIFT_ROWS)
                sp.wait_ge(const_ready, ONE + 3)
                for i in range(SHIFT_ROWS):
                    sp.dma_start(shift[i:i + 1, :].rearrange("o (m q) -> o m q", q=P), part_T[:, i, :]).then_inc(shift_ready, 16)
                sp.wait_ge(shift_ready, ONE + 16 * SHIFT_ROWS)

        def batch_loop(eng, body):
            with eng.Fori(0, B // 2 - 1) as pair:
                for j in range(2):
                    body(2 * pair + j, j, pair, True)
            for j in range(2):
                body(B - 2 + j, j, B // 2 - 1, j == 0)

        with nc.Block() as block:

            @block.sync
            def _(sp):
                def load_y(b, j):
                    sp.dma_start(y[j][:, :, 0:E], y_in[bass.ds(b, 1), :, :, :].rearrange("o c p e -> p (o c) e")).then_inc(y_ready[j], 16)
                load_y(0, 0)

                def body(b, j, pair, after):
                    if after:
                        if j == 0:
                            sp.wait_ge(prob_used[NPROB - 1], ONE + USES * HALVES * b)
                            load_y(b + 1, 1)
                        else:
                            sp.wait_ge(prob_used[NPROB - 1], ONE + USES * HALVES * b)
                            load_y(b + 1, 0)
                    for s in range(HALVES):
                        tokens = lambda a: a[bass.ds(b, 1), s * HALF:(s + 1) * HALF, :].rearrange("o (t p) e -> p (o t) e", p=P)
                        sp.wait_ge(out_ready[s], ONE + b)
                        sp.dma_start(x1_sb[s][:, :, :], tokens(x1)).then_inc(x1_ready[s], 16)
                    for s in range(HALVES):
                        tokens = lambda a: a[bass.ds(b, 1), s * HALF:(s + 1) * HALF, :].rearrange("o (t p) e -> p (o t) e", p=P)
                        sp.wait_ge(out_ready[s], ONE + b + 1)
                        sp.dma_start(tokens(out), h[s][:, :, :]).then_inc(o_stored[s], 16)
                batch_loop(sp, body)
                for s in range(HALVES):
                    sp.wait_ge(o_stored[s], ONE + 16 * B)

            @block.scalar
            def _(act):
                def body(b, j, pair, after):
                    for s in range(HALVES):
                        u = b * HALVES + s
                        for c in range(CHUNKS):
                            i, n = c % NPROB, USES * u + c // NPROB
                            act.wait_ge(logit_ready[i], ONE + n + 1)
                            act.wait_ge(prob_used[i], ONE + n)
                            act.activation(probs[i][:, :], logit_ps[i][:, :], ACT.Exp).then_inc(exp_ready[i], 1)
                batch_loop(act, body)

            @block.gpsimd
            def _(pool):
                def body(b, j, pair, after):
                    for s in range(HALVES):
                        u = b * HALVES + s
                        pool.wait_ge(ve_ready, ONE + u + 1)
                        pool.tensor_tensor(rstd[:, :], ve[:, :], minus_half[:, :], ALU.pow).then_inc(rstd_ready, 1)
                        pool.wait_ge(hn_ready, ONE + u + 1)
                        pool.wait_ge(x1_ready[s], ONE + 16 * (b + 1))
                        pool.tensor_tensor(h[s][:, :, :], h[s][:, :, :], x1_sb[s][:, :, :], ALU.add).then_inc(out_ready[s], 1)
                batch_loop(pool, body)

            @block.vector
            def _(dve):
                def body(b, j, pair, after):
                    for s in range(HALVES):
                        u = b * HALVES + s
                        step = Steps(dve, dve_step, 5 + u * DVE_HALF, DVE_HALF)
                        dve.wait_ge(prob_used[NPROB - 1], ONE + USES * (u + 1))
                        step.done(dve.reciprocal(inverse[:, :], o_ps[:, :, E]))
                        step.wait()
                        dve.wait_ge(o_stored[s], ONE + 16 * b)
                        for i in range(NT):
                            ins = dve.tensor_scalar(h[s][:, i, :], o_ps[:, i, 0:E], inverse[:, i:i + 1], None, ALU.mult)
                        ins.then_inc(o_out, 1)
                        dve.wait_ge(o_out, ONE + u + 1)
                        dve.wait_ge(rstd_ready, ONE + u)
                        moments.of(dve, step, [h[s][:, i, :] for i in range(NT)], E).then_inc(ve_ready, 1)
                        dve.wait_ge(rstd_ready, ONE + u + 1)
                        for i in range(NT):
                            ins = dve.tensor_scalar(h[s][:, i, :], h[s][:, i, :], mean[:, i:i + 1], rstd[:, i:i + 1],
                                                    ALU.subtract, ALU.mult)
                        ins.then_inc(hn_ready, 1)
                        step.end()
                batch_loop(dve, body)

            @block.tensor
            def _(pe):
                def products(u, j, c):
                    i, n = c % NPROB, USES * u + c // NPROB
                    pe.wait_ge(exp_ready[i], ONE + n + 1)
                    if c == 0:
                        pe.wait_ge(o_out, ONE + u)
                    for t in range(NT):
                        ins = pe.matmul(o_ps[:, t, 0:W], probs[i][:, t * P:(t + 1) * P], y[j][:, c, :],
                                        start=(c == 0), stop=(c == CHUNKS - 1), skip_group_check=True)
                    ins.then_inc(prob_used[i], 1)

                def body(b, j, pair, after):
                    pe.wait_ge(y_ready[j], ONE + 16 * (pair + 1))
                    for s in range(HALVES):
                        u = b * HALVES + s
                        columns = bass.ds(b * S + s * HALF, HALF)
                        for c in range(CHUNKS):
                            i, n = c % NPROB, USES * u + c // NPROB
                            pe.wait_ge(exp_ready[i], ONE + n)
                            for e in range(ET):
                                pe.matmul(logit_ps[i][:, :], phi_sb[:, e, c * P:(c + 1) * P], xfT[:, e, columns],
                                          start=(e == 0), stop=False)
                            pe.matmul(logit_ps[i][:, :], ones[:, :], shift[:, columns], start=False, stop=True).then_inc(logit_ready[i], 1)
                            if c >= 2:
                                products(u, j, c - 2)
                        for c in range(CHUNKS - 2, CHUNKS):
                            products(u, j, c)
                batch_loop(pe, body)


def block_kernel(nc, x, w_packed, b_packed, w_out, b_out, phi, w_exp, b_exp, out):
    B, S, E = x.shape
    scratch = lambda name, shape, dt=F32: nc.dram_tensor(name, shape, dt).ap()
    parts = scratch("parts", (3, 2 * E, B * S), BF16)
    v_ones = scratch("v_ones", (B, P, S // P, 2 * E))
    att_T = scratch("att_T", (B, 2 * E, S))
    x1 = scratch("x1", (B, S, E))
    xf = scratch("xf", (B, S, E))
    inverse = scratch("inverse", (B, HEADS, S))
    y = scratch("y", (B, phi.shape[1] * phi.shape[2] // P, P, E))
    with Place(nc, "all") as place:
        ident = place.sb("ident", [P, P])
        identb = place.sb("identb", [P, P], BF16)
        with Place(nc, "mask") as m:
            mask = m.sb("mask", [P, P])
            load_constants(nc, place, ident, identb, mask)
            project_qkv(nc, x, w_packed, b_packed, ident, parts, v_ones)
            attend(nc, parts, v_ones, identb, mask, att_T)
        with Place(nc, "moe") as moe:
            xfT_sb = moe.sb("xfT", [P, E // P, B * S])
            close_attention(nc, x, att_T, w_out, b_out, ident, inverse, x1, xf, xfT_sb)
            phi_sb = moe.sb("phi", [P, E // P, phi.shape[1] * phi.shape[2]])
            row_max = moe.sb("row_max", [P, S // P, B])
            loaded = moe.sem("loaded")
            moe.start_sems()
            with nc.Block() as block:

                @block.sync
                def _(sp):
                    sp.dma_start(phi_sb[:, :, :], phi.rearrange("(t p) x s -> p t (x s)", p=P)).then_inc(loaded, 16)
                    sp.wait_ge(loaded, ONE + 16)
            res = (xfT_sb, phi_sb, row_max)
            dispatch_and_experts(nc, res, xf, phi, w_exp, b_exp, ident, y)
            combine(nc, res, y, x1, ident, identb, out)


_INS = ["L0_attn_Q", "L0_attn_W_packed", "L0_attn_b_packed", "L0_attn_W_out", "L0_attn_b_out", "L0_ffn_phi", "L0_ffn_W", "L0_ffn_b"]


def kernel(**inputs):
    import numpy as _np
    import concourse.bacc as _bacc
    from concourse.bass_utils import run_bass_kernel_spmd as _run

    nc = _bacc.Bacc("TRN2", target_bir_lowering=False, num_devices=1)
    arrays, args = {}, []
    for name in _INS:
        a = _np.ascontiguousarray(inputs[name])
        arrays[f"in_{name}_dram"] = a
        args.append(nc.dram_tensor(f"in_{name}_dram", a.shape, mybir.dt.from_np(a.dtype), kind="ExternalInput").ap())
    out = nc.dram_tensor("out_0_dram", inputs["L0_attn_Q"].shape, F32, kind="ExternalOutput").ap()
    block_kernel(nc, *args, out)
    r = _run(nc, [arrays], core_ids=[0])
    return r.results[0]["out_0_dram"]
```

```python
from contextlib import ExitStack

import concourse.bass as bass
from concourse import mybir

F32 = mybir.dt.float32
BF16 = mybir.dt.bfloat16
F32R = mybir.dt.float32r
ACT = mybir.ActivationFunctionType
ALU = mybir.AluOpType
AX = mybir.AxisListType

P = 128
HALF = 512
EPS = 1e-5
NEG = -3.0e38
HEADS, HD, QUAD = 16, 16, 4
NQUAD = HEADS // QUAD
Q_PART = (0, 0, 1, 1, 0, 2)
K_PART = (0, 1, 0, 1, 2, 0)
SCORE_ROWS = HD * len(Q_PART)
SHIFT_ROWS = 3
STAT = 6
ONE = 1


class Place:

    def __init__(self, nc, prefix):
        self.nc, self.prefix, self.stack, self.all_sems = nc, prefix, ExitStack(), []

    def __enter__(self):
        return self

    def __exit__(self, *exc):
        return self.stack.__exit__(*exc)

    def sb(self, name, shape, dt=F32):
        return self.stack.enter_context(self.nc.sbuf_tensor(f"{self.prefix}_{name}", shape, dt))

    def ps(self, name, shape, dt=F32):
        return self.stack.enter_context(self.nc.psum_tensor(f"{self.prefix}_{name}", shape, dt))

    def sem(self, name):
        s = self.stack.enter_context(self.nc.semaphore(f"{self.prefix}_{name}"))
        self.all_sems.append(s)
        return s

    def sems(self, name, n):
        return [self.sem(f"{name}{i}") for i in range(n)]

    def start_sems(self):
        with self.nc.Block() as block:

            @block.sync
            def _(sp):
                for s in self.all_sems:
                    sp.sem_inc(s, ONE)


class Steps:

    def __init__(self, eng, sem, base, per_body=None):
        self.eng, self.sem, self.base, self.n, self.per_body = eng, sem, base, 0, per_body

    def done(self, ins):
        ins.then_inc(self.sem, 1)
        self.n += 1
        return ins

    def wait(self):
        self.eng.wait_ge(self.sem, ONE + self.base + self.n)

    def end(self):
        assert self.per_body == self.n, (self.per_body, self.n)


def flat(ap):
    return ap.rearrange("p a b -> p (a b)")


def load_constants(nc, place, ident, identb, mask):
    made = place.sem("made")
    place.start_sems()
    with nc.Block() as block:

        @block.gpsimd
        def _(pool):
            pool.memset(ident[:, :], 0.0).then_inc(made, 1)
            pool.memset(mask[:, :], 0.0).then_inc(made, 1)
            pool.wait_ge(made, ONE + 2)
            pool.affine_select(out=ident[:, :], in_=ident[:, :], compare_op=ALU.not_equal, fill=1.0, base=0,
                               pattern=[[-1, P]], channel_multiplier=1).then_inc(made, 1)
            pool.affine_select(out=mask[:, :], in_=mask[:, :], compare_op=ALU.is_ge, fill=NEG, base=0,
                               pattern=[[-1, P]], channel_multiplier=1).then_inc(made, 1)
            pool.wait_ge(made, ONE + 4)
            pool.tensor_copy(identb[:, :], ident[:, :]).then_inc(made, 1)
            pool.wait_ge(made, ONE + 5)


class Moments:
    STEPS = 6

    def __init__(self, place, name, tiles):
        self.stats = place.sb(f"{name}_stats", [P, tiles, STAT])
        self.mean2, self.diff, self.dev, self.square = (place.sb(f"{name}_{n}", [P, tiles]) for n in ("mean2", "diff", "dev", "square"))
        self.mean, self.ve = place.sb(f"{name}_mean", [P, tiles]), place.sb(f"{name}_ve", [P, tiles])

    def of(self, dve, step, rows, columns):
        st = self.stats
        for i, t in enumerate(rows):
            step.done(dve.bn_stats(st[:, i, :], t))
        step.wait()
        step.done(dve.tensor_tensor(self.mean2[:, :], st[:, :, 1], st[:, :, 4], ALU.add))
        step.done(dve.tensor_tensor(self.diff[:, :], st[:, :, 1], st[:, :, 4], ALU.subtract))
        step.done(dve.tensor_tensor(self.dev[:, :], st[:, :, 2], st[:, :, 5], ALU.add))
        step.wait()
        step.done(dve.scalar_tensor_tensor(out=self.square[:, :], in0=self.diff[:, :], scalar=columns / 4, in1=self.diff[:, :],
                                           op0=ALU.mult, op1=ALU.mult))
        step.done(dve.tensor_scalar(self.mean[:, :], self.mean2[:, :], 0.5, None, ALU.mult))
        step.wait()
        step.done(dve.tensor_tensor(self.dev[:, :], self.dev[:, :], self.square[:, :], ALU.add))
        step.wait()
        return dve.tensor_scalar(self.ve[:, :], self.dev[:, :], 1.0 / columns, EPS, ALU.mult, ALU.add)


def rounds(eng, body, total, per, extra=0):
    for j in range(per):
        body(j, j, 0)
    with eng.Fori(1, total // per - 1) as i:
        for j in range(per):
            body(per * i + j, j, i)
    for j in range(per + extra):
        body(total - per + j, j, total // per - 1)


def at_least(u, n):
    return not isinstance(u, int) or u >= n


def is_unit(u, units):
    return not isinstance(u, int) or 0 <= u < units


def project_qkv(nc, x, w_packed, b_packed, ident, parts_out, v_out):
    B, S, E = x.shape
    HALVES, NT, ET = S // HALF, HALF // P, E // P
    UNITS = B * HALVES
    QKT = 2 * E // P
    NBUF = 4
    with Place(nc, "qkv") as place:
        sb, ps, sem, sems = place.sb, place.ps, place.sem, place.sems
        w = sb("w", [P, ET, 3 * E])
        b_qk = sb("b_qk", [P, QKT])
        b_v = sb("b_v", [P, E])
        minus_half = sb("minus_half", [P, NT])
        xs = [sb(f"x{j}", [P, NT, E]) for j in range(NBUF)]
        xn = [sb(f"xn{k}", [P, NT, E]) for k in range(2)]
        xnT = [sb(f"xnT{k}", [P, ET, HALF]) for k in range(2)]
        moments = [Moments(place, f"x{k}", NT) for k in range(2)]
        rstd = [sb(f"rstd{k}", [P, NT]) for k in range(2)]
        qk = [sb(f"qk{c}", [P, HALF]) for c in range(QKT)]
        rest = [sb(f"rest{c}", [P, HALF]) for c in range(QKT)]
        parts = [[sb(f"parts{k}{c}", [P, 3, HALF], BF16) for c in range(QKT)] for k in range(2)]
        v_ones = [sb(f"v_ones{k}", [P, NT, HEADS, 2 * HD]) for k in range(2)]
        turned = [ps(f"turned{t}", [P, HALF]) for t in range(ET)]
        qk_ps = [ps(f"qk_ps{c}", [P, HALF]) for c in range(QKT)]
        v_ps = [ps(f"v_ps{i}", [P, 2, E]) for i in range(2)]

        w_ready = sem("w_ready")
        const_ready = sem("const_ready")
        x_ready = sems("x_ready", NBUF)
        ve_ready, rstd_ready, xn_ready = sem("ve_ready"), sem("rstd_ready"), sem("xn_ready")
        turned_ready, xnT_ready = sem("turned_ready"), sem("xnT_ready")
        qk_ps_ready, qk_ready = sem("qk_ps_ready"), sem("qk_ready")
        part0_ready, rest_ready, part1_ready, part2_ready = (sem(f"{n}_ready") for n in ("part0", "rest", "part1", "part2"))
        parts_stored = sems("parts_stored", 2)
        v_ps_ready, v_ready = sem("v_ps_ready"), sem("v_ready")
        v_stored = sems("v_stored", 2)
        dve_step = sem("dve_step")
        STEPS = NT + Moments.STEPS
        stored_before = lambda i, j: i * (NBUF // 2) + j // 2

        place.start_sems()
        with nc.Block() as block:

            @block.sync
            def _(sp):
                def load(i, j):
                    i, j = i + j // NBUF, j % NBUF
                    sp.dma_start(xs[j][:, :, :], x[bass.ds(i * (NBUF // HALVES) + j // HALVES, 1),
                                                   j % HALVES * HALF:(j % HALVES + 1) * HALF, :].rearrange("o (t p) e -> p (o t) e", p=P)
                                 ).then_inc(x_ready[j], 16)

                load(0, 0)
                sp.dma_start(w[:, :, :], w_packed.rearrange("(t p) n -> p t n", p=P)).then_inc(w_ready, 16)
                sp.dma_start(b_qk[:, :], b_packed[0:2 * E].rearrange("(t p) -> p t", p=P),
                             allow_slow_non_contiguous=True).then_inc(w_ready, 16)
                sp.dma_start(b_v[:, :], b_packed[2 * E:3 * E].partition_broadcast(P)).then_inc(w_ready, 16)
                AHEAD = NBUF - 1
                for j in range(1, AHEAD):
                    load(0, j)

                def body(u, j, i):
                    k = j % 2
                    if is_unit(u + AHEAD, UNITS):
                        if at_least(u, 1):
                            sp.wait_ge(xn_ready, ONE + u)
                        load(i, j + AHEAD)
                    columns = u * HALF if isinstance(u, int) else sp.snap(u * HALF)
                    for c in range(QKT):
                        sp.wait_ge(part2_ready, ONE + QKT * u + c + 1)
                        sp.dma_start(parts_out[:, c * P:(c + 1) * P, bass.ds(columns, HALF)].rearrange("i p n -> p i n"),
                                     parts[k][c][:, :, :]).then_inc(parts_stored[k], 16)
                    sp.wait_ge(v_ready, ONE + 2 * u + 2)
                    sp.dma_start(v_out[bass.ds(i * (NBUF // HALVES) + j // HALVES, 1), :, j % HALVES * NT:(j % HALVES + 1) * NT, :]
                                 .rearrange("o p t n -> (o p) t n"),
                                 v_ones[k][:, :, :, :].rearrange("p t h d -> p t (h d)")).then_inc(v_stored[k], 16)
                rounds(sp, body, UNITS, NBUF)
                for k in range(2):
                    sp.wait_ge(parts_stored[k], ONE + 16 * QKT * (UNITS // 2))
                    sp.wait_ge(v_stored[k], ONE + 16 * (UNITS // 2))

            @block.gpsimd
            def _(pool):
                pool.memset(minus_half[:, :], -0.5).then_inc(const_ready, 1)
                pool.memset(v_ones[0][:, :, :, :], 1.0).then_inc(const_ready, 1)
                pool.memset(v_ones[1][:, :, :, :], 1.0).then_inc(const_ready, 1)
                pool.wait_ge(const_ready, ONE + 3)

                def root(u, k):
                    pool.wait_ge(ve_ready, ONE + u + 1)
                    pool.tensor_tensor(rstd[k][:, :], moments[k].ve[:, :], minus_half[:, :], ALU.pow).then_inc(rstd_ready, 1)
                for k in range(2):
                    root(k, k)

                def body(u, j, i):
                    k = j % 2
                    for c in range(QKT):
                        if c == 1 and (is_unit(u + 2, UNITS)):
                            root(u + 2, k)
                        pool.wait_ge(part1_ready, ONE + QKT * u + c + 1)
                        pool.tensor_tensor(parts[k][c][:, 2, :], rest[c][:, :], parts[k][c][:, 1, :], ALU.subtract).then_inc(part2_ready, 1)
                rounds(pool, body, UNITS, NBUF)

            @block.vector
            def _(dve):
                def statistics(u, j, i):
                    k, step = j % 2, Steps(dve, dve_step, STEPS * u, STEPS)
                    dve.wait_ge(x_ready[j % NBUF], ONE + 16 * (i + j // NBUF + 1))
                    if at_least(u, 2):
                        dve.wait_ge(xn_ready, ONE + u - 1)
                    moments[k].of(dve, step, [xs[j % NBUF][:, t, :] for t in range(NT)], E).then_inc(ve_ready, 1)
                    step.end()

                def normalise(u, j):
                    k = j % 2
                    dve.wait_ge(rstd_ready, ONE + u + 1)
                    if at_least(u, 2):
                        dve.wait_ge(turned_ready, ONE + u - 1)
                    for t in range(NT):
                        ins = dve.tensor_scalar(xn[k][:, t, :], xs[j % NBUF][:, t, :], moments[k].mean[:, t:t + 1], rstd[k][:, t:t + 1],
                                                ALU.subtract, ALU.mult)
                    ins.then_inc(xn_ready, 1)

                for j in range(2):
                    statistics(j, j, 0)
                    normalise(j, j)
                dve.wait_ge(w_ready, ONE + 48)
                dve.wait_ge(const_ready, ONE + 3)

                def body(u, j, i):
                    k, more = j % 2, is_unit(u + 2, UNITS)
                    if more:
                        statistics(u + 2, j + 2, i)
                    for c in range(QKT):
                        dve.wait_ge(part0_ready, ONE + QKT * u + c + 1)
                        if at_least(u, 1):
                            dve.wait_ge(part2_ready, ONE + QKT * u - QKT + c + 1)
                        dve.tensor_tensor(rest[c][:, :], qk[c][:, :], parts[k][c][:, 0, :], ALU.subtract).then_inc(rest_ready, 1)
                        dve.wait_ge(rest_ready, ONE + QKT * u + c + 1)
                        dve.tensor_copy(parts[k][c][:, 1, :], rest[c][:, :]).then_inc(part1_ready, 1)
                        if more and c == 2:
                            normalise(u + 2, j + 2)
                    if at_least(u, 2):
                        dve.wait_ge(v_stored[k], ONE + 16 * stored_before(i, j))
                    for t in range(NT):
                        if t % 2 == 0:
                            dve.wait_ge(v_ps_ready, ONE + 2 * u + t // 2 + 1)
                        ins = dve.tensor_tensor(v_ones[k][:, t, :, 0:HD],
                                                v_ps[t // 2][:, t % 2, :].rearrange("p (h d) -> p h d", d=HD),
                                                b_v[:, :].rearrange("p (h d) -> p h d", d=HD), ALU.add)
                        if t % 2:
                            ins.then_inc(v_ready, 1)
                rounds(dve, body, UNITS, NBUF)

            @block.scalar
            def _(act):
                def turned_away(u, k):
                    act.wait_ge(turned_ready, ONE + u + 1)
                    if at_least(u, 2):
                        act.wait_ge(v_ps_ready, ONE + 2 * u - 2)
                    for t in range(ET):
                        ins = act.activation(xnT[k][:, t, :], turned[t][:, :], ACT.Copy)
                    ins.then_inc(xnT_ready, 1)

                turned_away(0, 0)
                act.wait_ge(w_ready, ONE + 48)

                def body(u, j, i):
                    k = j % 2
                    for c in range(QKT):
                        act.wait_ge(qk_ps_ready, ONE + QKT * u + c + 1)
                        if at_least(u, 1):
                            act.wait_ge(rest_ready, ONE + QKT * u - QKT + c + 1)
                        act.activation(qk[c][:, :], qk_ps[c][:, :], ACT.Identity, bias=b_qk[:, c:c + 1]).then_inc(qk_ready, 1)
                        if c == 0 and at_least(u, 2):
                            act.wait_ge(parts_stored[k], ONE + 16 * QKT * stored_before(i, j))
                        act.wait_ge(qk_ready, ONE + QKT * u + c + 1)
                        act.activation(parts[k][c][:, 0, :], qk[c][:, :], ACT.Copy).then_inc(part0_ready, 1)
                    if is_unit(u + 1, UNITS):
                        turned_away(u + 1, (j + 1) % 2)
                rounds(act, body, UNITS, NBUF)

            @block.tensor
            def _(pe):
                def turn(u, k):
                    pe.wait_ge(xn_ready, ONE + u + 1)
                    if at_least(u, 1):
                        pe.wait_ge(xnT_ready, ONE + u)
                    for e in range(ET):
                        for t in range(NT):
                            ins = pe.transpose(turned[e][:, t * P:(t + 1) * P], xn[k][:, t, e * P:(e + 1) * P], ident[:, :])
                    ins.then_inc(turned_ready, 1)

                turn(0, 0)
                pe.wait_ge(w_ready, ONE + 48)

                def body(u, j, i):
                    k = j % 2
                    pe.wait_ge(xnT_ready, ONE + u + 1)
                    for c in range(QKT):
                        if at_least(u, 1):
                            pe.wait_ge(qk_ready, ONE + QKT * u - QKT + c + 1)
                        for e in range(ET):
                            ins = pe.matmul(qk_ps[c][:, :], w[:, e, c * P:(c + 1) * P], xnT[k][:, e, :],
                                            start=(e == 0), stop=(e == ET - 1))
                        ins.then_inc(qk_ps_ready, 1)
                    if is_unit(u + 1, UNITS):
                        turn(u + 1, (j + 1) % 2)
                    for t in range(NT):
                        if t % 2 == 0 and at_least(u, 1):
                            pe.wait_ge(v_ready, ONE + 2 * u - 2 + t // 2 + 1)
                        for e in range(ET):
                            ins = pe.matmul(v_ps[t // 2][:, t % 2, :], xnT[k][:, e, t * P:(t + 1) * P], w[:, e, 2 * E:3 * E],
                                            start=(e == 0), stop=(e == ET - 1))
                        if t % 2:
                            ins.then_inc(v_ps_ready, 1)
                rounds(pe, body, UNITS, NBUF)


def attend(nc, parts_in, v_in, identb, mask, out_T):
    B, _, KT, _ = v_in.shape
    S = KT * P
    HPAD = 2 * HD
    VW = QUAD * HPAD
    with Place(nc, "att") as place:
        sb, ps, sem, sems = place.sb, place.ps, place.sem, place.sems
        q_rows = [sb(f"q{g}", [P, QUAD, S], BF16) for g in range(NQUAD)]
        k_rows = [sb(f"k{g}", [P, QUAD, S], BF16) for g in range(NQUAD)]
        v_ones = [sb(f"v{g}", [P, KT, VW]) for g in range(NQUAD)]
        maskb = sb("maskb", [P, P], BF16)
        gate = sb("gate", [1, 2])
        NPROB = 4
        probs = [sb(f"probs{i}", [P, QUAD, HALF]) for i in range(NPROB)]
        o_sb = sb("o_sb", [P, 2, HALF])
        QT = S // P
        mx = sb("mx", [P, QUAD, QT])
        neg = sb("neg", [P, QUAD * QT])
        neg_rest = sb("neg_rest", [P, QUAD * QT])
        shift = sb("shift", [P, SHIFT_ROWS, QUAD * QT], BF16)
        shift_T = sb("shift_T", [SHIFT_ROWS * QUAD * QT, P], BF16)
        row_ps = [ps(f"row_ps{i}", [P, 2, HALF]) for i in range(2)]
        NCOL = 3
        col_ps = [ps(f"col_ps{i}", [P, HALF]) for i in range(NCOL)]
        o_ps = ps("o_ps", [P, HALF])

        loaded = sems("loaded", NQUAD)
        v_loaded = sems("v_loaded", NQUAD)
        shift_loaded = sems("shift_loaded", NQUAD)
        ones_ready, ones_copied, gate_open = sem("ones_ready"), sem("ones_copied"), sem("gate_open")
        row_ready, row_used = sems("row_ready", 2), sems("row_used", 2)
        col_ready, col_used = sems("col_ready", NCOL), sems("col_used", NCOL)
        probs_masked, probs_used = sems("probs_masked", NPROB), sems("probs_used", NPROB)
        o_out = sem("o_out")
        o_stored = sem("o_stored")
        shift_ready = sem("shift_ready")
        dve_step = sem("dve_step")
        DVE_QUAD = 4

        groups = [(qt, (h,)) for qt in reversed(range(HALF // P, QT)) for h in range(QUAD)]
        groups += [(qt, (h, h + 1)) for qt in reversed(range(HALF // P)) for h in range(0, QUAD, 2)]
        NG = len(groups)
        RING = NG // 2
        TURN_AT = 4
        TURNED = (slice(0, SHIFT_ROWS * QUAD * QT), 1, slice(HALF - P // 2, HALF))
        assert TURN_AT % 2 == 0 and len(groups[TURN_AT][1]) == 1 and (groups[TURN_AT][0] + 1) * P <= 2 * HALF - P // 2

        blocks = [(1, kt) for kt in range(KT)] + [(0, kt) for kt in range(KT // 2)]
        NB = len(blocks)
        COLS = NB * QUAD // NCOL
        BLKS = NB // NPROB

        def wait_exp(eng, q, k):
            n = k * QUAD + QUAD - 1
            eng.wait_ge(col_used[n % NCOL], ONE + COLS * q + n // NCOL + 1)

        PV_LAG = 3
        ORDER = [((0, k), k - PV_LAG) for k in range(PV_LAG, NB)] + [((1, k), NB - PV_LAG + k) for k in range(PV_LAG)]

        def block_columns(k):
            c, kt = blocks[k]
            first = max(0, kt * P - c * HALF)
            return c * HALF + first, first, HALF - first, kt * P >= c * HALF

        def paced_rows():
            marks, at = [], 0
            for (_, k), kv in ORDER:
                for h in range(QUAD):
                    at += block_columns(k)[2]
                    marks.append(at)
                at += QUAD * block_columns(kv)[2]
            columns = [(qt + 1) * P * len(heads) + 64 for qt, heads in groups]
            out = []
            for m in marks:
                done = sum(1 for n in range(2 * NG) if sum(columns[:n // 2]) + columns[n // 2] * (n % 2) / 2 <= sum(columns) * m / at)
                out.append(done)
            out[-1] = 2 * NG
            return out

        def masked_before(k):
            return sum(block_columns(j)[3] for j in range(k) if j % NPROB == k % NPROB)

        def gates_before(k):
            return sum(block_columns(j)[3] for j in range(k))

        GATES = gates_before(NB)
        MASKED = [masked_before(NB + i) for i in range(NPROB)]

        def chunks_of(g):
            qt, heads = groups[g]
            n = (qt + 1) * P
            if len(heads) == 2:
                return [(heads[i], i, 0, n, i == 1) for i in range(2)]
            return [(heads[0], 0, 0, HALF, False), (heads[0], 1, HALF, n - HALF, True)]

        def use(q, gi):
            return RING * q + gi // 2

        def turn_use(q):
            if isinstance(q, int) and q == B * NQUAD - 1:
                return use(q + 1, 0)
            return use(q + 1, TURN_AT)

        def quad_loop(eng, body):
            with eng.Fori(0, B - 1) as b:
                for g in range(NQUAD):
                    body(b, g, True, True)
            for g in range(NQUAD):
                body(B - 1, g, g < NQUAD - 2, g < NQUAD - 3)

        TWO_ONES = 1 + 0x3F80 / 2 ** 23

        def ones_rows(g):
            return k_rows[g][SCORE_ROWS:P, :, :].rearrange("p h n -> p (h n)").bitcast(F32)

        place.start_sems()
        with nc.Block() as block:

            @block.sync
            def _(sp):
                def load(q, g, b, used=True):
                    tokens = bass.ds(b * S if isinstance(b, int) else sp.snap(b * S), S)
                    if used:
                        sp.wait_ge(probs_used[NPROB - 1], ONE + BLKS * (q - 3))
                    for rows, parts, base in ((q_rows[g], Q_PART, 0), (k_rows[g], K_PART, HEADS * HD)):
                        for i, part in enumerate(parts):
                            src = parts_in[part, base + g * QUAD * HD:base + (g + 1) * QUAD * HD, tokens]
                            sp.dma_start(rows[i * HD:(i + 1) * HD, :, :],
                                         src.rearrange("(h r) n -> r h n", r=HD)).then_inc(loaded[g], 16)
                    sp.dma_start(v_ones[g][:, :, :],
                                 v_in[bass.ds(b, 1), :, :, g * VW:(g + 1) * VW].rearrange("o p t n -> (o p) t n")
                                 ).then_inc(v_loaded[g], 16)

                def load_shift(q, g):
                    sp.wait_ge(row_used[0], ONE + turn_use(q) + 1)
                    sp.dma_start(q_rows[g][SCORE_ROWS:SCORE_ROWS + SHIFT_ROWS, :, :],
                                 shift_T[:, :]).then_inc(shift_loaded[g], 16)

                def store(q, g, b):
                    sp.wait_ge(o_out, ONE + 2 * q + 2)
                    sp.dma_start(out_T.rearrange("b r n -> (b r) n")[bass.ds(q * P, P), :], flat(o_sb[:, :, :])
                                 ).then_inc(o_stored, 16)

                for g in range(3):
                    load(g, g, 0, used=False)
                load_shift(0, 0)

                def body(b, g, two, three):
                    q = b * NQUAD + g
                    if three:
                        load(q + 3, (g + 3) % NQUAD, b + (g + 3) // NQUAD)
                    if not (isinstance(b, int) and g == NQUAD - 1):
                        load_shift(q + 1, (g + 1) % NQUAD)
                    store(q, g, b)
                quad_loop(sp, body)
                sp.wait_ge(o_stored, ONE + 16 * B * NQUAD)

            @block.gpsimd
            def _(pool):
                pool.tensor_copy(maskb[:, :], mask[:, :]).then_inc(ones_ready, 1)
                pool.memset(gate[:, :], 0.0).then_inc(gate_open, 1)
                pool.wait_ge(gate_open, ONE + 1)

                def body(b, g, two, three):
                    q = b * NQUAD + g
                    for k in range(NB):
                        _, first, width, diagonal = block_columns(k)
                        i = k % NPROB
                        if diagonal:
                            pool.wait_ge(gate_open, ONE + 1 + GATES * q + gates_before(k))
                            wait_exp(pool, q, k)
                            pool.tensor_tensor(gate[:, 1:2], gate[:, 0:1], gate[:, 0:1], ALU.add).then_inc(gate_open, 1)
                            pool.affine_select(out=probs[i][:, :, 0:P], in_=probs[i][:, :, 0:P], compare_op=ALU.is_ge, fill=0.0,
                                               base=0, pattern=[[0, QUAD], [1, P]], channel_multiplier=-1).then_inc(probs_masked[i], 1)
                quad_loop(pool, body)

            @block.scalar
            def _(act):
                def exponentials(q, k):
                    _, first, width, diagonal = block_columns(k)
                    i = k % NPROB
                    act.wait_ge(probs_used[i], ONE + BLKS * q + k // NPROB)
                    for h in range(QUAD):
                        n = k * QUAD + h
                        slot = n % NCOL
                        act.wait_ge(col_ready[slot], ONE + COLS * q + n // NCOL + 1)
                        ins = act.activation(probs[i][:, h, 0:width], col_ps[slot][:, 0:width], ACT.Exp, scale=float(HD) ** -0.5)
                        ins.then_inc(col_used[slot], 1)

                def evacuate(q, n):
                    k = (KT, NB)[n] - 1
                    act.wait_ge(probs_used[k % NPROB], ONE + BLKS * q + k // NPROB + 1)
                    act.wait_ge(o_stored, ONE + 16 * q)
                    act.activation(o_sb[:, 1 - n, :], o_ps[:, :], ACT.Copy).then_inc(o_out, 1)

                act.wait_ge(ones_ready, ONE + 2)
                for g in range(1, NQUAD):
                    act.activation(ones_rows(g), ones_rows(0), ACT.Copy).then_inc(ones_copied, 1)
                for k in range(PV_LAG):
                    exponentials(0, k)

                def body(b, g, two, three):
                    q = b * NQUAD + g
                    for (ahead, k), kv in ORDER:
                        if not ahead or two or g == NQUAD - 2:
                            exponentials(q + ahead, k)
                        if kv == KT - 1:
                            evacuate(q, 0)
                    evacuate(q, 1)
                quad_loop(act, body)

            @block.vector
            def _(dve):
                def reduce_group(q, gi, before):
                    qt, heads = groups[gi]
                    n = (qt + 1) * P
                    slot = gi % 2
                    dve.wait_ge(row_ready[slot], ONE + use(q, gi) + 1)
                    if len(heads) == 2:
                        src, dst = row_ps[slot][:, :, 0:n], mx[:, heads[0]:heads[0] + 2, qt]
                    else:
                        src, dst = flat(row_ps[slot][:, :, :])[:, 0:n], mx[:, heads[0], qt:qt + 1]
                    ins = dve.tensor_reduce(dst, src, AX.X, ALU.max)
                    if before is not None and gi == TURN_AT:
                        ins = turn_shift(before)
                    ins.then_inc(row_used[slot], 1)

                def turn_shift(before):
                    g, b = before
                    dve.wait_ge(shift_loaded[g], ONE + 16 * b)
                    return dve.tensor_copy(shift_T[:, :], row_ps[0][TURNED].bitcast(BF16))

                def split_maxima(q):
                    dve.wait_ge(row_used[0], ONE + use(q, NG - 2) + 1)
                    dve.wait_ge(row_used[1], ONE + use(q, NG - 1) + 1)
                    step = Steps(dve, dve_step, q * DVE_QUAD, DVE_QUAD)
                    mxf = flat(mx[:, :, :])
                    step.done(dve.tensor_scalar(shift[:, 0, :], mxf, -1.0, None, ALU.mult))
                    step.done(dve.tensor_scalar(neg[:, :], mxf, -1.0, None, ALU.mult))
                    step.wait()
                    step.done(dve.tensor_tensor(neg_rest[:, :], neg[:, :], shift[:, 0, :], ALU.subtract))
                    step.wait()
                    step.done(dve.tensor_copy(shift[:, 1, :], neg_rest[:, :]))
                    step.wait()
                    step.end()
                    dve.tensor_tensor(shift[:, 2, :], neg_rest[:, :], shift[:, 1, :], ALU.subtract).then_inc(shift_ready, 1)

                dve.memset(ones_rows(0), TWO_ONES).then_inc(ones_ready, 1)
                for gi in range(NG):
                    reduce_group(0, gi, None)
                split_maxima(0)
                for gi in range(NG):
                    reduce_group(1, gi, (0, 0))
                split_maxima(1)

                def body(b, g, two, three):
                    q = b * NQUAD + g
                    before = (g, b + 1)
                    if two:
                        for gi in range(NG):
                            reduce_group(q + 2, gi, before)
                        split_maxima(q + 2)
                    elif g == NQUAD - 2:
                        dve.wait_ge(row_ready[0], ONE + turn_use(q + 1) + 1)
                        turn_shift(before).then_inc(row_used[0], 1)
                quad_loop(dve, body)

            @block.tensor
            def _(pe):
                def row_chunk(q, g, n):
                    gi, part = n // 2, n % 2
                    qt, heads = groups[gi]
                    slot = gi % 2
                    h, bank, k0, width, last = chunks_of(gi)[part]
                    if part == 0:
                        pe.wait_ge(row_used[slot], ONE + use(q, gi))
                    dst = row_ps[slot][:, bank, 0:width]
                    diagonal = k0 + width == (qt + 1) * P
                    ins = pe.matmul(dst, q_rows[g][0:SCORE_ROWS, h, qt * P:(qt + 1) * P], k_rows[g][0:SCORE_ROWS, h, k0:k0 + width],
                                    start=True, stop=True)
                    if diagonal:
                        ins = pe.matmul(row_ps[slot][:, bank, width - P:width], identb[:, :], maskb[:, :],
                                        start=False, stop=True, skip_group_check=True)
                    if part == 1:
                        if gi == TURN_AT and not (isinstance(q, int) and q == 0):
                            ins = turn(q - 1)
                        ins.then_inc(row_ready[slot], 1)

                def turn(q):
                    pe.wait_ge(shift_ready, ONE + q + 1)
                    return pe.transpose(row_ps[0][TURNED].bitcast(BF16), shift[:, :, :].rearrange("p a b -> p (a b)"), identb[:, :])

                def rows_until(q, g, done, until):
                    for n in range(done, until):
                        row_chunk(q, g, n)

                def scores(q, g, k, h):
                    q0, _, width, _ = block_columns(k)
                    kt, n = blocks[k][1], k * QUAD + h
                    slot = n % NCOL
                    pe.wait_ge(col_used[slot], ONE + COLS * q + n // NCOL)
                    pe.matmul(col_ps[slot][:, 0:width], k_rows[g][0:SCORE_ROWS + SHIFT_ROWS, h, kt * P:(kt + 1) * P],
                              q_rows[g][0:SCORE_ROWS + SHIFT_ROWS, h, q0:q0 + width], start=True, stop=True
                              ).then_inc(col_ready[slot], 1)

                def pv(q, g, b, k):
                    c, kt = blocks[k]
                    _, first, width, diagonal = block_columns(k)
                    i = k % NPROB
                    if k == 0:
                        pe.wait_ge(v_loaded[g], ONE + 16 * b + 16)
                    if kt == 0:
                        pe.wait_ge(o_out, ONE + 2 * q + (1 - c))
                    if diagonal:
                        pe.wait_ge(probs_masked[i], ONE + MASKED[i] * q + masked_before(k) + 1)
                    else:
                        wait_exp(pe, q, k)
                    last = kt == (KT - 1 if c else KT // 2 - 1)
                    for h in range(QUAD):
                        ins = pe.matmul(o_ps[h * HPAD:(h + 1) * HPAD, first:HALF], v_ones[g][:, kt, h * HPAD:(h + 1) * HPAD],
                                        probs[i][:, h, 0:width], start=(kt == 0), stop=last, skip_group_check=True)
                    ins.then_inc(probs_used[i], 1)

                def body(b, g, two, three):
                    q = b * NQUAD + g
                    g2, b2 = (g + 2) % NQUAD, b + (g + 2) // NQUAD
                    if two:
                        pe.wait_ge(loaded[g2], ONE + 16 * 12 * (b2 + 1))
                    done = 0
                    for n, ((ahead, k), kv) in enumerate(ORDER):
                        if not two and g == NQUAD - 2 and n == 0:
                            pe.wait_ge(row_used[0], ONE + turn_use(q + 1))
                            turn(q + 1).then_inc(row_ready[0], 1)
                        for h in range(QUAD):
                            if not ahead:
                                scores(q, g, k, h)
                            elif two or g == NQUAD - 2:
                                if k == 0 and h == 0:
                                    pe.wait_ge(shift_loaded[(g + 1) % NQUAD], ONE + 16 * (b + (g + 1) // NQUAD + 1))
                                scores(q + 1, (g + 1) % NQUAD, k, h)
                            if two:
                                rows_until(q + 2, g2, done, PACE[n * QUAD + h])
                                done = PACE[n * QUAD + h]
                        pv(q, g, b, kv)
                    assert not two or done == 2 * NG

                PACE = paced_rows()
                pe.wait_ge(ones_ready, ONE + 2)
                for g in range(2):
                    pe.wait_ge(loaded[g], ONE + 16 * 12)
                    rows_until(g, g, 0, 2 * NG)
                pe.wait_ge(shift_loaded[0], ONE + 16)
                pe.wait_ge(ones_copied, ONE + NQUAD - 1)
                for k in range(PV_LAG):
                    for h in range(QUAD):
                        scores(0, 0, k, h)
                quad_loop(pe, body)


def close_attention(nc, x, att_T, w_out, b_out, ident, inverse_out, x1_out, xf_out, xfT, phi, phi_sb):
    B, S, E = x.shape
    HALVES, NT, ET = S // HALF, HALF // P, E // P
    UNITS = B * HALVES
    TB = E // HD // ET
    with Place(nc, "close") as place:
        sb, ps, sem, sems = place.sb, place.ps, place.sem, place.sems
        NBUF = 4
        w = sb("w", [P, ET, E])
        bo = sb("bo", [1, E])
        ones = sb("ones", [1, P])
        minus_half = sb("minus_half", [P, NT])
        num = [sb(f"num{j}", [P, ET, HALF]) for j in range(NBUF)]
        inv = [sb(f"inv{j}", [P, ET, HALF]) for j in range(NBUF)]
        xs = [sb(f"x{j}", [P, NT, E]) for j in range(NBUF)]
        x1 = [sb(f"x1{j}", [P, NT, E]) for j in range(NBUF)]
        xf = [sb(f"xf{j}", [P, NT, E]) for j in range(2)]
        moments = [[Moments(place, f"m{i}{k}", NT) for k in range(2)] for i in range(2)]
        rstd = [[sb(f"rstd{i}{k}", [P, NT]) for k in range(2)] for i in range(2)]
        h_ps = [ps(f"h_ps{k}", [P, NT, E]) for k in range(2)]
        turned = [ps(f"turned{t}", [P, HALF]) for t in range(ET)]

        w_ready, const_ready = sem("w_ready"), sem("const_ready")
        den_ready, inverse_made, inverse_ready = sem("den_ready"), sem("inverse_made"), sem("inverse_ready")
        in_ready, x_ready = sems("in_ready", NBUF), sems("x_ready", NBUF)
        att_ready = sem("att_ready")
        h_ready = sem("h_ready")
        ve_ready, rstd_ready = sems("ve_ready", 2), sems("rstd_ready", 2)
        hn_ready, x1_ready, xf_ready = sem("hn_ready"), sem("x1_ready"), sem("xf_ready")
        turned_ready, xfT_ready = sem("turned_ready"), sem("xfT_ready")
        x1_stored, xf_stored = sems("x1_stored", NBUF), sems("xf_stored", 2)
        dve_step = sem("dve_step")
        STEPS = NT + Moments.STEPS

        place.start_sems()
        with nc.Block() as block:

            @block.sync
            def _(sp):
                den_rows = att_T.rearrange("b (h r) n -> (b h) r n", r=2 * HD)[:, HD, :]
                sp.dma_start(flat(num[0][:, :, :]), den_rows).then_inc(den_ready, 16)
                sp.dma_start(w[:, :, :], w_out.rearrange("(t p) n -> p t n", p=P)).then_inc(w_ready, 16)
                sp.dma_start(bo[:, :], b_out.unsqueeze(0)).then_inc(w_ready, 16)
                sp.dma_start(phi_sb[:, :, :], phi.rearrange("(t p) x s -> p t (x s)", p=P)).then_inc(w_ready, 16)
                sp.wait_ge(inverse_made, ONE + 1)
                sp.dma_start(inverse_out.rearrange("b h n -> (b h) n"), flat(inv[0][:, :, :])).then_inc(inverse_ready, 16)
                sp.wait_ge(inverse_ready, ONE + 16)
                sp.wait_ge(w_ready, ONE + 48)

            @block.vector
            def _(dve):
                dve.wait_ge(den_ready, ONE + 16)
                dve.reciprocal(inv[0][:, :, :], num[0][:, :, :]).then_inc(inverse_made, 1)

            @block.gpsimd
            def _(pool):
                pool.memset(minus_half[:, :], -0.5).then_inc(const_ready, 1)
                pool.memset(ones[:, :], 1.0).then_inc(const_ready, 1)
                pool.wait_ge(const_ready, ONE + 2)

        with nc.Block() as block:

            @block.sync
            def _(sp):
                def place_of(i, j):
                    b, j = (i + j // NBUF) * (NBUF // HALVES) + j % NBUF // HALVES, j % NBUF
                    return bass.ds(b if isinstance(b, int) else sp.snap(b), 1), slice(j % HALVES * HALF, (j % HALVES + 1) * HALF)

                def tokens_of(a, rows):
                    return a.rearrange("b n e -> (b n) e")[rows, :].rearrange("(t p) e -> p t e", p=P)

                def tokens(a, b, n):
                    return a[b, n, :].rearrange("o (t p) e -> p (o t) e", p=P)

                def load(i, j, again):
                    b, n = place_of(i, j)
                    k, r = j % NBUF, i + j // NBUF
                    rows = att_T[b, :, n].rearrange("o (t h r) n -> (o t) h r n", t=ET, r=2 * HD)
                    inverses = inverse_out[b, :, n].rearrange("o (t h) n -> (o t) h n", t=ET)
                    if again:
                        sp.wait_ge(h_ready, ONE + NBUF * r + k - NBUF + 1)
                    for t in range(ET):
                        sp.dma_start(num[k][:, t, :], rows[t, :, 0:HD, :]).then_inc(in_ready[k], 16)
                        sp.dma_start(inv[k][:, t, :], inverses[t].unsqueeze(1).to_broadcast([TB, HD, HALF])).then_inc(in_ready[k], 16)
                    if again:
                        sp.wait_ge(x1_ready, ONE + NBUF * r + k - NBUF + 1)
                    sp.dma_start(xs[k][:, :, :], tokens(x, b, n)).then_inc(x_ready[k], 16)

                AHEAD = NBUF - 1
                for j in range(AHEAD):
                    load(0, j, False)

                def body(u, j, i):
                    if is_unit(u + AHEAD, UNITS):
                        load(i, j + AHEAD, at_least(u, NBUF - AHEAD))
                    if is_unit(u - 1, UNITS):
                        first = (u - 1) * HALF
                        rows = bass.ds(first if isinstance(u, int) else sp.snap(first), HALF)
                        sp.wait_ge(xf_ready, ONE + u)
                        sp.dma_start(tokens_of(x1_out, rows), x1[(j - 1) % NBUF][:, :, :]).then_inc(x1_stored[(j - 1) % NBUF], 16)
                        sp.dma_start(tokens_of(xf_out, rows), xf[(j - 1) % 2][:, :, :]).then_inc(xf_stored[(j - 1) % 2], 16)

                rounds(sp, body, UNITS, NBUF, extra=1)
                for j in range(NBUF):
                    sp.wait_ge(x1_stored[j], ONE + 16 * (UNITS // NBUF))
                for j in range(2):
                    sp.wait_ge(xf_stored[j], ONE + 16 * (UNITS // 2))

            @block.gpsimd
            def _(pool):
                def divide(u, j, i):
                    k = j % NBUF
                    pool.wait_ge(in_ready[k], ONE + 64 * (i + j // NBUF + 1))
                    pool.tensor_tensor(num[k][:, :, :], num[k][:, :, :], inv[k][:, :, :], ALU.mult).then_inc(att_ready, 1)

                for j in range(2):
                    divide(j, j, 0)

                def body(u, j, i):
                    if is_unit(u, UNITS):
                        pool.wait_ge(ve_ready[0], ONE + u + 1)
                        pool.tensor_tensor(rstd[0][j % 2][:, :], moments[0][j % 2].ve[:, :], minus_half[:, :], ALU.pow).then_inc(rstd_ready[0], 1)
                    if is_unit(u - 1, UNITS):
                        k = (j - 1) % 2
                        pool.wait_ge(ve_ready[1], ONE + u)
                        pool.tensor_tensor(rstd[1][k][:, :], moments[1][k].ve[:, :], minus_half[:, :], ALU.pow).then_inc(rstd_ready[1], 1)
                    if is_unit(u, UNITS):
                        pool.wait_ge(hn_ready, ONE + u + 1)
                        pool.wait_ge(x_ready[j], ONE + 16 * (i + 1))
                        pool.tensor_tensor(x1[j][:, :, :], x1[j][:, :, :], xs[j][:, :, :], ALU.add).then_inc(x1_ready, 1)
                    if is_unit(u + 2, UNITS):
                        divide(u + 2, j + 2, i)
                rounds(pool, body, UNITS, NBUF, extra=1)

            @block.vector
            def _(dve):
                def body(u, j, i):
                    now, before = is_unit(u, UNITS), is_unit(u - 1, UNITS)
                    at = 0 if isinstance(u, int) and u == 0 else 2 * STEPS * u - STEPS
                    step = Steps(dve, dve_step, at, STEPS * (now + before))
                    k, kb = j % 2, (j - 1) % 2
                    if now:
                        dve.wait_ge(h_ready, ONE + u + 1)
                        moments[0][k].of(dve, step, [h_ps[k][:, t, :] for t in range(NT)], E).then_inc(ve_ready[0], 1)
                    if before:
                        dve.wait_ge(x1_ready, ONE + u)
                        moments[1][kb].of(dve, step, [x1[(j - 1) % NBUF][:, t, :] for t in range(NT)], E).then_inc(ve_ready[1], 1)
                    if now:
                        dve.wait_ge(rstd_ready[0], ONE + u + 1)
                        if at_least(u, NBUF):
                            dve.wait_ge(x1_stored[j], ONE + 16 * i)
                        for t in range(NT):
                            ins = dve.tensor_scalar(x1[j][:, t, :], h_ps[k][:, t, :], moments[0][k].mean[:, t:t + 1],
                                                    rstd[0][k][:, t:t + 1], ALU.subtract, ALU.mult)
                        ins.then_inc(hn_ready, 1)
                    if before:
                        dve.wait_ge(rstd_ready[1], ONE + u)
                        if at_least(u, 3):
                            dve.wait_ge(xf_stored[kb], ONE + 16 * (i * (NBUF // 2) + (j - 1 - kb) // 2))
                            dve.wait_ge(turned_ready, ONE + u - 2)
                        for t in range(NT):
                            ins = dve.tensor_scalar(xf[kb][:, t, :], x1[(j - 1) % NBUF][:, t, :], moments[1][kb].mean[:, t:t + 1],
                                                    rstd[1][kb][:, t:t + 1], ALU.subtract, ALU.mult)
                        ins.then_inc(xf_ready, 1)
                    step.end()
                rounds(dve, body, UNITS, NBUF, extra=1)

            @block.scalar
            def _(act):
                with act.Fori(0, UNITS) as u:
                    act.wait_ge(turned_ready, ONE + u + 1)
                    for t in range(ET):
                        ins = act.activation(xfT[:, t, bass.ds(u * HALF, HALF)], turned[t][:, :], ACT.Copy)
                    ins.then_inc(xfT_ready, 1)

            @block.tensor
            def _(pe):
                def project(u, j):
                    k = j % 2
                    pe.wait_ge(att_ready, ONE + u + 1)
                    if at_least(u, 2):
                        pe.wait_ge(hn_ready, ONE + u - 1)
                    for t in range(NT):
                        pe.matmul(h_ps[k][:, t, :], ones[:, :], bo[:, :], start=(t % 2 == 0), stop=False, skip_group_check=True)
                        for e in range(ET):
                            ins = pe.matmul(h_ps[k][:, t, :], num[j % NBUF][:, e, t * P:(t + 1) * P], w[:, e, :],
                                            start=False, stop=(e == ET - 1), skip_group_check=True)
                    ins.then_inc(h_ready, 1)

                project(0, 0)

                def body(u, j, i):
                    if is_unit(u + 1, UNITS):
                        project(u + 1, j + 1)
                    if is_unit(u - 1, UNITS):
                        pe.wait_ge(xf_ready, ONE + u)
                        if at_least(u, 2):
                            pe.wait_ge(xfT_ready, ONE + u - 1)
                        for e in range(ET):
                            for t in range(NT):
                                ins = pe.transpose(turned[e][:, t * P:(t + 1) * P], xf[(j - 1) % 2][:, t, e * P:(e + 1) * P], ident[:, :])
                        ins.then_inc(turned_ready, 1)
                rounds(pe, body, UNITS, NBUF, extra=1)


def dispatch_and_experts(nc, res, xf_in, phi, w_exp, b_exp, ident, y_out):
    B, S, E = xf_in.shape
    _, NEXP, SLOTS = phi.shape
    ET, MT = E // P, S // P
    CHUNKS = NEXP * SLOTS // P
    PER = P // SLOTS
    xfT, phi_sb, row_max = res
    with Place(nc, "disp") as place:
        sb, ps, sem, sems = place.sb, place.ps, place.sem, place.sems
        NPROB = 4
        xf = sb("xf", [P, B * MT, E])
        probs = [sb(f"probs{i}", [P, B, P]) for i in range(NPROB)]
        batch_max = sb("batch_max", [P, P])
        total = sb("total", [P, P])
        inverse = [sb(f"inverse{i}", [P, P]) for i in range(2)]
        step_max = sb("step_max", [P, B])
        slots_sb = sb("slots_sb", [P, B, E])
        slots_T = sb("slots_T", [P, ET, B, P])
        w_sb = sb("w_sb", [P, PER, ET, E])
        bias = sb("bias", [P, E])
        y_sb = sb("y_sb", [P, B, E])
        ring = [ps(f"ring{i}", [P, B, P]) for i in range(2)]
        slots_ps = ps("slots_ps", [P, B, E])

        xf_ready, w_ready = sems("xf_ready", MT), sem("w_ready")
        ring_ready, ring_used = sems("ring_ready", 2), sems("ring_used", 2)
        shifted = sem("shifted")
        exp_ready, probs_ready = sem("exp_ready"), sem("probs_ready")
        inverse_ready = sem("inverse_ready")
        slots_ready = sem("slots_ready")
        slots_out = sem("slots_out")
        y_stored = sem("y_stored")
        dve_step = sem("dve_step")
        USES = ([("L", 0), ("L", 2), ("T", 0), ("L", 3), ("L", 4), ("L", 6)],
                [("L", 1), ("T", 1), ("Y", 1), ("Y", 0), ("L", 5), ("L", 7)])

        def use(c, what, i):
            slot = next(r for r in range(2) if (what, i) in USES[r])
            seen, at = USES[slot], c if what == "L" else c + 1
            logits_only = [x for x in seen if x[0] == "L"]
            if isinstance(at, int) and at == 0:
                return slot, logits_only.index((what, i))
            if isinstance(at, int) and at == CHUNKS:
                seen = [x for x in seen if x[0] != "L"]
            return slot, (at - 1) * len(USES[slot]) + len(logits_only) + seen.index((what, i))

        def chunk_loop(eng, body, last):
            body(0, False)
            with eng.Fori(1, CHUNKS) as c:
                body(c, True)
            last()

        place.start_sems()
        with nc.Block() as block:

            @block.sync
            def _(sp):
                def load_experts(c):
                    sp.dma_start(w_sb[:, :, :, :].rearrange("p x t e -> p (x t) e"),
                                 w_exp[bass.ds(c * PER, PER), :, :].rearrange("x (t p) e -> p (x t) e", p=P)).then_inc(w_ready, 16)
                    for x in range(PER):
                        sp.dma_start(bias[x * SLOTS:(x + 1) * SLOTS, :],
                                     b_exp[bass.ds(c * PER + x, 1), :].to_broadcast([SLOTS, E])).then_inc(w_ready, 16)

                def store(c):
                    slot, n = use(c, "Y", 0)
                    sp.wait_ge(ring_used[slot], ONE + n + 1)
                    sp.dma_start(y_out[:, bass.ds(c, 1), :, :].rearrange("b o p e -> p (b o) e"), y_sb[:, :, :]).then_inc(y_stored, 16)

                def body(c, before):
                    if before:
                        store(c - 1)
                        load_experts(c)
                    else:
                        load_experts(c)
                for t in range(MT):
                    sp.dma_start(xf[:, :, :].rearrange("p (b m) e -> p b m e", m=MT)[:, :, t, :],
                                 xf_in.rearrange("b (m p) e -> p b m e", p=P)[:, :, t, :]).then_inc(xf_ready[t], 16)
                chunk_loop(sp, body, lambda: store(CHUNKS - 1))
                sp.wait_ge(y_stored, ONE + 16 * CHUNKS)

            @block.vector
            def _(dve):
                PER_CHUNK = 3 * MT
                buf = lambda t: probs[t % NPROB][:, :, :]

                def logits(c, t, step):
                    slot, uses = use(c, "L", t)
                    dve.wait_ge(ring_ready[slot], ONE + uses + 1)
                    step.wait()
                    step.done(dve.tensor_reduce(batch_max[:, :], ring[slot][:, :, :].rearrange("p b n -> p n b"), AX.X, ALU.max))
                    n = MT * c + t
                    if not (isinstance(c, int) and c == 0 and t < NPROB):
                        dve.wait_ge(slots_ready, ONE + n - NPROB + 1)
                    step.wait()
                    dve.tensor_tensor(buf(t), ring[slot][:, :, :], batch_max[:, :].unsqueeze(1).to_broadcast([P, B, P]),
                                      ALU.subtract).then_inc(shifted, 1)
                    dve.tensor_reduce(step_max[:, :], ring[slot][:, :, :], AX.X, ALU.max).then_inc(ring_used[slot], 1)
                    dve.wait_ge(ring_used[slot], ONE + uses + 1)
                    step.done(dve.tensor_tensor(row_max[:, t, :], row_max[:, t, :], step_max[:, :], ALU.max))

                def sums(c, t, step):
                    n = MT * c + t
                    dve.wait_ge(exp_ready, ONE + n + 1)
                    dve.wait_ge(inverse_ready, ONE + n)
                    step.done(dve.tensor_reduce(total[:, :], buf(t).rearrange("p b n -> p n b"), AX.X, ALU.add))
                    if not (isinstance(c, int) and c == 0 and t < 2):
                        dve.wait_ge(probs_ready, ONE + n - 1)
                    step.wait()
                    dve.reciprocal(inverse[t % 2][:, :], total[:, :]).then_inc(inverse_ready, 1)

                def add_bias(c, j):
                    dve.wait_ge(w_ready, ONE + 16 * (1 + PER) * (c + 1))
                    dve.wait_ge(y_stored, ONE + 16 * c)
                    slot, n = use(c, "Y", j)
                    dve.wait_ge(ring_ready[slot], ONE + n + 1)
                    out = y_sb[:, j * B // 2:(j + 1) * B // 2, :]
                    dve.tensor_tensor(out, ring[slot][:, :, :].rearrange("p b n -> p (b n)").rearrange("p (b e) -> p b e", e=E),
                                      bias[:, :].unsqueeze(1).to_broadcast([P, B // 2, E]), ALU.add).then_inc(ring_used[slot], 1)

                def body(c, before):
                    step = Steps(dve, dve_step, 1 + c * PER_CHUNK, PER_CHUNK)
                    for t in range(MT):
                        if before and t == 3:
                            add_bias(c - 1, 1)
                        logits(c, t, step)
                        sums(c, t, step)
                        if before and t == 3:
                            add_bias(c - 1, 0)
                    step.end()
                dve.memset(row_max[:, :, :], NEG).then_inc(dve_step, 1)

                def last():
                    for j in (1, 0):
                        add_bias(CHUNKS - 1, j)
                chunk_loop(dve, body, last)

            @block.scalar
            def _(act):
                def slots_away(c):
                    act.wait_ge(slots_ready, ONE + MT * c + MT)
                    act.activation(slots_sb[:, :, :], slots_ps[:, :, :], ACT.Copy).then_inc(slots_out, 1)

                def turned(c):
                    for j in (1, 0):
                        slot, n = use(c, "T", j)
                        act.wait_ge(ring_ready[slot], ONE + n + 1)
                        act.activation(slots_T[:, :, j * B // 2:(j + 1) * B // 2, :].rearrange("p t b n -> p t (b n)"),
                                       ring[slot][:, :, :].rearrange("p (t b) n -> p t (b n)", t=ET), ACT.Copy).then_inc(ring_used[slot], 1)

                def body(c, before):
                    for t in range(MT):
                        act.wait_ge(shifted, ONE + MT * c + t + 1)
                        act.activation(probs[t % NPROB][:, :, :], probs[t % NPROB][:, :, :], ACT.Exp).then_inc(exp_ready, 1)
                        if before and t == 1:
                            slots_away(c - 1)
                        if before and t == 2:
                            turned(c - 1)

                def last():
                    slots_away(CHUNKS - 1)
                    turned(CHUNKS - 1)
                chunk_loop(act, body, last)

            @block.gpsimd
            def _(pool):
                def body(c, before):
                    for t in range(MT):
                        n = MT * c + t
                        pool.wait_ge(inverse_ready, ONE + n + 1)
                        pool.tensor_tensor(probs[t % NPROB][:, :, :], probs[t % NPROB][:, :, :],
                                           inverse[t % 2][:, :].unsqueeze(1).to_broadcast([P, B, P]), ALU.mult).then_inc(probs_ready, 1)
                body(0, False)
                with pool.Fori(1, CHUNKS) as c:
                    body(c, True)

            @block.tensor
            def _(pe):
                def logits(c, t):
                    slot, n = use(c, "L", t)
                    pe.wait_ge(ring_used[slot], ONE + n)
                    for b in range(B):
                        for e in range(ET):
                            ins = pe.matmul(ring[slot][:, b, :], xfT[:, e, b * S + t * P:b * S + (t + 1) * P],
                                            phi_sb[:, e, bass.ds(c * P, P)], start=(e == 0), stop=(e == ET - 1), skip_group_check=True)
                    ins.then_inc(ring_ready[slot], 1)

                def slots(c, t):
                    n = MT * c + t
                    pe.wait_ge(probs_ready, ONE + n + 1)
                    pe.wait_ge(xf_ready[t], ONE + 16)
                    if t == 0:
                        pe.wait_ge(slots_out, ONE + c)
                    for b in range(B):
                        ins = pe.matmul(slots_ps[:, b, :], probs[t % NPROB][:, b, :], xf[:, b * MT + t, :],
                                        start=(t == 0 and b % 2 == 0), stop=(t == MT - 1), skip_group_check=True)
                    ins.then_inc(slots_ready, 1)

                def turn_slots(c):
                    pe.wait_ge(slots_out, ONE + c + 1)
                    for j in (1, 0):
                        slot, n = use(c, "T", j)
                        pe.wait_ge(ring_used[slot], ONE + n)
                        for e in range(ET):
                            for b in range(B // 2):
                                ins = pe.transpose(ring[slot][:, e * B // 2 + b, :], slots_sb[:, j * B // 2 + b, e * P:(e + 1) * P], ident[:, :])
                        ins.then_inc(ring_ready[slot], 1)

                def experts(c, j):
                    pe.wait_ge(w_ready, ONE + 16 * (1 + PER) * (c + 1))
                    slot, n = use(c, "T", j)
                    pe.wait_ge(ring_used[slot], ONE + n + 1)
                    slot, n = use(c, "Y", j)
                    pe.wait_ge(ring_used[slot], ONE + n)
                    y_ps = ring[slot][:, :, :].rearrange("p b n -> p (b n)").rearrange("p (b e) -> p b e", e=E)
                    for b in range(B // 2):
                        for e in range(ET):
                            for x in range(PER):
                                ins = pe.matmul(y_ps[x * SLOTS:(x + 1) * SLOTS, b, :],
                                                slots_T[:, e, j * B // 2 + b, x * SLOTS:(x + 1) * SLOTS], w_sb[:, x, e, :],
                                                start=(e == 0 and b % 2 == 0), stop=(e == ET - 1), skip_group_check=True)
                    ins.then_inc(ring_ready[slot], 1)

                def body(c, before):
                    logits(c, 0)
                    if before:
                        slots(c - 1, MT - 2)
                    logits(c, 1)
                    if before:
                        slots(c - 1, MT - 1)
                    logits(c, 2)
                    slots(c, 0)
                    if before:
                        turn_slots(c - 1)
                    slots(c, 1)
                    if before:
                        experts(c - 1, 1)
                    logits(c, 3)
                    if before:
                        experts(c - 1, 0)
                    for t in range(4, MT):
                        logits(c, t)
                        slots(c, t - 2)

                def last():
                    slots(CHUNKS - 1, MT - 2)
                    slots(CHUNKS - 1, MT - 1)
                    turn_slots(CHUNKS - 1)
                    for j in (1, 0):
                        experts(CHUNKS - 1, j)
                chunk_loop(pe, body, last)


def combine(nc, xfT, row_max, phi, y_in, x1, identb, out):
    B, CHUNKS, _, E = y_in.shape
    S = x1.shape[1]
    ET, MT, HALVES, NT = E // P, S // P, S // HALF, HALF // P
    UNITS = B * HALVES
    W = E + 2
    NSUM = SHIFT_ROWS * B
    with Place(nc, "comb") as place:
        sb, ps, sem, sems = place.sb, place.ps, place.sem, place.sems
        neg, rest = sb("neg", [P, B, MT]), sb("rest", [P, B, MT])
        part = [sb(f"part{i}", [P, B, MT], BF16) for i in range(SHIFT_ROWS)]
        part_T = sb("part_T", [B * MT, SHIFT_ROWS, P], BF16)
        shift = sb("shift", [NSUM, S], BF16)
        select = sb("select", [NSUM, B, P], BF16)
        phi_hi = sb("phi_hi", [P, ET, CHUNKS * P], F32R)
        xfT_hi = [sb(f"xfT_hi{k}", [P, ET, HALF], F32R) for k in range(2)]
        phi_lo = sb("phi_lo", [P, ET, CHUNKS * P], F32R)
        xfT_lo = [sb(f"xfT_lo{k}", [P, ET, HALF], F32R) for k in range(2)]
        y_ends = sb("y_ends", [P, 2, CHUNKS, W - E])
        NBANK, NPROB, NEXP = 4, 4, 2
        exps = [sb(f"exps{i}", [P, HALF]) for i in range(NEXP)]
        probs = [[sb(f"probs_{n}{i}", [P, HALF], F32R) for n in ("hi", "lo")] for i in range(NPROB)]
        GROUP = 4
        GROUPS = CHUNKS // GROUP
        y_raw = [sb(f"y_raw{i}", [P, GROUP, E]) for i in range(2)]
        y = [sb(f"y_{n}", [P, CHUNKS, W], F32R) for n in ("hi", "lo")]
        x1_sb = [sb(f"x1{i}", [P, NT, E]) for i in range(2)]
        h = [sb(f"h{i}", [P, NT, E]) for i in range(2)]
        inverse = sb("inverse", [P, NT])
        minus_half = sb("minus_half", [P, NT])
        rstd = sb("rstd", [P, NT])
        moments = Moments(place, "h", NT)
        mean, ve = moments.mean, moments.ve
        logit_ps = [ps(f"logit_ps{i}", [P, HALF]) for i in range(NBANK)]
        o_ps = ps("o_ps", [P, NT, HALF])

        const_ready, turned, part_T_ready, shift_ready = (sem(n) for n in ("const_ready", "turned", "part_T_ready", "shift_ready"))
        phi_ready, phi_hi_ready, phi_split, ends_ready = (sem(n) for n in ("phi_ready", "phi_hi_ready", "phi_split", "ends_ready"))
        y_ready = sems("y_ready", 2)
        y_hi_ready, y_split = sem("y_hi_ready"), sem("y_split")
        xfT_hi_ready, xfT_split = sem("xfT_hi_ready"), sem("xfT_split")
        x1_ready, o_stored = sems("x1_ready", 2), sems("o_stored", 2)
        logit_ready, exp_ready, hi_ready, prob_ready, prob_used = (
            sem(n) for n in ("logit_ready", "exp_ready", "hi_ready", "prob_ready", "prob_used"))
        inverse_ready, h_ready = sem("inverse_ready"), sem("h_ready")
        ve_ready, rstd_ready, hn_ready, out_ready = sem("ve_ready"), sem("rstd_ready"), sem("hn_ready"), sem("out_ready")
        dve_step = sem("dve_step")
        SETUP = 5
        STEPS = NT + Moments.STEPS

        pieces = h + x1_sb
        piece = NT * E
        PIECES = [(e, slice(i * piece, (i + 1) * piece)) for e in range(ET) for i in range(CHUNKS * P // piece)]
        assert len(PIECES) == len(pieces)

        place.start_sems()
        with nc.Block() as block:

            @block.gpsimd
            def _(pool):
                pool.memset(minus_half[:, :], -0.5).then_inc(const_ready, 1)
                ones_at = flat(y_raw[0][:, :, :])[0:NSUM, 0:B * P].rearrange("p (b n) -> p b n", n=P)
                pool.memset(ones_at, 0.0).then_inc(const_ready, 1)
                for i in range(SHIFT_ROWS):
                    pool.wait_ge(const_ready, ONE + 2 + i)
                    pool.affine_select(out=ones_at, in_=ones_at, compare_op=ALU.not_equal, fill=1.0, base=-i * B,
                                       pattern=[[-1, B], [0, P]], channel_multiplier=1).then_inc(const_ready, 1)
                pool.wait_ge(const_ready, ONE + 2 + SHIFT_ROWS)
                pool.tensor_copy(select[:, :, :], ones_at).then_inc(const_ready, 1)
                pool.wait_ge(const_ready, ONE + 3 + SHIFT_ROWS)

            @block.vector
            def _(dve):
                step = Steps(dve, dve_step, 0, SETUP)
                maxima = row_max[:, :, :].rearrange("p m b -> p b m")
                step.done(dve.tensor_scalar(neg[:, :, :], maxima, -1.0, None, ALU.mult))
                step.done(dve.tensor_scalar(part[0][:, :, :], maxima, -1.0, None, ALU.mult))
                step.wait()
                step.done(dve.tensor_tensor(rest[:, :, :], neg[:, :, :], part[0][:, :, :], ALU.subtract))
                step.wait()
                step.done(dve.tensor_copy(part[1][:, :, :], rest[:, :, :]))
                step.wait()
                step.done(dve.tensor_tensor(part[2][:, :, :], rest[:, :, :], part[1][:, :, :], ALU.subtract))
                step.end()
                dve.memset(y_ends[:, 0, :, :], 1.0).then_inc(ends_ready, 1)
                dve.memset(y_ends[:, 1, :, :], 0.0).then_inc(ends_ready, 1)
                dve.wait_ge(phi_ready, ONE + 16 * len(pieces))
                for (e, n), raw in zip(PIECES, pieces):
                    dve.tensor_copy(phi_hi[:, e, n], flat(raw[:, :, :])).then_inc(phi_hi_ready, 1)
                for i in range(SHIFT_ROWS):
                    dve.wait_ge(turned, ONE + i + 1)
                    dve.tensor_copy(part_T[:, i, :], logit_ps[i][0:B * MT, 0:P // 2].bitcast(BF16)).then_inc(part_T_ready, 1)
                dve.wait_ge(phi_hi_ready, ONE + len(pieces))
                for (e, n), raw in zip(PIECES, pieces):
                    dve.tensor_tensor(phi_lo[:, e, n], flat(raw[:, :, :]), phi_hi[:, e, n].bitcast(F32), ALU.subtract).then_inc(phi_split, 1)
                dve.wait_ge(ends_ready, ONE + 2)
                for i in range(2):
                    dve.tensor_copy(y[i][:, :, E:W], y_ends[:, i, :, :]).then_inc(ends_ready, 1)

            @block.tensor
            def _(pe):
                pe.wait_ge(dve_step, ONE + SETUP)
                for i in range(SHIFT_ROWS):
                    pe.transpose(logit_ps[i][0:B * MT, 0:P // 2].bitcast(BF16), flat(part[i][:, :, :]), identb[:, :]).then_inc(turned, 1)

            @block.sync
            def _(sp):
                rows = phi.rearrange("(t p) x s -> t p (x s)", p=P)
                for (e, n), raw in zip(PIECES, pieces):
                    sp.dma_start(flat(raw[:, :, :]), rows[e, :, n]).then_inc(phi_ready, 16)
                sp.wait_ge(part_T_ready, ONE + SHIFT_ROWS)
                for i in range(SHIFT_ROWS):
                    sp.dma_start(shift[i * B:(i + 1) * B, :].rearrange("b (m q) -> b m q", q=P), part_T[:, i, :]).then_inc(shift_ready, 16)
                sp.wait_ge(shift_ready, ONE + 16 * SHIFT_ROWS)

        def batch_loop(eng, body):
            body(0)
            with eng.Fori(1, B - 1) as b:
                body(b)
            body(B - 1)

        with nc.Block() as block:

            @block.sync
            def _(sp):
                def load_y(b, g):
                    if g >= GROUPS:
                        if isinstance(b, int) and b == B - 1:
                            return
                        b, g = b + 1, g - GROUPS
                    if at_least(b, 1) or g >= 2:
                        sp.wait_ge(y_split, ONE + GROUPS * b + g - 1)
                    sp.dma_start(y_raw[g % 2][:, :, :], y_in[bass.ds(b, 1), g * GROUP:(g + 1) * GROUP, :, :].rearrange("o c p e -> p (o c) e")
                                 ).then_inc(y_ready[g % 2], 16)

                def load_x1(b, s):
                    if at_least(b, 1):
                        sp.wait_ge(out_ready, ONE + HALVES * b - HALVES + s + 1)
                    sp.dma_start(x1_sb[s][:, :, :], tokens(x1, b, s)).then_inc(x1_ready[s], 16)

                def tokens(a, b, s):
                    return a[bass.ds(b, 1), s * HALF:(s + 1) * HALF, :].rearrange("o (t p) e -> p (o t) e", p=P)

                def store(b, s):
                    sp.wait_ge(out_ready, ONE + HALVES * b + s + 1)
                    sp.dma_start(tokens(out, b, s), h[s][:, :, :]).then_inc(o_stored[s], 16)

                load_y(0, 0)
                load_y(0, 1)

                def body(b):
                    load_y(b, 2)
                    load_y(b, 3)
                    load_x1(b, 0)
                    if at_least(b, 1):
                        store(b - 1, 1)
                    load_x1(b, 1)
                    load_y(b, 4)
                    load_y(b, 5)
                    store(b, 0)
                batch_loop(sp, body)
                store(B - 1, 1)
                for s in range(HALVES):
                    sp.wait_ge(o_stored[s], ONE + 16 * B)

            @block.scalar
            def _(act):
                def quotient(u, b, s):
                    act.wait_ge(inverse_ready, ONE + u + 1)
                    if at_least(b, 1):
                        act.wait_ge(o_stored[s], ONE + 16 * b)
                    for t in range(NT):
                        ins = act.activation(h[s][:, t, :], o_ps[:, t, 0:E], ACT.Copy, scale=inverse[:, t:t + 1])
                    ins.then_inc(h_ready, 1)

                def body(b):
                    for s in range(HALVES):
                        u = b * HALVES + s
                        for c in range(CHUNKS):
                            n = CHUNKS * u + c
                            act.wait_ge(logit_ready, ONE + n + 1)
                            if at_least(n, NEXP):
                                act.wait_ge(prob_ready, ONE + n - NEXP + 1)
                            act.activation(exps[c % NEXP][:, :], logit_ps[c % NBANK][:, :], ACT.Exp).then_inc(exp_ready, 1)
                            if c == 0 and at_least(u, 1):
                                quotient(u - 1, b if s else b - 1, 1 - s)
                batch_loop(act, body)
                quotient(UNITS - 1, B - 1, 1)

            @block.gpsimd
            def _(pool):
                with pool.Fori(0, B) as b:
                    for s in range(HALVES):
                        u = b * HALVES + s
                        pool.wait_ge(ve_ready, ONE + u + 1)
                        pool.tensor_tensor(rstd[:, :], ve[:, :], minus_half[:, :], ALU.pow).then_inc(rstd_ready, 1)
                        pool.wait_ge(hn_ready, ONE + u + 1)
                        pool.wait_ge(x1_ready[s], ONE + 16 * (b + 1))
                        pool.tensor_tensor(h[s][:, :, :], h[s][:, :, :], x1_sb[s][:, :, :], ALU.add).then_inc(out_ready, 1)

            @block.vector
            def _(dve):
                def split_y(b, g):
                    r = GROUPS * b + g
                    dve.wait_ge(y_ready[g % 2], ONE + 16 * (b * (GROUPS // 2) + g // 2 + 1))
                    if at_least(b, 1):
                        dve.wait_ge(prob_used, ONE + CHUNKS * HALVES * b - CHUNKS + (g + 1) * GROUP)
                    part_of = lambda i: y[i][:, g * GROUP:(g + 1) * GROUP, 0:E]
                    dve.tensor_copy(part_of(0), y_raw[g % 2][:, :, :]).then_inc(y_hi_ready, 1)
                    dve.wait_ge(y_hi_ready, ONE + r + 1)
                    dve.tensor_tensor(part_of(1), y_raw[g % 2][:, :, :], part_of(0).bitcast(F32), ALU.subtract).then_inc(y_split, 1)

                def split_xfT(u, k):
                    columns = bass.ds(u * HALF, HALF)
                    if at_least(u, 2):
                        dve.wait_ge(logit_ready, ONE + CHUNKS * u - CHUNKS)
                    dve.tensor_copy(xfT_hi[k][:, :, :], xfT[:, :, columns]).then_inc(xfT_hi_ready, 1)
                    dve.wait_ge(xfT_hi_ready, ONE + u + 1)
                    dve.tensor_tensor(xfT_lo[k][:, :, :], xfT[:, :, columns], xfT_hi[k][:, :, :].bitcast(F32),
                                      ALU.subtract).then_inc(xfT_split, 1)

                def split_exponentials(u, c):
                    n, i = CHUNKS * u + c, c % NPROB
                    dve.wait_ge(exp_ready, ONE + n + 1)
                    if at_least(n, NPROB):
                        dve.wait_ge(prob_used, ONE + n - NPROB + 1)
                    hi, lo = probs[i]
                    dve.tensor_copy(hi[:, :], exps[c % NEXP][:, :]).then_inc(hi_ready, 1)
                    dve.wait_ge(hi_ready, ONE + n + 1)
                    dve.tensor_tensor(lo[:, :], exps[c % NEXP][:, :], hi[:, :].bitcast(F32), ALU.subtract).then_inc(prob_ready, 1)

                def invert(u):
                    dve.wait_ge(prob_used, ONE + CHUNKS * u + CHUNKS)
                    if at_least(u, 1):
                        dve.wait_ge(h_ready, ONE + u)
                    dve.reciprocal(inverse[:, :], o_ps[:, :, E]).then_inc(inverse_ready, 1)

                def statistics(u, s):
                    step = Steps(dve, dve_step, SETUP + u * STEPS, STEPS)
                    dve.wait_ge(h_ready, ONE + u + 1)
                    if at_least(u, 1):
                        dve.wait_ge(hn_ready, ONE + u)
                    moments.of(dve, step, [h[s][:, t, :] for t in range(NT)], E).then_inc(ve_ready, 1)
                    step.end()

                def normalise(u, s):
                    dve.wait_ge(rstd_ready, ONE + u + 1)
                    for t in range(NT):
                        ins = dve.tensor_scalar(h[s][:, t, :], h[s][:, t, :], mean[:, t:t + 1], rstd[:, t:t + 1],
                                                ALU.subtract, ALU.mult)
                    ins.then_inc(hn_ready, 1)

                split_xfT(0, 0)
                split_y(0, 0)

                def body(b):
                    for s in range(HALVES):
                        u = b * HALVES + s
                        for c in range(CHUNKS):
                            split_exponentials(u, c)
                            if at_least(u, 1):
                                if c == 0:
                                    invert(u - 1)
                                if c == 3:
                                    statistics(u - 1, 1 - s)
                                if c == 5:
                                    normalise(u - 1, 1 - s)
                            if isinstance(u, int) and u == 0 and c < 2:
                                split_y(0, c + 1)
                            if s == 0 and c == 2:
                                split_y(b, 3)
                            if c == 8 and is_unit(u + 1, UNITS):
                                split_xfT(u + 1, 1 - s)
                            if s == 1 and c >= 6 and (c - 6) % GROUP == 0 and is_unit(b + 1, B):
                                split_y(b + 1, (c - 6) // GROUP)
                batch_loop(dve, body)
                invert(UNITS - 1)
                statistics(UNITS - 1, 1)
                normalise(UNITS - 1, 1)

            @block.tensor
            def _(pe):
                PASSES = ((0, 0), (0, 1), (1, 0))

                def logits(u, b, s, c):
                    n = CHUNKS * u + c
                    if c == 0:
                        pe.wait_ge(xfT_split, ONE + u + 1)
                    if at_least(n, NBANK):
                        pe.wait_ge(exp_ready, ONE + n - NBANK + 1)
                    bank = logit_ps[c % NBANK][:, :]
                    for e in range(ET):
                        for i, j in PASSES:
                            pe.matmul(bank, (phi_hi, phi_lo)[i][:, e, c * P:(c + 1) * P],
                                      (xfT_hi, xfT_lo)[j][s][:, e, :],
                                      start=(e == 0 and i == j == 0), stop=False)
                    pe.matmul(bank, select[:, bass.ds(b, 1), :].rearrange("p o n -> p (o n)"), shift[:, s * HALF:(s + 1) * HALF],
                              start=False, stop=True).then_inc(logit_ready, 1)

                def products(u, b, s, c):
                    n = CHUNKS * u + c
                    pe.wait_ge(prob_ready, ONE + n + 1)
                    if c % GROUP == 0 and s == 0:
                        pe.wait_ge(y_split, ONE + GROUPS * b + c // GROUP + 1)
                    if c == 0 and at_least(u, 1):
                        pe.wait_ge(h_ready, ONE + u)
                    for t in range(NT):
                        for i, j in PASSES:
                            ins = pe.matmul(o_ps[:, t, 0:W], probs[c % NPROB][i][:, t * P:(t + 1) * P], y[j][:, c, :],
                                            start=(c == 0 and i == j == 0), stop=(c == CHUNKS - 1 and i == 1), skip_group_check=True)
                    ins.then_inc(prob_used, 1)

                def body(b):
                    for s in range(HALVES):
                        u = b * HALVES + s
                        for c in range(CHUNKS):
                            logits(u, b, s, c)
                            if c >= 2:
                                products(u, b, s, c - 2)
                        for c in range(CHUNKS - 2, CHUNKS):
                            products(u, b, s, c)
                batch_loop(pe, body)


def block_kernel(nc, x, w_packed, b_packed, w_out, b_out, phi, w_exp, b_exp, out):
    B, S, E = x.shape
    scratch = lambda name, shape, dt=F32: nc.dram_tensor(name, shape, dt).ap()
    parts = scratch("parts", (3, 2 * E, B * S), BF16)
    v_ones = scratch("v_ones", (B, P, S // P, 2 * E))
    att_T = scratch("att_T", (B, 2 * E, S))
    x1 = scratch("x1", (B, S, E))
    xf = scratch("xf", (B, S, E))
    inverse = scratch("inverse", (B, HEADS, S))
    y = scratch("y", (B, phi.shape[1] * phi.shape[2] // P, P, E))
    with Place(nc, "all") as place:
        ident = place.sb("ident", [P, P])
        identb = place.sb("identb", [P, P], BF16)
        with Place(nc, "mask") as m:
            mask = m.sb("mask", [P, P])
            load_constants(nc, place, ident, identb, mask)
            project_qkv(nc, x, w_packed, b_packed, ident, parts, v_ones)
            attend(nc, parts, v_ones, identb, mask, att_T)
        with Place(nc, "moe") as moe:
            xfT_sb = moe.sb("xfT", [P, E // P, B * S])
            row_max = moe.sb("row_max", [P, S // P, B])
            with Place(nc, "router") as router:
                phi_sb = router.sb("phi", [P, E // P, phi.shape[1] * phi.shape[2]])
                close_attention(nc, x, att_T, w_out, b_out, ident, inverse, x1, xf, xfT_sb, phi, phi_sb)
                dispatch_and_experts(nc, (xfT_sb, phi_sb, row_max), xf, phi, w_exp, b_exp, ident, y)
            combine(nc, xfT_sb, row_max, phi, y, x1, identb, out)


_INS = ["L0_attn_Q", "L0_attn_W_packed", "L0_attn_b_packed", "L0_attn_W_out", "L0_attn_b_out", "L0_ffn_phi", "L0_ffn_W", "L0_ffn_b"]


def kernel(**inputs):
    import numpy as _np
    import concourse.bacc as _bacc
    from concourse.bass_utils import run_bass_kernel_spmd as _run

    nc = _bacc.Bacc("TRN2", target_bir_lowering=False, num_devices=1)
    arrays, args = {}, []
    for name in _INS:
        a = _np.ascontiguousarray(inputs[name])
        arrays[f"in_{name}_dram"] = a
        args.append(nc.dram_tensor(f"in_{name}_dram", a.shape, mybir.dt.from_np(a.dtype), kind="ExternalInput").ap())
    out = nc.dram_tensor("out_0_dram", inputs["L0_attn_Q"].shape, F32, kind="ExternalOutput").ap()
    block_kernel(nc, *args, out)
    r = _run(nc, [arrays], core_ids=[0])
    return r.results[0]["out_0_dram"]
```
